# Optimizing a Trainium2 kernel written in Bass

```python
import numpy as np
import jax
import jax.numpy as jnp

def _softmax(x, axis=-1):
    return jax.nn.softmax(x, axis=axis)

def _gelu(x):
    return jax.nn.gelu(x, approximate=True)

def _silu(x):
    return jax.nn.silu(x)

def _sigmoid(x):
    return jax.nn.sigmoid(x)

def _layernorm(x, axis=-1, eps=1e-05):
    m = jnp.mean(x, axis=axis, keepdims=True)
    v = jnp.var(x, axis=axis, keepdims=True)
    return (x - m) / jnp.sqrt(v + eps)

def _scatter_add(tgt, idx, src, axis=0):
    return tgt.at[idx].add(src)

def _segment_sum(src, seg, n):
    return jax.ops.segment_sum(src, seg, n)
kernel_name = 'mk_sandwich_d1_jaxref_r2_f2e052'

def setup_inputs(seed: int=0):
    np.random.seed(seed)
    _w = jnp.asarray

    def _L0_attn_setup():
        import jax, jax.numpy as jnp
        import numpy as np
        B, L, D, N = (8, 512, 512, 32)
        DT_MIN, DT_MAX = (0.001, 0.1)
        key = jax.random.key(seed)
        ks = jax.random.split(key, 12)
        s = 1.0 / np.sqrt(D)
        inp = {'x': jax.random.normal(ks[0], (B, L, D), jnp.float32), 'in_W': jax.random.uniform(ks[1], (D, D), jnp.float32, -s, s), 'in_b': jax.random.uniform(ks[2], (D,), jnp.float32, -s, s), 'log_dt': (np.log(DT_MIN) + jax.random.uniform(ks[3], (D,), jnp.float32) * (np.log(DT_MAX) - np.log(DT_MIN))).astype(jnp.float32), 'C': jax.random.normal(ks[4], (D, N, 2), jnp.float32), 'log_A_real': jnp.log(0.5 * jnp.ones((D, N), jnp.float32)), 'A_imag': jnp.tile((np.pi * jnp.arange(N, dtype=np.float32))[None, :], (D, 1)), 'D_skip': jax.random.normal(ks[5], (D,), jnp.float32), 'glu_W': jax.random.uniform(ks[6], (2 * D, D), jnp.float32, -s, s), 'glu_b': jax.random.uniform(ks[7], (2 * D,), jnp.float32, -s, s), 'out_W': jax.random.uniform(ks[8], (D, D), jnp.float32, -s, s), 'out_b': jax.random.uniform(ks[9], (D,), jnp.float32, -s, s)}
        return inp
    _L0_attn_in = _L0_attn_setup()

    def _L0_ffn_setup():
        import jax, jax.numpy as jnp
        import numpy as np
        B, S, H, F, E = (8, 1024, 512, 2048, 8)
        INIT_LAMBDA = 0.2
        key = jax.random.key(seed)
        ks = jax.random.split(key, 12)
        std = 0.02
        return {'hidden_states': jax.random.normal(ks[0], (B, S, H), jnp.float32), 'gate_w1': jax.random.normal(ks[1], (H, H), jnp.float32) * 0.01, 'gate_b1': jnp.zeros((H,), jnp.float32), 'gate_w2': jax.random.normal(ks[2], (E, H), jnp.float32) * 0.01, 'gate_b2': jnp.full((E,), INIT_LAMBDA, jnp.float32), 'W1': jax.random.normal(ks[3], (F, H), jnp.float32) * std, 'b1': jax.random.normal(ks[4], (F,), jnp.float32) * std, 'W2': jax.random.normal(ks[5], (H, F), jnp.float32) * std, 'b2': jax.random.normal(ks[6], (H,), jnp.float32) * std, 'TW1': jax.random.normal(ks[7], (E, F, H), jnp.float32) * std, 'Tb1': jax.random.normal(ks[8], (E, F), jnp.float32) * std, 'TW2': jax.random.normal(ks[9], (E, H, F), jnp.float32) * std, 'Tb2': jax.random.normal(ks[10], (E, H), jnp.float32) * std}
    _L0_ffn_in = _L0_ffn_setup()
    _d = {'L0_attn_x': _L0_attn_in['x'], 'L0_attn_in_W': _L0_attn_in['in_W'], 'L0_attn_in_b': _L0_attn_in['in_b'], 'L0_attn_log_dt': _L0_attn_in['log_dt'], 'L0_attn_C': _L0_attn_in['C'], 'L0_attn_log_A_real': _L0_attn_in['log_A_real'], 'L0_attn_A_imag': _L0_attn_in['A_imag'], 'L0_attn_D_skip': _L0_attn_in['D_skip'], 'L0_attn_glu_W': _L0_attn_in['glu_W'], 'L0_attn_glu_b': _L0_attn_in['glu_b'], 'L0_attn_out_W': _L0_attn_in['out_W'], 'L0_attn_out_b': _L0_attn_in['out_b'], 'L0_ffn_gate_w1': _L0_ffn_in['gate_w1'], 'L0_ffn_gate_b1': _L0_ffn_in['gate_b1'], 'L0_ffn_gate_w2': _L0_ffn_in['gate_w2'], 'L0_ffn_gate_b2': _L0_ffn_in['gate_b2'], 'L0_ffn_W1': _L0_ffn_in['W1'], 'L0_ffn_b1': _L0_ffn_in['b1'], 'L0_ffn_W2': _L0_ffn_in['W2'], 'L0_ffn_b2': _L0_ffn_in['b2'], 'L0_ffn_TW1': _L0_ffn_in['TW1'], 'L0_ffn_Tb1': _L0_ffn_in['Tb1'], 'L0_ffn_TW2': _L0_ffn_in['TW2'], 'L0_ffn_Tb2': _L0_ffn_in['Tb2']}
    _x0 = _d['L0_attn_x']
    _d['L0_attn_x'] = jax.random.normal(jax.random.fold_in(jax.random.key(seed), 1), (1, 8192, 512), dtype=_x0.dtype)
    del _x0
    return _d

def reference(L0_attn_x, L0_attn_in_W, L0_attn_in_b, L0_attn_log_dt, L0_attn_C, L0_attn_log_A_real, L0_attn_A_imag, L0_attn_D_skip, L0_attn_glu_W, L0_attn_glu_b, L0_attn_out_W, L0_attn_out_b, L0_ffn_gate_w1, L0_ffn_gate_b1, L0_ffn_gate_w2, L0_ffn_gate_b2, L0_ffn_W1, L0_ffn_b1, L0_ffn_W2, L0_ffn_b2, L0_ffn_TW1, L0_ffn_Tb1, L0_ffn_TW2, L0_ffn_Tb2):

    def _L0_attn_ref(x, in_W, in_b, log_dt, C, log_A_real, A_imag, D_skip, glu_W, glu_b, out_W, out_b):
        import jax, jax.numpy as jnp
        import numpy as np
        B, L, D, N = (8, 512, 512, 32)
        DT_MIN, DT_MAX = (0.001, 0.1)
        x_in = x @ in_W.T + in_b
        u = jnp.swapaxes(x_in, 1, 2)
        Lseq = u.shape[-1]
        dt = jnp.exp(log_dt)
        Cc = (C[..., 0] + 1j * C[..., 1]).astype(jnp.complex64)
        A = (-jnp.exp(log_A_real) + 1j * A_imag).astype(jnp.complex64)
        dtA = A * dt[:, None].astype(jnp.complex64)
        K = jnp.exp(dtA[:, :, None] * jnp.arange(Lseq, dtype=jnp.float32))
        Ceff = Cc * (jnp.exp(dtA) - 1.0) / A
        k = 2.0 * jnp.einsum('hn,hnl->hl', Ceff, K).real
        n = 2 * Lseq
        k_f = jnp.fft.rfft(k, n=n)
        u_f = jnp.fft.rfft(u, n=n)
        y = jnp.fft.irfft(u_f * k_f, n=n)[..., :Lseq]
        y = y + u * D_skip[:, None]
        y = jax.nn.gelu(y, approximate=False)
        z = jnp.einsum('oh,bhl->bol', glu_W, y) + glu_b[None, :, None]
        a, g = jnp.split(z, 2, axis=1)
        y = a * jax.nn.sigmoid(g)
        y = jnp.swapaxes(y, 1, 2)
        out = y @ out_W.T + out_b
        return out + x

    def _L0_ffn_ref(hidden_states, gate_w1, gate_b1, gate_w2, gate_b2, W1, b1, W2, b2, TW1, Tb1, TW2, Tb2):
        import jax, jax.numpy as jnp
        import numpy as np
        B, S, H, F, E = (8, 1024, 512, 2048, 8)
        INIT_LAMBDA = 0.2
        x = hidden_states
        h = jax.nn.relu(jnp.einsum('bsh,oh->bso', x, gate_w1) + gate_b1)
        g = jnp.einsum('bso,eo->bse', h, gate_w2) + gate_b2
        g = g.mean(axis=1)
        mW1 = W1 + jnp.einsum('be,efh->bfh', g, TW1)
        mb1 = b1 + g @ Tb1
        mW2 = W2 + jnp.einsum('be,ehf->bhf', g, TW2)
        mb2 = b2 + g @ Tb2
        u = jax.nn.gelu(jnp.einsum('bsh,bfh->bsf', x, mW1) + mb1[:, None, :])
        out = jnp.einsum('bsf,bhf->bsh', u, mW2) + mb2[:, None, :]
        return out
    x = L0_attn_x
    x = x + _layernorm(_L0_attn_ref(_layernorm(x, axis=-1), L0_attn_in_W, L0_attn_in_b, L0_attn_log_dt, L0_attn_C, L0_attn_log_A_real, L0_attn_A_imag, L0_attn_D_skip, L0_attn_glu_W, L0_attn_glu_b, L0_attn_out_W, L0_attn_out_b), axis=-1)
    x = x + _layernorm(_L0_ffn_ref(_layernorm(x, axis=-1), L0_ffn_gate_w1, L0_ffn_gate_b1, L0_ffn_gate_w2, L0_ffn_gate_b2, L0_ffn_W1, L0_ffn_b1, L0_ffn_W2, L0_ffn_b2, L0_ffn_TW1, L0_ffn_Tb1, L0_ffn_TW2, L0_ffn_Tb2), axis=-1)
    return x

_drawn_inputs = setup_inputs


def setup_inputs(seed=0):
    import zlib

    import numpy as np

    out = dict(_drawn_inputs(seed))
    spreads = {'L0_attn_log_A_real': (-0.6931471824645996, 0.6),
     'L0_ffn_gate_b1': (0.0, 0.8),
     'L0_ffn_gate_b2': (0.20000000298023224, 0.2)}
    factors = {'L0_attn_in_b': 8.0,
     'L0_attn_glu_b': 8.0,
     'L0_attn_out_b': 4.369,
     'L0_ffn_gate_w1': 8.0,
     'L0_ffn_b1': 3.22,
     'L0_ffn_Tb1': 5.392,
     'L0_ffn_Tb2': 3.555}
    for name, (base, spread) in spreads.items():
        noise = np.random.default_rng([zlib.crc32(name.encode()), seed]).standard_normal(out[name].shape)
        drawn = base * np.exp(spread * noise) if base else spread * noise
        out[name] = jnp.asarray(drawn.astype(out[name].dtype))
    for name, factor in factors.items():
        out[name] = (out[name] * factor).astype(out[name].dtype)
    return out
```

```python
import math
from contextlib import ExitStack

import concourse.bass as bass
from concourse import mybir

F32 = mybir.dt.float32
F32R = mybir.dt.float32r
I32 = mybir.dt.int32
ALU = mybir.AluOpType
ACT = mybir.ActivationFunctionType
AX_X = mybir.AxisListType.X
ds = bass.ds

P = 128
EPS = 1e-5
ROUND = 12582912.0
LOG2E = 1.4426950408889634
LN2_HI, LN2_LO = 0.693359375, -2.12194440054690583e-4
TURN_HI, TURN_MID = 6.28125, 1.93500518798828125e-3
TURN_LO = 2 * math.pi - TURN_HI - TURN_MID


class At:

    def __init__(self, loop, off, unroll):
        self.loop, self.off, self.unroll = loop, off, unroll

    def __add__(self, k):
        return At(self.loop, self.off + k, self.unroll)

    @property
    def n(self):
        return self.off if self.loop is None else self.loop * self.unroll + self.off

    def turn(self, ring):
        assert self.unroll % ring == 0
        return self.off // ring if self.loop is None else self.loop * (self.unroll // ring) + self.off // ring

    def slot(self, ring):
        assert self.unroll % ring == 0
        return self.off % ring

    def within(self, count):
        return self.loop is not None or 0 <= self.off < count

    def reuses(self, ring):
        return self.loop is not None or self.off >= ring


def hold(eng, passed):
    eng.sem_inc(passed, 1)


def run_steps(eng, first, count, unroll, head, tail, step):
    loops = max(0, (count - tail - head) // unroll)
    if loops < 2:
        loops = 0
    for n in range(first, head):
        step(At(None, n, unroll))
    if loops:
        with eng.Fori(0, loops) as i:
            for r in range(unroll):
                step(At(i, head + r, unroll))
    for n in range(head + loops * unroll, count):
        step(At(None, n, unroll))


def s4d_glu_and_gated_ffn(
    nc, x, x_rev, in_WT, in_b, log_dt, C_re, C_im, log_A_real, A_imag, D_skip, glu_WT, glu_b, out_WT, out_b,
    gate_w1T, gate_b1, gate_w2T, gate_b2, W1T, b1, W2T, b2, TW1T, Tb1T, TW2T, Tb2, out,
):
    L, D = x.shape
    F = W1T.shape[1]
    E = TW1T.shape[0]
    N = 32
    Q = P // N
    G = D // Q
    CH = L // P
    KD = D // P
    FT = F // P
    BG = P // Q
    NBATCH = G // BG
    TB = 4
    BT = TB * P
    NBLK = CH // TB
    POW = 8

    scratch = lambda name, shape: nc.dram_tensor(name, shape, F32, kind="Internal").ap()
    powers_d = scratch("powers_d", (G, P, 2, P))
    kernel_d = scratch("kernel_d", (D, 2 * P))
    y_d = scratch("y_d", (CH, P, D))
    x1_d = scratch("x1_d", (CH, P, D))
    x2T_d = scratch("x2T_d", (D, L))

    with ExitStack() as whole:
        def tensors(ctx):
            sb = lambda name, shape, dt=F32: ctx.enter_context(nc.sbuf_tensor(name, shape, dt))
            ps = lambda name, shape: ctx.enter_context(nc.psum_tensor(name, shape, F32))
            sem = lambda name: ctx.enter_context(nc.semaphore(name))
            return sb, ps, sem

        sb, _, _ = tensors(whole)
        ident = sb("ident", [P, P])
        minus_half = sb("minus_half", [P, 1])

        def three_pass(out_, pairs, lhs, rhs, free=None):
            last = None
            for k in range(pairs):
                lh, ll = lhs(k)
                rh, rl = rhs(k)
                for m, (a, b) in enumerate(((lh, rh), (lh, rl), (ll, rh))):
                    last = nc.tensor.matmul(out_, a, b, start=(k == 0 and m == 0),
                                            stop=(k == pairs - 1 and m == 2))
            return last

        with ExitStack() as conv:
            sb, _, _ = tensors(conv)
            u = sb("u", [P, CH, D])
            head_mask = sb("head_mask", [P, Q])
            scan_same = sb("scan_same", [P, 2, G])
            scan_cross = sb("scan_cross", [P, 2, G])
            carry_scale = sb("carry_scale", [P, 2, G])
            tap_weights = sb("tap_weights", [P, 2, G, Q])
            skip = sb("skip", [P, KD])

            with ExitStack() as ctx:
                sb, ps, sem = tensors(ctx)
                x_t = sb("x_t", [P, 4, D])
                xn = sb("xn", [P, 2, D])
                xn_hi = sb("xn_hi", [P, 2, KD, P], F32R)
                xn_lo = sb("xn_lo", [P, 2, KD, P], F32R)
                w_hi = sb("w_hi", [P, KD, D], F32R)
                w_lo = sb("w_lo", [P, KD, D], F32R)
                in_bias = sb("in_bias", [P, D])
                st = sb("st", [P, 4, 6])
                mv = sb("mv", [P, 4, 2])
                var = sb("var", [P, 4, 1])
                rstd = sb("rstd", [P, 4, 1])
                GB = 8
                w_pow = sb("w_pow", [P, 2, POW, G])
                pw = sb("pw", [P, GB, 2, P])
                pw_tmp = sb("pw_tmp", [P, GB, P // 2])
                tp = ps("tp", [P, 2, 512])
                up = ps("up", [P, 2, 512])

                w_loaded, const_ready, w_split = sem("w_loaded"), sem("const_ready"), sem("w_split")
                ident_step = sem("ident_step")
                setup_loaded, setup_step, setup_ready = sem("setup_loaded"), sem("setup_step"), sem("setup_ready")
                x_loaded = [sem(f"x_loaded{i}") for i in range(4)]
                stats_done, aggr_done, var_ready, rstd_ready = (
                    sem("stats_done"), sem("aggr_done"), sem("var_ready"), sem("rstd_ready"))
                xn_ready, tp_ready, hi_ready, lo_ready, u_ready, u_stored = (
                    sem("xn_ready"), sem("tp_ready"), sem("hi_ready"), sem("lo_ready"), sem("u_ready"), sem("u_stored"))
                pw_step, pw_saved = sem("pw_step"), sem("pw_saved")
                dve_passed, pool_passed = sem("dve_passed"), sem("pool_passed")

                room = u[:, :, :].rearrange("p c d -> p (c d)")
                took = [0]

                def take(*shape, dt=F32):
                    n = math.prod(shape)
                    t = room[:, took[0]:took[0] + n]
                    took[0] += n
                    if dt is not F32:
                        t = t.bitcast(dt)
                    names = "abc"[:len(shape)]
                    return t.rearrange(f"p ({' '.join(names)}) -> p {' '.join(names)}",
                                       **dict(zip(names, shape)))

                w_stage = take(KD, D)
                la_dt = take(2, G)
                a_im = take(1, G)
                c_ri = take(2, G)
                WIDE = (POW, G)

                with nc.Block() as block:
                    @block.sync
                    def _(sp):
                        sp.dma_start(w_stage, in_WT.rearrange("(k p) h -> p k h", p=P)).then_inc(w_loaded, 16)

                        def load(s):
                            if s.reuses(4):
                                sp.wait_ge(xn_ready, s.n - 3)
                            sp.dma_start(x_t[:, s.slot(4), :], x_rev[ds(s.n, 1)].rearrange("a p d -> (a p) d")
                                         ).then_inc(x_loaded[s.slot(4)], 16)

                        run_steps(sp, 0, CH, 4, 4, 4, load)

                    @block.scalar
                    def _(act):
                        act.dma_start(la_dt[:, 0], log_A_real).then_inc(setup_loaded, 16)
                        for q in range(Q):
                            act.dma_start(la_dt[N * q:N * q + N, 1], log_dt[q:q + 1, :].rearrange("a g -> (a g)")
                                          .partition_broadcast(N)).then_inc(setup_loaded, 16)
                        act.dma_start(a_im[:, 0], A_imag).then_inc(setup_loaded, 16)
                        act.dma_start(c_ri[:, 0], C_re).then_inc(setup_loaded, 16)
                        act.dma_start(c_ri[:, 1], C_im).then_inc(setup_loaded, 16)
                        act.dma_start(skip[:, :], D_skip).then_inc(setup_loaded, 16)
                        act.dma_start(in_bias[:, :], in_b.partition_broadcast(P)).then_inc(setup_loaded, 16)
                        act.wait_ge(w_loaded, 16)
                        nc.scalar.activation(w_hi[:, :, :], w_stage, ACT.Copy).then_inc(w_split, 1)

                        def step(s):
                            c = s + 1
                            if c.within(CH):
                                act.wait_ge(tp_ready, c.n + 1)
                                if c.reuses(2):
                                    act.wait_ge(u_ready, c.n - 1)
                                nc.scalar.activation(xn_hi[:, c.slot(2)].rearrange("p k t -> p (k t)"),
                                                     tp[:, c.slot(2), :], ACT.Copy).then_inc(hi_ready, 1)

                        run_steps(act, -1, CH, 4, 4, 4, step)

                    @block.tensor
                    def _(pe):
                        pe.wait_ge(ident_step, 2)
                        pe.wait_ge(w_split, 2)

                        def step(s):
                            c = s + 1
                            if c.within(CH):
                                pe.wait_ge(xn_ready, c.n + 1)
                                if c.reuses(2):
                                    pe.wait_ge(lo_ready, c.n - 1)
                                for k in range(KD):
                                    last = nc.tensor.transpose(tp[:, c.slot(2), k * P:(k + 1) * P],
                                                               xn[:, c.slot(2), k * P:(k + 1) * P], ident[:, :])
                                last.then_inc(tp_ready, 1)
                            if s.within(CH):
                                pe.wait_ge(lo_ready, s.n + 1)
                                if s.reuses(2):
                                    pe.wait_ge(u_stored, s.n - 1)
                                three_pass(up[:, s.slot(2), :], KD,
                                           lambda k: (xn_hi[:, s.slot(2), k], xn_lo[:, s.slot(2), k]),
                                           lambda k: (w_hi[:, k], w_lo[:, k])).then_inc(u_ready, 1)

                        run_steps(pe, -1, CH, 4, 4, 4, step)

                    @block.vector
                    def _(dve):
                        dve.wait_ge(w_split, 1)
                        nc.vector.tensor_tensor(w_lo[:, :, :], w_stage, w_hi[:, :, :].bitcast(F32),
                                                ALU.subtract).then_inc(w_split, 1)
                        dve.wait_ge(w_split, 2)
                        dve.wait_ge(setup_loaded, 16 * (6 + Q))
                        dve.wait_ge(const_ready, 2)
                        count = [0]

                        def link(ins):
                            count[0] += 1
                            ins.then_inc(setup_step, 1)
                            dve.wait_ge(setup_step, count[0])

                        def exp_of(dst, src, r, p, k, e_int):
                            link(nc.vector.tensor_scalar(src, src, -100.0, 88.3, ALU.max, ALU.min))
                            link(nc.vector.tensor_scalar(k, src, LOG2E, ROUND, ALU.mult, ALU.add))
                            link(nc.vector.tensor_scalar(k, k, -ROUND, -127.0, ALU.add, ALU.max))
                            link(nc.vector.scalar_tensor_tensor(r, k, -LN2_HI, src, ALU.mult, ALU.add))
                            link(nc.vector.scalar_tensor_tensor(r, k, -LN2_LO, r, ALU.mult, ALU.add))
                            link(nc.vector.tensor_scalar(p, r, 1.0 / math.factorial(8), None, ALU.mult))
                            for m in range(7, 0, -1):
                                link(nc.vector.scalar_tensor_tensor(p, p, 1.0 / math.factorial(m), r,
                                                                    ALU.add, ALU.mult))
                            link(nc.vector.tensor_scalar(k, k, 127.0, 8388608.0, ALU.add, ALU.mult))
                            link(nc.vector.tensor_copy(e_int, k))
                            link(nc.vector.scalar_tensor_tensor(dst, p, 1.0, e_int.bitcast(F32), ALU.add, ALU.mult))

                        two = [take(2, G) for _ in range(4)]
                        two_i = take(2, G, dt=I32)
                        exp_of(two[0], la_dt, two[1], two[2], two[3], two_i)
                        minus_a, dt_ = two[0][:, 0], two[0][:, 1]
                        re_k, ph_k = take(*WIDE), take(*WIDE)
                        link(nc.vector.scalar_tensor_tensor(re_k[:, 0], minus_a, -1.0, dt_, ALU.mult, ALU.mult))
                        for k in range(1, POW):
                            link(nc.vector.tensor_scalar(re_k[:, k], re_k[:, 0], float(2 ** k), None, ALU.mult))
                        ang, trn = take(1, G)[:, 0], take(1, G)[:, 0]
                        link(nc.vector.tensor_tensor(ang, a_im[:, 0], dt_, ALU.mult))
                        link(nc.vector.tensor_scalar(trn, ang, 1.0 / (2 * math.pi), ROUND, ALU.mult, ALU.add))
                        link(nc.vector.tensor_scalar(trn, trn, -ROUND, None, ALU.add))
                        for part in (TURN_HI, TURN_MID, TURN_LO):
                            link(nc.vector.scalar_tensor_tensor(ang, trn, -part, ang, ALU.mult, ALU.add))
                        link(nc.vector.tensor_scalar(ph_k[:, 0], ang, 1.0 / (2 * math.pi), None, ALU.mult))
                        for k in range(1, POW):
                            link(nc.vector.tensor_scalar(ang, ph_k[:, k - 1], 2.0, None, ALU.mult))
                            link(nc.vector.tensor_scalar(trn, ang, ROUND, None, ALU.add))
                            link(nc.vector.tensor_scalar(trn, trn, -ROUND, None, ALU.add))
                            link(nc.vector.tensor_tensor(ph_k[:, k], ang, trn, ALU.subtract))
                        mag, r_, p_, k_ = (take(*WIDE) for _ in range(4))
                        k_i = take(*WIDE, dt=I32)
                        exp_of(mag, re_k, r_, p_, k_, k_i)
                        half, sq = r_, p_
                        sin_h, cos_h = k_, re_k
                        link(nc.vector.tensor_scalar(half, ph_k, math.pi, None, ALU.mult))
                        link(nc.vector.tensor_tensor(sq, half, half, ALU.mult))
                        for dst, top in ((sin_h, 13), (cos_h, 14)):
                            sign = lambda m: (-1.0) ** (m // 2)
                            link(nc.vector.tensor_scalar(dst, sq, sign(top) / math.factorial(top), None, ALU.mult))
                            for m in range(top - 2, 1, -2):
                                link(nc.vector.scalar_tensor_tensor(dst, dst, sign(m) / math.factorial(m), sq,
                                                                    ALU.add, ALU.mult))
                        link(nc.vector.scalar_tensor_tensor(sin_h, sin_h, 1.0, half, ALU.add, ALU.mult))
                        link(nc.vector.tensor_scalar(cos_h, cos_h, 1.0, None, ALU.add))
                        link(nc.vector.scalar_tensor_tensor(cos_h, cos_h, 2.0, sin_h, ALU.mult, ALU.mult))
                        link(nc.vector.scalar_tensor_tensor(sin_h, sin_h, -2.0, sin_h, ALU.mult, ALU.mult))
                        link(nc.vector.scalar_tensor_tensor(w_pow[:, 0], sin_h, 1.0, mag, ALU.add, ALU.mult))
                        link(nc.vector.tensor_tensor(w_pow[:, 1], cos_h, mag, ALU.mult))
                        w128r, w128i = w_pow[:, 0, POW - 1], w_pow[:, 1, POW - 1]
                        link(nc.vector.tensor_copy(scan_same[:, 0], w128r))
                        link(nc.vector.tensor_copy(scan_same[:, 1], w128r))
                        link(nc.vector.tensor_scalar(scan_cross[:, 0], w128i, -1.0, None, ALU.mult))
                        link(nc.vector.tensor_copy(scan_cross[:, 1], w128i))
                        wr, wi = w_pow[:, 0, 0], w_pow[:, 1, 0]
                        den, t, qr, qi, cr, ci, wm = (take(1, G)[:, 0] for _ in range(7))
                        link(nc.vector.tensor_tensor(den, minus_a, minus_a, ALU.mult))
                        link(nc.vector.tensor_tensor(t, a_im[:, 0], a_im[:, 0], ALU.mult))
                        link(nc.vector.tensor_tensor(den, den, t, ALU.add))
                        link(nc.vector.reciprocal(den, den))
                        link(nc.vector.tensor_scalar(wm, wr, -1.0, None, ALU.add))
                        link(nc.vector.tensor_tensor(qr, wi, a_im[:, 0], ALU.mult))
                        link(nc.vector.tensor_tensor(t, wm, minus_a, ALU.mult))
                        link(nc.vector.tensor_tensor(qr, qr, t, ALU.subtract))
                        link(nc.vector.tensor_tensor(qi, wm, a_im[:, 0], ALU.mult))
                        link(nc.vector.tensor_tensor(t, wi, minus_a, ALU.mult))
                        link(nc.vector.scalar_tensor_tensor(qi, qi, -1.0, t, ALU.mult, ALU.subtract))
                        link(nc.vector.tensor_tensor(qr, qr, den, ALU.mult))
                        link(nc.vector.tensor_tensor(qi, qi, den, ALU.mult))
                        C_r, C_i = c_ri[:, 0], c_ri[:, 1]
                        link(nc.vector.tensor_tensor(cr, C_r, qr, ALU.mult))
                        link(nc.vector.tensor_tensor(t, C_i, qi, ALU.mult))
                        link(nc.vector.tensor_tensor(cr, cr, t, ALU.subtract))
                        link(nc.vector.tensor_tensor(ci, C_r, qi, ALU.mult))
                        link(nc.vector.tensor_tensor(t, C_i, qr, ALU.mult))
                        link(nc.vector.tensor_tensor(ci, ci, t, ALU.add))
                        link(nc.vector.tensor_scalar(cr, cr, 2.0, None, ALU.mult))
                        link(nc.vector.tensor_scalar(ci, ci, 2.0, None, ALU.mult))
                        for q in range(Q):
                            link(nc.vector.tensor_scalar(tap_weights[:, 0, :, q], cr, head_mask[:, q:q + 1], None,
                                                         ALU.mult))
                            link(nc.vector.tensor_scalar(tap_weights[:, 1, :, q], ci, head_mask[:, q:q + 1], -1.0,
                                                         ALU.mult, ALU.mult))
                        link(nc.vector.tensor_tensor(qr, cr, wr, ALU.mult))
                        link(nc.vector.tensor_tensor(t, ci, wi, ALU.mult))
                        link(nc.vector.tensor_tensor(carry_scale[:, 0], qr, t, ALU.subtract))
                        link(nc.vector.tensor_tensor(qi, cr, wi, ALU.mult))
                        link(nc.vector.tensor_tensor(t, ci, wr, ALU.mult))
                        nc.vector.tensor_tensor(carry_scale[:, 1], qi, t, ALU.add).then_inc(setup_ready, 1)
                        dve.wait_ge(setup_ready, 1)

                        def step(s):
                            c = s + 3
                            if c.within(CH):
                                i = c.slot(4)
                                dve.wait_ge(x_loaded[i], 16 * c.turn(4) + 16)
                                nc.vector.bn_stats(st[:, i], x_t[:, i]).then_inc(stats_done, 1)
                                dve.wait_ge(stats_done, c.n + 1)
                                hold(dve, dve_passed)
                                nc.vector.bn_aggr(mv[:, i], st[:, i]).then_inc(aggr_done, 1)
                                dve.wait_ge(aggr_done, c.n + 1)
                                nc.vector.tensor_scalar(var[:, i], mv[:, i, 1:2], EPS, None,
                                                        ALU.add).then_inc(var_ready, 1)
                            c = s + 2
                            if c.within(CH):
                                dve.wait_ge(rstd_ready, c.n + 1)
                                if c.reuses(2):
                                    dve.wait_ge(tp_ready, c.n - 1)
                                i = c.slot(4)
                                nc.vector.tensor_scalar(xn[:, c.slot(2)], x_t[:, i], mv[:, i, 0:1], rstd[:, i],
                                                        ALU.subtract, ALU.mult).then_inc(xn_ready, 1)
                            c = s + 1
                            if c.within(CH):
                                dve.wait_ge(hi_ready, c.n + 1)
                                nc.vector.tensor_tensor(
                                    xn_lo[:, c.slot(2)].rearrange("p k t -> p (k t)"), tp[:, c.slot(2), :],
                                    xn_hi[:, c.slot(2)].rearrange("p k t -> p (k t)").bitcast(F32),
                                    ALU.subtract).then_inc(lo_ready, 1)
                            if s.within(CH):
                                dve.wait_ge(u_ready, s.n + 1)
                                nc.vector.tensor_tensor(u[:, ds(s.n, 1), :].rearrange("p a d -> p (a d)"),
                                                        up[:, s.slot(2), :], in_bias[:, :],
                                                        ALU.add).then_inc(u_stored, 1)

                        run_steps(dve, -3, CH, 4, 4, 4, step)

                    @block.gpsimd
                    def _(pool):
                        nc.gpsimd.memset(minus_half[:, :], -0.5).then_inc(const_ready, 1)
                        nc.gpsimd.memset(ident[:, :], 0.0).then_inc(ident_step, 1)
                        pool.wait_ge(ident_step, 1)
                        nc.gpsimd.affine_select(out=ident[:, :], in_=ident[:, :], compare_op=ALU.not_equal, fill=1.0,
                                                base=0, pattern=[[-1, P]], channel_multiplier=1
                                                ).then_inc(ident_step, 1)
                        nc.gpsimd.memset(head_mask[:, :], 0.0).then_inc(ident_step, 1)
                        pool.wait_ge(ident_step, 3)
                        for q in range(Q):
                            last = nc.gpsimd.memset(head_mask[N * q:N * q + N, q:q + 1], 1.0)
                        last.then_inc(const_ready, 1)

                        def step(c):
                            pool.wait_ge(var_ready, c.n + 1)
                            i = c.slot(4)
                            nc.gpsimd.tensor_tensor(rstd[:, i], var[:, i], minus_half[:, :],
                                                    ALU.pow).then_inc(rstd_ready, 1)

                        total = 2 + 6 * (POW - 1)

                        def link(ins, base, count):
                            count[0] += 1
                            ins.then_inc(pw_step, 1)
                            pool.wait_ge(pw_step, base + count[0])
                            hold(pool, pool_passed)

                        def powers(b, part, count):
                            base = b * total
                            if part == 0:
                                link(nc.gpsimd.memset(pw[:, :, 0, 0:1], 1.0), base, count)
                                link(nc.gpsimd.memset(pw[:, :, 1, 0:1], 0.0), base, count)
                            levels = (range(POW - 3), [POW - 3], [POW - 2], [POW - 2])[part]
                            for k in levels:
                                n = 2 ** k
                                wr = w_pow[:, 0, k, ds(b * GB, GB)].unsqueeze(2).to_broadcast([P, GB, n])
                                wi = w_pow[:, 1, k, ds(b * GB, GB)].unsqueeze(2).to_broadcast([P, GB, n])
                                re, im = pw[:, :, 0, 0:n], pw[:, :, 1, 0:n]
                                re2, im2, t = pw[:, :, 0, n:2 * n], pw[:, :, 1, n:2 * n], pw_tmp[:, :, 0:n]
                                if part < 3:
                                    link(nc.gpsimd.tensor_tensor(re2, re, wr, ALU.mult), base, count)
                                    link(nc.gpsimd.tensor_tensor(t, im, wi, ALU.mult), base, count)
                                    link(nc.gpsimd.tensor_tensor(re2, re2, t, ALU.subtract), base, count)
                                if part != 2:
                                    link(nc.gpsimd.tensor_tensor(im2, re, wi, ALU.mult), base, count)
                                    link(nc.gpsimd.tensor_tensor(t, im, wr, ALU.mult), base, count)
                                    link(nc.gpsimd.tensor_tensor(im2, im2, t, ALU.add), base, count)
                            if part == 3:
                                pool.dma_start(powers_d[ds(b * GB, GB)].rearrange("g p r j -> p g (r j)"),
                                               pw[:, :, :, :].rearrange("p g r j -> p g (r j)")).then_inc(pw_saved, 16)
                                pool.wait_ge(pw_saved, 16 * b + 16)
                                hold(pool, pool_passed)

                        rounds = CH // 4
                        per_round = G // GB // rounds
                        pool.wait_ge(setup_ready, 1)
                        with pool.Fori(0, rounds) as r:
                            for m in range(per_round):
                                count = [0]
                                for part in range(4):
                                    if m == 0:
                                        step(At(r, part, 4))
                                    powers(r * per_round + m, part, count)

            with ExitStack() as ctx:
                sb, ps, sem = tensors(ctx)
                XR = 3
                states = sb("states", [P, XR, CH, 2, BG])
                pf = sb("pf", [P, 2, 2, P])
                v = sb("v", [P, 2, 2, P])
                pb = sb("pb", [P, 2, 2, P])
                taps = sb("taps", [P, 2, Q, P])
                carry = sb("carry", [P, 2, 2, CH, Q])
                taps_t = sb("taps_t", [P, P])
                kpad = sb("kpad", [P, 2 * P])
                scan_a = sb("scan_a", [P, 2, BG])
                scan_b = sb("scan_b", [P, 2, BG])
                SC = 8
                prod_a = sb("prod_a", [P, SC, BG])
                prod_b = sb("prod_b", [P, SC, BG])
                prod_c = sb("prod_c", [P, SC, BG])
                prod_d = sb("prod_d", [P, SC, BG])
                vp = ps("vp", [P, 512])
                xp = ps("xp", [P, 2, 512])
                kp = ps("kp", [P, 512])
                kt = ps("kt", [P, 512])
                yp = ps("yp", [P, 2, 512])

                pf_loaded = [sem(f"pf_loaded{i}") for i in range(2)]
                pb_loaded = [sem(f"pb_loaded{i}") for i in range(2)]
                taps_loaded = [sem(f"taps_loaded{i}") for i in range(2)]
                pf_used, v_turned, v_ready, x_ready, x_kept = (
                    sem("pf_used"), sem("v_turned"), sem("v_ready"), sem("x_ready"), sem("x_kept"))
                taps_made, taps_copied, taps_turned, kpad_step, kpad_saved = (
                    sem("taps_made"), sem("taps_copied"), sem("taps_turned"), sem("kpad_step"), sem("kpad_saved"))
                scan_prod, scan_sum, scale_step = sem("scan_prod"), sem("scan_sum"), sem("scale_step")
                cleared, carry_ready, y_ready, y_kept, y_saved = (
                    sem("cleared"), sem("carry_ready"), sem("y_ready"), sem("y_kept"), sem("y_saved"))
                kpad_cleared = sem("kpad_cleared")
                b_passed = {e: sem(f"b_passed_{e}") for e in ("pe", "act", "dve", "pool")}

                ORDER = [("in", 0), ("in", 1)]
                for b in range(NBATCH - 2):
                    ORDER += [("in", b + 2), ("out", b)]
                ORDER += [("out", NBATCH - 2), ("out", NBATCH - 1)]
                XN = CH * Q

                def group(i, r, b):
                    return At(i + b * (BG // 2), r, 2)

                def u_of(g):
                    return u[:, :, ds(g.n * Q, Q)]

                with nc.Block() as block:
                    @block.sync
                    def _(sp):
                        for kind, b in ORDER:
                            if kind == "out":
                                sp.wait_ge(kpad_saved, 16 * (b + 1))
                            with sp.Fori(0, BG // 2) as i:
                                for r in range(2):
                                    g = group(i, r, b)
                                    powers = powers_d[ds(g.n, 1)].rearrange("a p r j -> (a p) r j")
                                    if kind == "in":
                                        sp.wait_ge(pf_used, g.n + 1)
                                        sp.dma_start(pf[:, r], powers).then_inc(pf_loaded[r], 16)
                                    else:
                                        sp.wait_ge(y_ready, g.n + 1)
                                        sp.dma_start(pb[:, r], powers).then_inc(pb_loaded[r], 16)
                                        rows = kernel_d[ds(g.n * Q, Q), 0:P]
                                        sp.dma_start(taps[:, r],
                                                     bass.AP(rows.tensor, rows.offset, [[1, P], [2 * P, Q], [1, P]])
                                                     ).then_inc(taps_loaded[r], 16)

                    @block.tensor
                    def _(pe):
                        pe.sem_inc(pf_used, 2)
                        pe.sem_inc(x_ready, 2)
                        pe.sem_inc(y_ready, 2)

                        def turn(g, local):
                            r = g.slot(2)
                            pe.wait_ge(pf_loaded[r], 16 * g.turn(2) + 16)
                            pe.wait_ge(v_ready, g.n + 1)
                            for m in range(2):
                                last = nc.tensor.transpose(vp[:, m * P:(m + 1) * P], pf[:, r, m], ident[:, :])
                            last.then_inc(v_turned, 1)
                            for m in range(2):
                                last = nc.tensor.matmul(kp[:, ds(local * Q, Q)], pf[:, r, m],
                                                        tap_weights[:, m, ds(g.n, 1), :].rearrange("p a q -> p (a q)"),
                                                        start=(m == 0), stop=(m == 1), skip_group_check=True)
                            last.then_inc(pf_used, 1)

                        def inputs(g):
                            pe.wait_ge(v_ready, g.n + 2)
                            pe.wait_ge(x_kept, g.n + 1)
                            for m in range(2):
                                last = nc.tensor.matmul(xp[:, g.slot(2), m * XN:(m + 1) * XN], v[:, g.slot(2), m],
                                                        u_of(g), start=True, stop=True)
                            last.then_inc(x_ready, 1)

                        for kind, b in ORDER:
                            if kind == "in":
                                if b > 0:
                                    pe.wait_ge(taps_copied, b)
                                g0 = At(None, b * BG, 2)
                                turn(g0, 0)
                                with pe.Fori(0, BG // 2 - 1) as i:
                                    for r in range(2):
                                        turn(group(i, r + 1, b), i * 2 + (r + 1))
                                        inputs(group(i, r, b))
                                turn(g0 + (BG - 1), BG - 1)
                                inputs(g0 + (BG - 2))
                                inputs(g0 + (BG - 1))
                                pe.wait_ge(taps_copied, b + 1)
                                if b > 0:
                                    pe.wait_ge(kpad_step, 2 * b)
                                nc.tensor.transpose(kt[:, 0:P], taps_t[:, :], ident[:, :]).then_inc(taps_turned, 1)
                            else:
                                with pe.Fori(0, BG // 2) as i:
                                    for r in range(2):
                                        g = group(i, r, b)
                                        pe.wait_ge(pb_loaded[r], 16 * g.turn(2) + 16)
                                        pe.wait_ge(taps_loaded[r], 16 * g.turn(2) + 16)
                                        pe.wait_ge(carry_ready, g.n + 1)
                                        pe.wait_ge(y_kept, g.n + 1)
                                        for m in range(2):
                                            nc.tensor.matmul(yp[:, r, 0:XN], pb[:, r, m],
                                                             carry[:, r, m].rearrange("p c q -> p (c q)"),
                                                             start=(m == 0), stop=False, skip_group_check=True)
                                        for q in range(Q):
                                            last = nc.tensor.matmul(
                                                yp[:, r, 0:XN].rearrange("p (c q) -> p c q", q=Q)[:, :, q],
                                                taps[:, r, q],
                                                u[:, :, ds(g.n * Q + q, 1)].rearrange("p c a -> p (c a)"),
                                                start=False, stop=(q == Q - 1), skip_group_check=True)
                                        last.then_inc(y_ready, 1)

                    @block.scalar
                    def _(act):
                        act.sem_inc(v_ready, 1)
                        act.sem_inc(x_kept, 2)
                        act.sem_inc(y_kept, 2)

                        def copy_v(g):
                            act.wait_ge(v_turned, g.n + 1)
                            act.wait_ge(x_ready, g.n + 1)
                            nc.scalar.activation(v[:, g.slot(2)].rearrange("p m j -> p (m j)"), vp[:, 0:2 * P],
                                                 ACT.Copy).then_inc(v_ready, 1)

                        def keep_x(g, local, b):
                            act.wait_ge(x_ready, g.n + 3)
                            hold(act, b_passed["act"])
                            for q in range(Q):
                                rows = slice(N * q, N * q + N)
                                last = nc.scalar.activation(
                                    states[rows, b % XR, :, :, ds(local, 1)].rearrange("p c m a -> p m (c a)"),
                                    xp[rows, g.slot(2), 0:2 * XN].rearrange("p (m c q) -> p m c q", m=2, q=Q)[:, :, :, q],
                                    ACT.Copy)
                            last.then_inc(x_kept, 1)

                        for kind, b in ORDER:
                            if kind == "in":
                                if b >= XR:
                                    act.wait_ge(carry_ready, BG * (b - XR + 1))
                                g0 = At(None, b * BG, 2)
                                copy_v(g0)
                                with act.Fori(0, BG // 2 - 1) as i:
                                    for r in range(2):
                                        copy_v(group(i, r + 1, b))
                                        keep_x(group(i, r, b), i * 2 + r, b)
                                copy_v(g0 + (BG - 1))
                                keep_x(g0 + (BG - 2), BG - 2, b)
                                keep_x(g0 + (BG - 1), BG - 1, b)
                                act.wait_ge(pf_used, 2 + BG * (b + 1))
                                if b > 0:
                                    act.wait_ge(taps_turned, b)
                                nc.scalar.activation(taps_t[:, :], kp[:, 0:P], ACT.Copy).then_inc(taps_copied, 1)
                            else:
                                with act.Fori(0, BG // 2) as i:
                                    for r in range(2):
                                        g = group(i, r, b)
                                        act.wait_ge(y_ready, g.n + 3)
                                        hold(act, b_passed["act"])
                                        nc.scalar.activation(u_of(g).rearrange("p c q -> p c q"),
                                                             yp[:, r, 0:XN].rearrange("p (c q) -> p c q", q=Q),
                                                             ACT.Copy).then_inc(y_kept, 1)
                                act.wait_ge(y_kept, 2 + BG * (b + 1))
                                act.dma_start(y_d[:, :, b * P:(b + 1) * P].rearrange("c p d -> p c d"),
                                              u[:, :, b * P:(b + 1) * P]).then_inc(y_saved, 16)
                        act.wait_ge(y_saved, 16 * NBATCH)

                    @block.vector
                    def _(dve):
                        nc.vector.memset(kpad[:, :], 0.0).then_inc(kpad_cleared, 1)
                        dve.wait_ge(kpad_cleared, 1)
                        for kind, b in ORDER:
                            if kind != "in":
                                continue
                            dve.wait_ge(taps_turned, b + 1)
                            if b > 0:
                                dve.wait_ge(kpad_saved, 16 * b)
                            nc.vector.tensor_copy(kpad[:, P - 1:2 * P - 1], kt[:, 0:P]).then_inc(kpad_step, 1)
                            dve.wait_ge(kpad_step, 2 * b + 1)
                            nc.vector.tensor_tensor(kpad[:, P - 1:P], kpad[:, P - 1:P], skip[:, b:b + 1],
                                                    ALU.add).then_inc(kpad_step, 1)
                            dve.wait_ge(x_kept, 2 + BG * (b + 1))
                            S = states[:, b % XR]
                            same, cross = (t[:, :, b * BG:(b + 1) * BG] for t in (scan_same, scan_cross))
                            done = b * (CH - 1)
                            with dve.Fori(0, CH - 1) as i:
                                before = S[:, ds(i, 1)].rearrange("p a m g -> p (a m) g")
                                now = S[:, ds(i + 1, 1)].rearrange("p a m g -> p (a m) g")
                                nc.vector.tensor_tensor(scan_a[:, :, :], same, before, ALU.mult).then_inc(scan_prod, 1)
                                for m in range(2):
                                    nc.vector.tensor_tensor(scan_b[:, m], cross[:, m], before[:, 1 - m],
                                                            ALU.mult).then_inc(scan_prod, 1)
                                dve.wait_ge(scan_prod, (i + done) * 3 + 3)
                                nc.vector.tensor_tensor(scan_a[:, :, :], scan_a[:, :, :], scan_b[:, :, :],
                                                        ALU.add).then_inc(scan_sum, 1)
                                dve.wait_ge(scan_sum, (i + done) * 2 + 1)
                                nc.vector.tensor_tensor(now, now, scan_a[:, :, :], ALU.add).then_inc(scan_sum, 1)
                                dve.wait_ge(scan_sum, (i + done) * 2 + 2)
                            count = [6 * b * (CH // SC)]
                            for c0 in range(0, CH, SC):
                                re, im = S[:, c0:c0 + SC, 0, :], S[:, c0:c0 + SC, 1, :]
                                Dr, Di = (carry_scale[:, m, b * BG:(b + 1) * BG].unsqueeze(1).to_broadcast([P, SC, BG])
                                          for m in range(2))
                                if count[0]:
                                    dve.wait_ge(scale_step, count[0])
                                nc.vector.tensor_tensor(prod_a[:, :, :], re, Dr, ALU.mult).then_inc(scale_step, 1)
                                nc.vector.tensor_tensor(prod_b[:, :, :], im, Di, ALU.mult).then_inc(scale_step, 1)
                                nc.vector.tensor_tensor(prod_c[:, :, :], re, Di, ALU.mult).then_inc(scale_step, 1)
                                count[0] += 3
                                dve.wait_ge(scale_step, count[0])
                                nc.vector.tensor_tensor(re, prod_a[:, :, :], prod_b[:, :, :],
                                                        ALU.subtract).then_inc(scale_step, 1)
                                nc.vector.tensor_tensor(prod_d[:, :, :], im, Dr, ALU.mult).then_inc(scale_step, 1)
                                count[0] += 2
                                dve.wait_ge(scale_step, count[0])
                                nc.vector.scalar_tensor_tensor(im, prod_c[:, :, :], -1.0, prod_d[:, :, :], ALU.mult,
                                                               ALU.subtract).then_inc(scale_step, 1)
                                count[0] += 1

                    @block.gpsimd
                    def _(pool):
                        nc.gpsimd.memset(carry[:, :, :, 0:1, :], 0.0).then_inc(cleared, 1)
                        pool.wait_ge(cleared, 1)
                        for kind, b in ORDER:
                            if kind == "in":
                                pool.wait_ge(kpad_step, 2 * (b + 1))
                                pool.dma_start(kernel_d[b * P:(b + 1) * P, :], kpad[:, :]).then_inc(kpad_saved, 16)
                            else:
                                pool.wait_ge(scale_step, 6 * (CH // SC) * (b + 1))
                                with pool.Fori(0, BG // 2) as i:
                                    for r in range(2):
                                        g = group(i, r, b)
                                        pool.wait_ge(y_ready, g.n + 1)
                                        hold(pool, b_passed["pool"])
                                        nc.gpsimd.tensor_tensor(
                                            carry[:, r, :, 1:CH, :],
                                            states[:, b % XR, 0:CH - 1, :, ds(i * 2 + r, 1)]
                                            .rearrange("p c m a -> p m (c a)").unsqueeze(3).to_broadcast([P, 2, CH - 1, Q]),
                                            head_mask[:, :].unsqueeze(1).unsqueeze(1).to_broadcast([P, 2, CH - 1, Q]),
                                            ALU.mult).then_inc(carry_ready, 1)

        with ExitStack() as ctx:
            sb, ps, sem = tensors(ctx)
            gw_hi, gw_lo = sb("gw_hi", [P, KD, 2 * D], F32R), sb("gw_lo", [P, KD, 2 * D], F32R)
            ow_hi, ow_lo = sb("ow_hi", [P, KD, D], F32R), sb("ow_lo", [P, KD, D], F32R)
            glu_bias, half_bias = sb("glu_bias", [P, 2 * KD]), sb("half_bias", [P, KD])
            out_bias = sb("out_bias", [P, D])
            y_t, xc = sb("y_t", [P, 2, TB, D]), sb("xc", [P, 2, TB, D])
            g_f = sb("g_f", [P, 2, BT])
            g_hi, g_lo = sb("g_hi", [P, 2, KD, BT], F32R), sb("g_lo", [P, 2, KD, BT], F32R)
            th, za_b, v_f = sb("th", [P, 2, BT]), sb("za_b", [P, 2, BT]), sb("v_f", [P, 2, BT])
            v_hi, v_lo = sb("v_hi", [P, 2, KD, BT], F32R), sb("v_lo", [P, 2, KD, BT], F32R)
            xn_c, xnb, r_t, rn = (sb(n, [P, 2, D]) for n in ("xn_c", "xnb", "r_t", "rn"))
            x1_t, x2_t = sb("x1_t", [P, 2, TB, D]), sb("x2_t", [P, 2, D])
            x2T = sb("x2T", [P, 2, KD, P])
            stc, mvc = sb("stc", [P, 3, 4, 6]), sb("mvc", [P, 3, 4, 2])
            varc, rstdc = sb("varc", [P, 3, 4, 1]), sb("rstdc", [P, 3, 4, 1])
            typ, zp = ps("typ", [P, 512]), ps("zp", [P, 2, 2, 512])
            op, txp = ps("op", [P, 2, 512]), ps("txp", [P, 512])

            wl, bl, ws_, wstep = sem("wl"), sem("bl"), sem("ws_"), sem("wstep")
            y_loaded = [sem(f"y_loaded{i}") for i in range(2)]
            xc_loaded = [sem(f"xc_loaded{i}") for i in range(2)]
            (ty_ready, g_ready, g_hi_ready, g_lo_ready, z_ready, th_ready, za_ready, v_ready_c, v_hi_ready, v_lo_ready,
             o_ready, r_ready, rn_ready, x1_ready, x2_ready, tx_ready, x2T_ready, xn_done, xnb_ready) = (
                sem(n) for n in ("ty_ready", "g_ready", "g_hi_ready", "g_lo_ready", "z_ready", "th_ready", "za_ready",
                                 "v_ready_c", "v_hi_ready", "v_lo_ready", "o_ready", "r_ready", "rn_ready", "x1_ready",
                                 "x2_ready", "tx_ready", "x2T_ready", "xn_done", "xnb_ready"))
            stat, aggr, var_c, root = ([sem(f"{n}_{w}") for w in ("x", "r", "x1")] for n in ("stat", "aggr", "var", "root"))
            x1_saved = [sem(f"x1_saved{i}") for i in range(2)]
            x2T_saved = [sem(f"x2T_saved{i}") for i in range(2)]
            dve_held = sem("dve_held")
            gw_stage = y_t[:, :, :, :].rearrange("p a k t -> p (a k t)").rearrange("p (k n) -> p k n", k=KD)
            ow_stage = xc[:, 0]

            def of_block(a):
                return a.slot(8) // 4, a.slot(8) % 4

            def quarters(eng, step, first=-5, last=8):
                run_steps(eng, first, CH + last, 8, 16, 14, step)

            with nc.Block() as block:
                @block.sync
                def _(sp):
                    sp.dma_start(gw_stage, glu_WT.rearrange("(k p) n -> p k n", p=P)).then_inc(wl, 16)
                    sp.dma_start(ow_stage, out_WT.rearrange("(k p) n -> p k n", p=P)).then_inc(wl, 16)
                    sp.dma_start(glu_bias[:, :], glu_b).then_inc(bl, 16)
                    sp.dma_start(out_bias[:, :], out_b.partition_broadcast(P)).then_inc(bl, 16)
                    x_b = x.rearrange("(b j p) d -> b p j d", p=P, j=TB)
                    y_b = y_d.rearrange("(b j) p d -> b p j d", j=TB)
                    x1_b = x1_d.rearrange("(b j) p d -> b p j d", j=TB)
                    def one(ap, n):
                        return ap[ds(n, 1)].rearrange("a p j d -> (a p) j d")

                    def step(s):
                        b = s + 2
                        if b.within(NBLK):
                            if b.reuses(2):
                                sp.wait_ge(ty_ready, (b.n - 1) * 4)
                            sp.dma_start(y_t[:, b.slot(2)], one(y_b, b.n)).then_inc(y_loaded[b.slot(2)], 16)
                        if s.within(NBLK):
                            if s.reuses(2):
                                sp.wait_ge(x1_ready, (s.n - 1) * 4)
                            sp.dma_start(xc[:, s.slot(2)], one(x_b, s.n)).then_inc(xc_loaded[s.slot(2)], 16)
                        b = s + (-3)
                        if b.within(NBLK):
                            sp.wait_ge(x1_ready, b.n * 4 + 4)
                            sp.dma_start(one(x1_b, b.n), x1_t[:, b.slot(2)]).then_inc(x1_saved[b.slot(2)], 16)

                    sp.wait_ge(wstep, 2)
                    run_steps(sp, -2, NBLK + 3, 2, 6, 5, step)
                    for i in range(2):
                        sp.wait_ge(x1_saved[i], 16 * NBLK // 2)
                        sp.wait_ge(x2T_saved[i], 16 * CH // 2)

                @block.tensor
                def _(pe):
                    pe.wait_ge(wstep, 4)

                    def step(m):
                        if m.within(CH):
                            bs, o = of_block(m)
                            pe.wait_ge(g_lo_ready, m.n + 1 + (3 - o))
                            if m.reuses(2):
                                pe.wait_ge(th_ready, m.n - 1)
                                pe.wait_ge(za_ready, m.n - 1)
                            for half in range(2):
                                cols = slice(half * D + o * P, half * D + (o + 1) * P)
                                last = three_pass(zp[:, m.slot(2), half], KD,
                                                  lambda k: (gw_hi[:, k, cols], gw_lo[:, k, cols]),
                                                  lambda k: (g_hi[:, bs, k], g_lo[:, bs, k]))
                            last.then_inc(z_ready, 1)
                        a = m + 5
                        if a.within(CH):
                            bs, k = of_block(a)
                            if k == 0:
                                pe.wait_ge(y_loaded[bs], 16 * a.turn(8) + 16)
                            if a.reuses(1):
                                pe.wait_ge(g_ready, a.n)
                            for j in range(TB):
                                last = nc.tensor.transpose(typ[:, j * P:(j + 1) * P],
                                                           y_t[:, bs, j, k * P:(k + 1) * P], ident[:, :])
                            last.then_inc(ty_ready, 1)
                        a = m + (-4)
                        if a.within(CH):
                            bs, j = of_block(a)
                            pe.wait_ge(v_lo_ready, a.n + 1 + (3 - j))
                            if a.reuses(2):
                                pe.wait_ge(r_ready, a.n - 1)
                            toks = slice(j * P, (j + 1) * P)
                            three_pass(op[:, a.slot(2)], KD,
                                       lambda k: (v_hi[:, bs, k, toks], v_lo[:, bs, k, toks]),
                                       lambda k: (ow_hi[:, k], ow_lo[:, k])).then_inc(o_ready, 1)
                        a = m + (-7)
                        if a.within(CH):
                            pe.wait_ge(x2_ready, a.n + 1)
                            if a.reuses(1):
                                pe.wait_ge(x2T_ready, a.n)
                            for k in range(KD):
                                last = nc.tensor.transpose(txp[:, k * P:(k + 1) * P],
                                                           x2_t[:, a.slot(2), k * P:(k + 1) * P], ident[:, :])
                            last.then_inc(tx_ready, 1)

                    quarters(pe, step)

                @block.scalar
                def _(act):
                    act.wait_ge(wl, 32)
                    nc.scalar.activation(gw_hi[:, :, :], gw_stage, ACT.Copy).then_inc(ws_, 1)
                    nc.scalar.activation(ow_hi[:, :, :], ow_stage, ACT.Copy).then_inc(ws_, 1)
                    act.wait_ge(wstep, 4)

                    def step(m):
                        if m.within(CH):
                            o, r = m.slot(4), m.slot(2)
                            act.wait_ge(z_ready, m.n + 1)
                            if m.reuses(2):
                                act.wait_ge(v_ready_c, m.n - 1)
                            nc.scalar.activation(th[:, r], zp[:, r, 1], ACT.Tanh, bias=half_bias[:, o:o + 1],
                                                 scale=0.5).then_inc(th_ready, 1)
                            nc.scalar.activation(za_b[:, r], zp[:, r, 0], ACT.Identity, bias=glu_bias[:, o:o + 1],
                                                 scale=1.0).then_inc(za_ready, 1)
                        a = m + 5
                        if a.within(CH):
                            bs, k = of_block(a)
                            act.wait_ge(ty_ready, a.n + 1)
                            if a.reuses(2):
                                act.wait_ge(g_lo_ready, a.n - 1)
                            nc.scalar.activation(g_f[:, a.slot(2)], typ[:, :], ACT.Gelu).then_inc(g_ready, 1)
                            if a.reuses(8):
                                act.wait_ge(z_ready, a.n - 4 - k)
                            act.wait_ge(g_ready, a.n + 1)
                            nc.scalar.activation(g_hi[:, bs, k], g_f[:, a.slot(2)], ACT.Copy).then_inc(g_hi_ready, 1)
                        if m.within(CH):
                            bs, o = of_block(m)
                            act.wait_ge(v_ready_c, m.n + 1)
                            if m.reuses(8):
                                act.wait_ge(o_ready, m.n - 4 - o)
                            nc.scalar.activation(v_hi[:, bs, o], v_f[:, m.slot(2)], ACT.Copy).then_inc(v_hi_ready, 1)
                        a = m + (-7)
                        if a.within(CH):
                            act.wait_ge(tx_ready, a.n + 1)
                            if a.reuses(2):
                                act.wait_ge(x2T_saved[a.slot(2)], 16 * a.turn(2))
                            nc.scalar.activation(x2T[:, a.slot(2)], txp[:, :].rearrange("p (k t) -> p k t", k=KD),
                                                 ACT.Copy).then_inc(x2T_ready, 1)
                        a = m + (-8)
                        if a.within(CH):
                            act.wait_ge(x2T_ready, a.n + 1)
                            act.dma_start(x2T_d.rearrange("(k p) t -> p k t", p=P)[:, :, ds(a.n * P, P)],
                                          x2T[:, a.slot(2)]).then_inc(x2T_saved[a.slot(2)], 16)

                    quarters(act, step)

                @block.vector
                def _(dve):
                    dve.wait_ge(ws_, 2)
                    nc.vector.tensor_tensor(ow_lo[:, :, :], ow_stage, ow_hi[:, :, :].bitcast(F32),
                                            ALU.subtract).then_inc(wstep, 1)
                    nc.vector.tensor_tensor(gw_lo[:, :, :], gw_stage, gw_hi[:, :, :].bitcast(F32),
                                            ALU.subtract).then_inc(wstep, 1)
                    dve.wait_ge(bl, 32)
                    nc.vector.tensor_scalar(half_bias[:, :], glu_bias[:, KD:2 * KD], 0.5, None, ALU.mult).then_inc(wstep, 1)
                    nc.vector.memset(stc[:, :, :, :], 0.0).then_inc(wstep, 1)
                    dve.wait_ge(wstep, 4)

                    def variance(which, a, src):
                        i = a.slot(4)
                        nc.vector.bn_stats(stc[:, which, i], src).then_inc(stat[which], 1)
                        dve.wait_ge(stat[which], a.n + 1)
                        hold(dve, dve_held)
                        nc.vector.bn_aggr(mvc[:, which, i], stc[:, which, i]).then_inc(aggr[which], 1)
                        dve.wait_ge(aggr[which], a.n + 1)
                        nc.vector.tensor_scalar(varc[:, which, i], mvc[:, which, i, 1:2], EPS, None,
                                                ALU.add).then_inc(var_c[which], 1)

                    def normalise(which, a, dst, src, done):
                        i = a.slot(4)
                        dve.wait_ge(root[which], a.n + 1)
                        nc.vector.tensor_scalar(dst, src, mvc[:, which, i, 0:1], rstdc[:, which, i], ALU.subtract,
                                                ALU.mult).then_inc(done, 1)

                    def step(m):
                        a = m + (-6)
                        if a.within(CH):
                            bs, j = of_block(a)
                            if a.reuses(2):
                                dve.wait_ge(tx_ready, a.n - 1)
                            normalise(2, a, x2_t[:, a.slot(2)], x1_t[:, bs, j], x2_ready)
                        a = m + (-5)
                        if a.within(CH):
                            if a.reuses(2):
                                dve.wait_ge(x1_ready, a.n - 1)
                            normalise(1, a, rn[:, a.slot(2)], r_t[:, a.slot(2)], rn_ready)
                        a = m + (-3)
                        if a.within(CH):
                            bs, j = of_block(a)
                            if j == 0:
                                dve.wait_ge(xc_loaded[bs], 16 * a.turn(8) + 16)
                            variance(0, a, xc[:, bs, j])
                        a = m + (-4)
                        if a.within(CH):
                            bs, j = of_block(a)
                            if a.reuses(2):
                                dve.wait_ge(xnb_ready, a.n - 1)
                            normalise(0, a, xn_c[:, a.slot(2)], xc[:, bs, j], xn_done)
                        if m.within(CH):
                            r = m.slot(2)
                            dve.wait_ge(th_ready, m.n + 1)
                            dve.wait_ge(za_ready, m.n + 1)
                            if m.reuses(2):
                                dve.wait_ge(v_lo_ready, m.n - 1)
                            nc.vector.scalar_tensor_tensor(v_f[:, r], th[:, r], 1.0, za_b[:, r], ALU.add,
                                                           ALU.mult).then_inc(v_ready_c, 1)
                        a = m + 5
                        if a.within(CH):
                            bs, k = of_block(a)
                            dve.wait_ge(g_hi_ready, a.n + 1)
                            nc.vector.tensor_tensor(g_lo[:, bs, k], g_f[:, a.slot(2)], g_hi[:, bs, k].bitcast(F32),
                                                    ALU.subtract).then_inc(g_lo_ready, 1)
                        if m.within(CH):
                            bs, o = of_block(m)
                            dve.wait_ge(v_hi_ready, m.n + 1)
                            nc.vector.tensor_tensor(v_lo[:, bs, o], v_f[:, m.slot(2)], v_hi[:, bs, o].bitcast(F32),
                                                    ALU.subtract).then_inc(v_lo_ready, 1)
                        a = m + (-4)
                        if a.within(CH):
                            dve.wait_ge(o_ready, a.n + 1)
                            dve.wait_ge(xnb_ready, a.n + 1)
                            nc.vector.scalar_tensor_tensor(r_t[:, a.slot(2)], op[:, a.slot(2)], 0.5, xnb[:, a.slot(2)],
                                                           ALU.mult, ALU.add).then_inc(r_ready, 1)
                            dve.wait_ge(r_ready, a.n + 1)
                            variance(1, a, r_t[:, a.slot(2)])
                        a = m + (-5)
                        if a.within(CH):
                            bs, j = of_block(a)
                            dve.wait_ge(x1_ready, a.n + 1)
                            variance(2, a, x1_t[:, bs, j])

                    quarters(dve, step)

                @block.gpsimd
                def _(pool):
                    def root_of(which, a):
                        i = a.slot(4)
                        pool.wait_ge(var_c[which], a.n + 1)
                        nc.gpsimd.tensor_tensor(rstdc[:, which, i], varc[:, which, i], minus_half[:, :],
                                                ALU.pow).then_inc(root[which], 1)

                    def step(m):
                        a = m + (-5)
                        if a.within(CH):
                            bs, j = of_block(a)
                            pool.wait_ge(rn_ready, a.n + 1)
                            if a.reuses(8) and j == 0:
                                pool.wait_ge(x1_saved[bs], 16 * a.turn(8))
                            nc.gpsimd.tensor_tensor(x1_t[:, bs, j], rn[:, a.slot(2)], xc[:, bs, j],
                                                    ALU.add).then_inc(x1_ready, 1)
                        a = m + (-3)
                        if a.within(CH):
                            root_of(0, a)
                        a = m + (-4)
                        if a.within(CH):
                            pool.wait_ge(xn_done, a.n + 1)
                            if a.reuses(2):
                                pool.wait_ge(r_ready, a.n - 1)
                            nc.gpsimd.tensor_tensor(xnb[:, a.slot(2)], xn_c[:, a.slot(2)], out_bias[:, :],
                                                    ALU.add).then_inc(xnb_ready, 1)
                            root_of(1, a)
                        a = m + (-5)
                        if a.within(CH):
                            root_of(2, a)

                    pool.wait_ge(bl, 32)
                    quarters(pool, step)

        with ExitStack() as ffn:
            sb, _, _ = tensors(ffn)
            m1_hi, m1_lo = sb("m1_hi", [P, KD, F], F32R), sb("m1_lo", [P, KD, F], F32R)
            m2_hi, m2_lo = sb("m2_hi", [P, FT, D], F32R), sb("m2_lo", [P, FT, D], F32R)
            mb1, mb2 = sb("mb1", [P, FT]), sb("mb2", [P, D])
            gate_sum = sb("gate_sum", [P, KD, NBLK])
            gate = sb("gate", [P, E])

            with ExitStack() as ctx:
                sb, ps, sem = tensors(ctx)
                gs = sb("gs", [P, KD, D])
                gt_hi, gt_lo = sb("gt_hi", [P, KD, D], F32R), sb("gt_lo", [P, KD, D], F32R)
                gate_bias = sb("gate_bias", [P, KD])
                x2_in = sb("x2_in", [P, KD, BT])
                xg_hi, xg_lo = sb("xg_hi", [P, KD, BT], F32R), sb("xg_lo", [P, KD, BT], F32R)
                relu = sb("relu", [P, BT])
                hp = ps("hp", [P, 4, 512])
                gw_loaded, gsplit, gb_loaded = sem("gw_loaded"), sem("gsplit"), sem("gb_loaded")
                xg_loaded, xg_hi_ready, xg_lo_ready, h_ready, h_summed = (
                    sem("xg_loaded"), sem("xg_hi_ready"), sem("xg_lo_ready"), sem("h_ready"), sem("h_summed"))
                h_passed = sem("h_passed")

                with nc.Block() as block:
                    @block.sync
                    def _(sp):
                        sp.dma_start(gs[:, :, :], gate_w1T.rearrange("(k p) o -> p k o", p=P)).then_inc(gw_loaded, 16)
                        sp.dma_start(gate_bias[:, :], gate_b1).then_inc(gb_loaded, 16)
                        x2T_b = x2T_d.rearrange("(k p) t -> p k t", p=P)

                        def step(s):
                            if s.reuses(1):
                                sp.wait_ge(xg_lo_ready, s.n)
                            sp.dma_start(x2_in[:, :, :], x2T_b[:, :, ds(s.n * BT, BT)]).then_inc(xg_loaded, 16)

                        run_steps(sp, 0, NBLK, 1, 2, 2, step)

                    @block.scalar
                    def _(act):
                        act.wait_ge(gw_loaded, 16)
                        nc.scalar.activation(gt_hi[:, :, :], gs[:, :, :], ACT.Copy).then_inc(gsplit, 1)
                        act.wait_ge(gb_loaded, 16)

                        def step(s):
                            if s.within(NBLK):
                                act.wait_ge(xg_loaded, 16 * s.n + 16)
                                if s.reuses(1):
                                    act.wait_ge(h_ready, 4 * s.n)
                                nc.scalar.activation(xg_hi[:, :, :], x2_in[:, :, :], ACT.Copy).then_inc(xg_hi_ready, 1)
                                for o in range(KD):
                                    act.wait_ge(h_ready, 4 * s.n + o + 1)
                                    if o or s.reuses(1):
                                        act.wait_ge(h_summed, 4 * s.n + o)
                                    hold(act, h_passed)
                                    nc.scalar.activation(relu[:, :], hp[:, o], ACT.Relu, bias=gate_bias[:, o:o + 1],
                                                         scale=1.0, accum_out=gate_sum[:, o, ds(s.n, 1)]
                                                         ).then_inc(h_summed, 1)

                        run_steps(act, 0, NBLK, 1, 2, 2, step)

                    @block.vector
                    def _(dve):
                        dve.wait_ge(gsplit, 1)
                        nc.vector.tensor_tensor(gt_lo[:, :, :], gs[:, :, :], gt_hi[:, :, :].bitcast(F32),
                                                ALU.subtract).then_inc(gsplit, 1)

                        def step(s):
                            dve.wait_ge(xg_hi_ready, s.n + 1)
                            nc.vector.tensor_tensor(xg_lo[:, :, :], x2_in[:, :, :], xg_hi[:, :, :].bitcast(F32),
                                                    ALU.subtract).then_inc(xg_lo_ready, 1)

                        run_steps(dve, 0, NBLK, 1, 2, 2, step)

                    @block.tensor
                    def _(pe):
                        pe.wait_ge(gsplit, 2)

                        def step(s):
                            pe.wait_ge(xg_lo_ready, s.n + 1)
                            for o in range(KD):
                                if s.reuses(1):
                                    pe.wait_ge(h_summed, 4 * (s.n - 1) + o + 1)
                                cols = slice(o * P, (o + 1) * P)
                                three_pass(hp[:, o], KD, lambda k: (gt_hi[:, k, cols], gt_lo[:, k, cols]),
                                           lambda k: (xg_hi[:, k], xg_lo[:, k])).then_inc(h_ready, 1)

                        run_steps(pe, 0, NBLK, 1, 2, 2, step)

            with ExitStack() as ctx:
                sb, ps, sem = tensors(ctx)
                PC = F // 2
                PIECES = KD * F // PC
                expert, base_w, mixed = sb("expert", [P, E, PC]), sb("base_w", [P, 2, PC]), sb("mixed", [P, 2, PC])
                g_mean, g_wide = sb("g_mean", [P, KD]), sb("g_wide", [P, KD, P])
                gw2, gb2 = sb("gw2", [P, KD, E]), sb("gb2", [P, E])
                tb1, tb2 = sb("tb1", [P, E, FT]), sb("tb2", [P, E, D])
                gp = ps("gp", [P, 512])
                small_loaded, g_step, g_prod, g_ready, bias_step = (
                    sem("small_loaded"), sem("g_step"), sem("g_prod"), sem("gate_ready"), sem("bias_step"))
                expert_loaded = [sem(f"expert_loaded{e}") for e in range(E)]
                base_loaded = [sem(f"base_loaded{i}") for i in range(2)]
                mix_step, mix_hi, mix_lo = sem("mix_step"), sem("mix_hi"), sem("mix_lo")
                mix_passed = sem("mix_passed")

                def pieces(eng, weight, step):
                    with eng.Fori(0, PIECES // 2) as i:
                        for r in range(2):
                            step(At(i + weight * (PIECES // 2), r, 2), i, r)

                def piece_of(weight, wide, i, r):
                    if weight == 0:
                        return wide.rearrange("(k p) (r f) -> k r p f", p=P, r=2)[ds(i, 1), r].rearrange("a p f -> (a p) f")
                    return wide.rearrange("(i r q p) h -> i r p q h", p=P, r=2, q=2)[ds(i, 1), r].rearrange(
                        "a p q h -> (a p) q h")

                def to(weight, tile):
                    return tile if weight == 0 else tile.rearrange("p (q h) -> p q h", q=2)

                def place(weight, half, i, r):
                    if weight == 0:
                        return half[:, ds(i, 1), r * PC:(r + 1) * PC].rearrange("p a f -> p (a f)")
                    return half[:, ds(i * 4 + 2 * r, 2), :].rearrange("p a f -> p (a f)")

                with nc.Block() as block:
                    @block.sync
                    def _(sp):
                        for weight, (W, TW) in enumerate(((W1T, TW1T), (W2T, TW2T))):
                            def step(s, i, r):
                                sp.wait_ge(mix_step, s.n * E + 1)
                                sp.dma_start(to(weight, base_w[:, r]), piece_of(weight, W, i, r)).then_inc(base_loaded[r], 16)
                                for e in range(E):
                                    sp.wait_ge(mix_step, (s.n + 1) * E + e + 1)
                                    sp.dma_start(to(weight, expert[:, e]), piece_of(weight, TW[e], i, r)
                                                 ).then_inc(expert_loaded[e], 16)
                            pieces(sp, weight, step)

                    @block.scalar
                    def _(act):
                        act.dma_start(gw2[:, :, :], gate_w2T.rearrange("(k p) e -> p k e", p=P)).then_inc(small_loaded, 16)
                        act.dma_start(gb2[:, :], gate_b2.partition_broadcast(P)).then_inc(small_loaded, 16)
                        act.dma_start(mb1[:, :], b1).then_inc(small_loaded, 16)
                        act.dma_start(mb2[:, :], b2.partition_broadcast(P)).then_inc(small_loaded, 16)
                        act.dma_start(tb1[:, :, :], Tb1T).then_inc(small_loaded, 16)
                        act.dma_start(tb2[:, :, :].rearrange("p e d -> p (e d)"),
                                      Tb2.rearrange("e d -> (e d)").partition_broadcast(P)).then_inc(small_loaded, 16)
                        for weight, hi in enumerate((m1_hi, m2_hi)):
                            def step(s, i, r):
                                act.wait_ge(mix_step, (s.n + 3) * E)
                                hold(act, mix_passed)
                                nc.scalar.activation(place(weight, hi, i, r), mixed[:, r], ACT.Copy).then_inc(mix_hi, 1)
                            pieces(act, weight, step)

                    @block.tensor
                    def _(pe):
                        pe.wait_ge(g_step, 3)
                        for k in range(KD):
                            last = nc.tensor.matmul(gp[:, 0:E], g_wide[:, k], gw2[:, k], start=(k == 0), stop=(k == KD - 1))
                        last.then_inc(g_prod, 1)

                    @block.vector
                    def _(dve):
                        dve.sem_inc(mix_step, 2 * E)
                        nc.vector.reduce_sum(g_mean[:, :], gate_sum[:, :, :], AX_X).then_inc(g_step, 1)
                        dve.wait_ge(g_step, 1)
                        nc.vector.tensor_scalar(g_mean[:, :], g_mean[:, :], 1.0 / L, None, ALU.mult).then_inc(g_step, 1)
                        dve.wait_ge(g_step, 2)
                        dve.wait_ge(small_loaded, 16 * 6)
                        nc.vector.tensor_copy(g_wide[:, :, :], g_mean[:, :].unsqueeze(2).to_broadcast([P, KD, P])
                                              ).then_inc(g_step, 1)
                        dve.wait_ge(g_prod, 1)
                        nc.vector.tensor_tensor(gate[:, :], gp[:, 0:E], gb2[:, :], ALU.add).then_inc(g_ready, 1)
                        dve.wait_ge(g_ready, 1)
                        count = 0
                        for e in range(E):
                            for dst, src in ((mb1, tb1), (mb2, tb2)):
                                if count > 1:
                                    dve.wait_ge(bias_step, count - 1)
                                nc.vector.scalar_tensor_tensor(dst[:, :], src[:, e], gate[:, e:e + 1], dst[:, :],
                                                               ALU.mult, ALU.add).then_inc(bias_step, 1)
                                count += 1
                        for weight, (hi, lo) in enumerate(((m1_hi, m1_lo), (m2_hi, m2_lo))):
                            def step(s, i, r):
                                dve.wait_ge(base_loaded[r], 16 * s.turn(2) + 16)
                                dve.wait_ge(mix_lo, s.n + 1)
                                for e in range(E):
                                    dve.wait_ge(expert_loaded[e], 16 * s.n + 16)
                                    if e:
                                        dve.wait_ge(mix_step, (s.n + 2) * E + e)
                                    nc.vector.scalar_tensor_tensor(mixed[:, r], expert[:, e], gate[:, e:e + 1],
                                                                   base_w[:, r] if e == 0 else mixed[:, r],
                                                                   ALU.mult, ALU.add).then_inc(mix_step, 1)
                                dve.wait_ge(mix_hi, s.n + 1)
                                nc.vector.tensor_tensor(place(weight, lo, i, r), mixed[:, r],
                                                        place(weight, hi, i, r).bitcast(F32),
                                                        ALU.subtract).then_inc(mix_lo, 1)
                            pieces(dve, weight, step)

                    @block.gpsimd
                    def _(pool):
                        pool.sem_inc(mix_lo, 2)

            with ExitStack() as ctx:
                sb, ps, sem = tensors(ctx)
                x2_f = sb("x2_f", [P, KD, BT])
                xf_hi, xf_lo = sb("xf_hi", [P, KD, BT], F32R), sb("xf_lo", [P, KD, BT], F32R)
                h_f = sb("h_f", [P, 2, BT])
                h_hi, h_lo = sb("h_hi", [P, 4, BT], F32R), sb("h_lo", [P, 4, BT], F32R)
                o_t, x1_f, fin = sb("o_t", [P, TB, D]), sb("x1_f", [P, TB, D]), sb("fin", [P, TB, D])
                stf, mvf = sb("stf", [P, TB, 6]), sb("mvf", [P, TB, 2])
                varf, rstdf = sb("varf", [P, TB, 1]), sb("rstdf", [P, TB, 1])
                hp2, opf = ps("hp2", [P, 4, 512]), ps("opf", [P, TB, 512])
                x2f_loaded, x1f_loaded, fin_saved = sem("x2f_loaded"), sem("x1f_loaded"), sem("fin_saved")
                xf_hi_ready, xf_lo_ready, h1_ready, hf_ready, h_hi_ready, h_lo_ready, mm2_done = (
                    sem(n) for n in ("xf_hi_ready", "xf_lo_ready", "h1_ready", "hf_ready", "h_hi_ready", "h_lo_ready",
                                     "mm2_done"))
                ot_ready, statf, aggrf, var_f, root_f, norm_f, fin_ready, f_held = (
                    sem(n) for n in ("ot_ready", "statf", "aggrf", "var_f", "root_f", "norm_f", "fin_ready", "f_held"))
                NM = NBLK * FT
                LAG = 2

                def tiles(eng, step):
                    run_steps(eng, -1, NM + FT // 2, FT, FT, FT + FT // 2, step)

                def block_of(m):
                    return (m.off // FT if m.loop is None else m.loop + m.off // FT), m.off % FT

                with nc.Block() as block:
                    @block.sync
                    def _(sp):
                        x2T_b = x2T_d.rearrange("(k p) t -> p k t", p=P)
                        x1_b = x1_d.rearrange("(b j) p d -> b p j d", j=TB)
                        out_b_ = out.rearrange("(b j p) d -> b p j d", j=TB, p=P)

                        def one(ap, n):
                            return ap[ds(n, 1)].rearrange("a p j d -> (a p) j d")

                        def step(s):
                            b = s + 1
                            if b.within(NBLK):
                                if b.reuses(1):
                                    sp.wait_ge(xf_lo_ready, b.n)
                                sp.dma_start(x2_f[:, :, :], x2T_b[:, :, ds(b.n * BT, BT)]).then_inc(x2f_loaded, 16)
                            b = s + (-1)
                            if s.within(NBLK):
                                if s.reuses(1):
                                    sp.wait_ge(fin_ready, (s.n + 1) * TB)
                                sp.dma_start(x1_f[:, :, :], one(x1_b, s.n)).then_inc(x1f_loaded, 16)
                            if b.within(NBLK):
                                sp.wait_ge(fin_ready, (b.n + 2) * TB)
                                sp.dma_start(one(out_b_, b.n), fin[:, :, :]).then_inc(fin_saved, 16)

                        run_steps(sp, -1, NBLK + 1, 1, 2, 2, step)
                        sp.wait_ge(fin_saved, 16 * NBLK)

                    @block.tensor
                    def _(pe):
                        def inner(m):
                            if not m.within(NM):
                                return
                            b, f = block_of(m)
                            if f == 0:
                                pe.wait_ge(xf_lo_ready, b + 1)
                            if m.reuses(4):
                                pe.wait_ge(hf_ready, m.n - 3)
                            cols = slice(f * P, (f + 1) * P)
                            three_pass(hp2[:, m.slot(4)], KD, lambda k: (m1_hi[:, k, cols], m1_lo[:, k, cols]),
                                       lambda k: (xf_hi[:, k], xf_lo[:, k])).then_inc(h1_ready, 1)

                        def outer(m):
                            if not m.within(NM):
                                return
                            b, f = block_of(m)
                            pe.wait_ge(h_lo_ready, m.n + 1)
                            s4 = m.slot(4)
                            for j in range(TB):
                                if f == 0 and m.reuses(FT):
                                    pe.wait_ge(ot_ready, (b - 1) * TB + j + 1)
                                toks = slice(j * P, (j + 1) * P)
                                passes = ((h_hi, m2_hi), (h_hi, m2_lo), (h_lo, m2_hi))
                                for n, (l, r) in enumerate(passes):
                                    last = nc.tensor.matmul(opf[:, j], l[:, s4, toks], r[:, f],
                                                            start=(f == 0 and n == 0), stop=(f == FT - 1 and n == 2))
                            last.then_inc(mm2_done, 1)

                        def step(m):
                            if m.off % FT == 0:
                                outer(m + (-LAG))
                                inner(m)
                            else:
                                inner(m)
                                outer(m + (-LAG))

                        tiles(pe, step)

                    @block.scalar
                    def _(act):
                        def split(b, first):
                            act.wait_ge(x2f_loaded, 16 * b + 16)
                            if not first:
                                act.wait_ge(h1_ready, b * FT)
                            nc.scalar.activation(xf_hi[:, :, :], x2_f[:, :, :], ACT.Copy).then_inc(xf_hi_ready, 1)

                        def step(m):
                            if m.loop is None and m.off == -1:
                                split(0, True)
                                return
                            if not m.within(NM):
                                return
                            b, f = block_of(m)
                            act.wait_ge(h1_ready, m.n + 1)
                            if m.reuses(2):
                                act.wait_ge(h_lo_ready, m.n - 1)
                            nc.scalar.activation(h_f[:, m.slot(2)], hp2[:, m.slot(4)], ACT.Gelu_apprx_tanh,
                                                 bias=mb1[:, f:f + 1], scale=1.0).then_inc(hf_ready, 1)
                            act.wait_ge(hf_ready, m.n + 1)
                            if m.reuses(4):
                                act.wait_ge(mm2_done, m.n - 3)
                            nc.scalar.activation(h_hi[:, m.slot(4)], h_f[:, m.slot(2)], ACT.Copy).then_inc(h_hi_ready, 1)
                            if f == FT - 1 and (m + FT).within(NM):
                                split(b + 1, False)

                        tiles(act, step)

                    @block.vector
                    def _(dve):
                        def split(b):
                            dve.wait_ge(xf_hi_ready, b + 1)
                            nc.vector.tensor_tensor(xf_lo[:, :, :], x2_f[:, :, :], xf_hi[:, :, :].bitcast(F32),
                                                    ALU.subtract).then_inc(xf_lo_ready, 1)

                        def step(m):
                            if m.loop is None and m.off == -1:
                                split(0)
                                return
                            b, f = block_of(m)
                            if m.within(NM):
                                dve.wait_ge(h_hi_ready, m.n + 1)
                                if m.reuses(4):
                                    dve.wait_ge(mm2_done, m.n - 3)
                                nc.vector.tensor_tensor(h_lo[:, m.slot(4)], h_f[:, m.slot(2)],
                                                        h_hi[:, m.slot(4)].bitcast(F32),
                                                        ALU.subtract).then_inc(h_lo_ready, 1)
                                if f == FT - 1 and (m + FT).within(NM):
                                    split(b + 1)
                            if not m.reuses(FT) or not (m + (-FT)).within(NM):
                                return
                            c = b - 1
                            if f == LAG - 1:
                                dve.wait_ge(mm2_done, b * FT)
                                dve.wait_ge(fin_ready, b * TB)
                                for j in range(TB):
                                    nc.vector.tensor_tensor(o_t[:, j], opf[:, j], mb2[:, :], ALU.add).then_inc(ot_ready, 1)
                            j = f - LAG
                            if 0 <= j < TB:
                                dve.wait_ge(ot_ready, c * TB + j + 1)
                                nc.vector.bn_stats(stf[:, j], o_t[:, j]).then_inc(statf, 1)
                                dve.wait_ge(statf, c * TB + j + 1)
                                hold(dve, f_held)
                                nc.vector.bn_aggr(mvf[:, j], stf[:, j]).then_inc(aggrf, 1)
                                dve.wait_ge(aggrf, c * TB + j + 1)
                                nc.vector.tensor_scalar(varf[:, j], mvf[:, j, 1:2], EPS, None, ALU.add).then_inc(var_f, 1)
                            j -= 1
                            if 0 <= j < TB:
                                dve.wait_ge(root_f, c * TB + j + 1)
                                nc.vector.tensor_scalar(o_t[:, j], o_t[:, j], mvf[:, j, 0:1], rstdf[:, j], ALU.subtract,
                                                        ALU.mult).then_inc(norm_f, 1)

                        tiles(dve, step)

                    @block.gpsimd
                    def _(pool):
                        def step(s):
                            pool.wait_ge(x1f_loaded, 16 * s.n + 16)
                            if s.reuses(1):
                                pool.wait_ge(fin_saved, 16 * s.n)
                            for j in range(TB):
                                pool.wait_ge(var_f, s.n * TB + j + 1)
                                nc.gpsimd.tensor_tensor(rstdf[:, j], varf[:, j], minus_half[:, :],
                                                        ALU.pow).then_inc(root_f, 1)
                                pool.wait_ge(norm_f, s.n * TB + j + 1)
                                nc.gpsimd.tensor_tensor(fin[:, j], o_t[:, j], x1_f[:, j], ALU.add).then_inc(fin_ready, 1)

                        pool.sem_inc(fin_ready, TB)
                        run_steps(pool, 0, NBLK, 1, 2, 2, step)


def laid_out(a):
    import numpy as np

    a = {k: np.asarray(v) for k, v in a.items()}
    x = a["L0_attn_x"][0]
    L, D = x.shape
    E, F, _ = a["L0_ffn_TW1"].shape
    N = a["L0_attn_C"].shape[1]
    Q, G = P // N, D * N // P
    columns = lambda v: v.reshape(-1, P).T
    by_group = lambda v: v.reshape(G, Q, N).transpose(1, 2, 0).reshape(P, G)
    given = {
        "x": x,
        "x_rev": x.reshape(L // P, P, D)[:, ::-1],
        "in_WT": a["L0_attn_in_W"].T,
        "in_b": a["L0_attn_in_b"],
        "log_dt": a["L0_attn_log_dt"].reshape(G, Q).T,
        "C_re": by_group(a["L0_attn_C"][..., 0]),
        "C_im": by_group(a["L0_attn_C"][..., 1]),
        "log_A_real": by_group(a["L0_attn_log_A_real"]),
        "A_imag": by_group(a["L0_attn_A_imag"]),
        "D_skip": columns(a["L0_attn_D_skip"]),
        "glu_WT": a["L0_attn_glu_W"].T,
        "glu_b": columns(a["L0_attn_glu_b"]),
        "out_WT": a["L0_attn_out_W"].T,
        "out_b": a["L0_attn_out_b"],
        "gate_w1T": a["L0_ffn_gate_w1"].T,
        "gate_b1": columns(a["L0_ffn_gate_b1"]),
        "gate_w2T": a["L0_ffn_gate_w2"].T,
        "gate_b2": a["L0_ffn_gate_b2"],
        "W1T": a["L0_ffn_W1"].T,
        "b1": columns(a["L0_ffn_b1"]),
        "W2T": a["L0_ffn_W2"].T,
        "b2": a["L0_ffn_b2"],
        "TW1T": a["L0_ffn_TW1"].transpose(0, 2, 1),
        "Tb1T": a["L0_ffn_Tb1"].reshape(E, F // P, P).transpose(2, 0, 1),
        "TW2T": a["L0_ffn_TW2"].transpose(0, 2, 1),
        "Tb2": a["L0_ffn_Tb2"],
    }
    return {k: np.ascontiguousarray(v) for k, v in given.items()}


def kernel(**inputs):
    import concourse.bacc as bacc
    from concourse.bass_utils import run_bass_kernel_spmd

    arrays = laid_out(inputs)
    nc = bacc.Bacc("TRN2", target_bir_lowering=False, num_devices=1)
    args = [nc.dram_tensor(f"in_{k}", v.shape, mybir.dt.from_np(v.dtype), kind="ExternalInput").ap()
            for k, v in arrays.items()]
    out = nc.dram_tensor("out", arrays["x"].shape, F32, kind="ExternalOutput").ap()
    s4d_glu_and_gated_ffn(nc, *args, out)
    r = run_bass_kernel_spmd(nc, [{f"in_{k}": v for k, v in arrays.items()}], core_ids=[0])
    return r.results[0]["out"][None]
```

```python
import math
from contextlib import ExitStack

import concourse.bass as bass
from concourse import mybir

F32 = mybir.dt.float32
F32R = mybir.dt.float32r
I32 = mybir.dt.int32
ALU = mybir.AluOpType
ACT = mybir.ActivationFunctionType
AX_X = mybir.AxisListType.X
ds = bass.ds

P = 128
EPS = 1e-5
ROUND = 12582912.0
LOG2E = 1.4426950408889634
LN2_HI, LN2_LO = 0.693359375, -2.12194440054690583e-4
TURN_HI, TURN_MID = 6.28125, 1.93500518798828125e-3
TURN_LO = 2 * math.pi - TURN_HI - TURN_MID


class At:

    def __init__(self, loop, off, unroll):
        self.loop, self.off, self.unroll = loop, off, unroll

    def __add__(self, k):
        return At(self.loop, self.off + k, self.unroll)

    @property
    def n(self):
        return self.off if self.loop is None else self.loop * self.unroll + self.off

    def turn(self, ring):
        assert self.unroll % ring == 0
        return self.off // ring if self.loop is None else self.loop * (self.unroll // ring) + self.off // ring

    def slot(self, ring):
        assert self.unroll % ring == 0
        return self.off % ring

    def within(self, count):
        return self.loop is not None or 0 <= self.off < count

    def reuses(self, ring):
        return self.loop is not None or self.off >= ring


def hold(eng, passed):
    eng.sem_inc(passed, 1)


def run_steps(eng, first, count, unroll, head, tail, step):
    loops = max(0, (count - tail - head) // unroll)
    if loops < 2:
        loops = 0
    for n in range(first, head):
        step(At(None, n, unroll))
    if loops:
        with eng.Fori(0, loops) as i:
            for r in range(unroll):
                step(At(i, head + r, unroll))
    for n in range(head + loops * unroll, count):
        step(At(None, n, unroll))


def s4d_glu_and_gated_ffn(
    nc, x, x_rev, in_WT, in_b, log_dt, C_re, C_im, log_A_real, A_imag, D_skip, glu_WT, glu_b, out_WT, out_b,
    gate_w1T, gate_b1, gate_w2T, gate_b2, W1T, b1, W2T, b2, TW1T, Tb1T, TW2T, Tb2, out,
):
    L, D = x.shape
    F = W1T.shape[1]
    E = TW1T.shape[0]
    N = 32
    Q = P // N
    G = D // Q
    CH = L // P
    KD = D // P
    FT = F // P
    BG = P // Q
    NBATCH = G // BG
    TB = 4
    BT = TB * P
    NBLK = CH // TB
    POW = 8

    scratch = lambda name, shape: nc.dram_tensor(name, shape, F32, kind="Internal").ap()
    powers_d = scratch("powers_d", (G, P, 2, P))
    kernel_d = scratch("kernel_d", (D, 2 * P))
    y_d = scratch("y_d", (CH, P, D))
    x1_d = scratch("x1_d", (CH, P, D))
    x2T_d = scratch("x2T_d", (D, L))

    with ExitStack() as whole:
        def tensors(ctx):
            sb = lambda name, shape, dt=F32: ctx.enter_context(nc.sbuf_tensor(name, shape, dt))
            ps = lambda name, shape: ctx.enter_context(nc.psum_tensor(name, shape, F32))
            sem = lambda name: ctx.enter_context(nc.semaphore(name))
            return sb, ps, sem

        sb, _, _ = tensors(whole)
        ident = sb("ident", [P, P])
        minus_half = sb("minus_half", [P, 1])

        def three_pass(out_, pairs, lhs, rhs, free=None):
            last = None
            for k in range(pairs):
                lh, ll = lhs(k)
                rh, rl = rhs(k)
                for m, (a, b) in enumerate(((lh, rh), (lh, rl), (ll, rh))):
                    last = nc.tensor.matmul(out_, a, b, start=(k == 0 and m == 0),
                                            stop=(k == pairs - 1 and m == 2))
            return last

        with ExitStack() as conv:
            sb, _, _ = tensors(conv)
            u = sb("u", [P, CH, D])
            head_mask = sb("head_mask", [P, Q])
            scan_same = sb("scan_same", [P, 2, G])
            scan_cross = sb("scan_cross", [P, 2, G])
            carry_scale = sb("carry_scale", [P, 2, G])
            tap_weights = sb("tap_weights", [P, 2, G, Q])
            skip = sb("skip", [P, KD])

            with ExitStack() as ctx:
                sb, ps, sem = tensors(ctx)
                x_t = sb("x_t", [P, 4, D])
                xn = sb("xn", [P, 2, D])
                xn_hi = sb("xn_hi", [P, 2, KD, P], F32R)
                xn_lo = sb("xn_lo", [P, 2, KD, P], F32R)
                w_hi = sb("w_hi", [P, KD, D], F32R)
                w_lo = sb("w_lo", [P, KD, D], F32R)
                in_bias = sb("in_bias", [P, D])
                st = sb("st", [P, 4, 6])
                mv = sb("mv", [P, 4, 2])
                var = sb("var", [P, 4, 1])
                rstd = sb("rstd", [P, 4, 1])
                shift = sb("shift", [P, 4, 1])
                w_pow = sb("w_pow", [P, 2, POW, G])
                GB = 8
                pw = sb("pw", [P, 2, GB, 2, P])
                pw_tmp = sb("pw_tmp", [P, GB, 2, P // 2])
                tp = ps("tp", [P, 2, 512])
                up = ps("up", [P, 2, 512])

                w_loaded, const_ready, w_split = sem("w_loaded"), sem("const_ready"), sem("w_split")
                ident_step = sem("ident_step")
                setup_loaded, setup_step, setup_ready = sem("setup_loaded"), sem("setup_step"), sem("setup_ready")
                x_loaded = [sem(f"x_loaded{i}") for i in range(4)]
                stats_done, aggr_done, var_ready, rstd_ready, shift_ready = (
                    sem("stats_done"), sem("aggr_done"), sem("var_ready"), sem("rstd_ready"), sem("shift_ready"))
                xn_ready, tp_ready, hi_ready, lo_ready, u_ready, u_stored = (
                    sem("xn_ready"), sem("tp_ready"), sem("hi_ready"), sem("lo_ready"), sem("u_ready"), sem("u_stored"))
                dve_passed, pool_passed = sem("dve_passed"), sem("pool_passed")
                pw_step, pw_saved = sem("pw_step"), [sem(f"pw_saved{i}") for i in range(2)]

                SETUP_SHARE = 12 * G
                A_SHARE = 2
                room = u[:, :, :].rearrange("p c d -> p (c d)")
                took = [CH * D - 14 * POW * G]
                setup_chunk = took[0] // D

                def take(*shape, dt=F32):
                    n = math.prod(shape)
                    t = room[:, took[0]:took[0] + n]
                    took[0] += n
                    if dt is not F32:
                        t = t.bitcast(dt)
                    names = "abc"[:len(shape)]
                    return t.rearrange(f"p ({' '.join(names)}) -> p {' '.join(names)}",
                                       **dict(zip(names, shape)))

                w_stage = take(KD, D)
                la_dt = take(2, G)
                a_im = take(1, G)
                c_ri = take(2, G)
                WIDE = (POW, G)

                done = [0]
                ROUNDS = G // GB
                PW_STEPS = 2 + 4 * (POW - 1)

                def powers(dve, b, half):
                    s = b.slot(2)
                    base = b.n * PW_STEPS
                    if half == 0:
                        if b.reuses(2):
                            dve.wait_ge(pw_saved[s], 16 * b.turn(2))
                        nc.vector.memset(pw[:, s, :, 0, 0:1], 1.0).then_inc(pw_step, 1)
                        nc.vector.memset(pw[:, s, :, 1, 0:1], 0.0).then_inc(pw_step, 1)
                    for k in (range(POW - 2), [POW - 2])[half]:
                        n = 2 ** k
                        wr, wi = (w_pow[:, m, k, ds(b.n * GB, GB)].unsqueeze(2).unsqueeze(2)
                                  .to_broadcast([P, GB, 2, n]) for m in range(2))
                        low, high, t = pw[:, s, :, :, 0:n], pw[:, s, :, :, n:2 * n], pw_tmp[:, :, :, 0:n]
                        dve.wait_ge(pw_step, base + 2 + 4 * k)
                        nc.vector.tensor_tensor(t, low, wi, ALU.mult).then_inc(pw_step, 1)
                        nc.vector.tensor_tensor(high, low, wr, ALU.mult).then_inc(pw_step, 1)
                        dve.wait_ge(pw_step, base + 4 + 4 * k)
                        nc.vector.tensor_tensor(high[:, :, 0], high[:, :, 0], t[:, :, 1],
                                                ALU.subtract).then_inc(pw_step, 1)
                        nc.vector.tensor_tensor(high[:, :, 1], high[:, :, 1], t[:, :, 0],
                                                ALU.add).then_inc(pw_step, 1)

                def save_powers(pool, b):
                    pool.wait_ge(pw_step, (b.n + 1) * PW_STEPS)
                    pool.dma_start(powers_d[ds(b.n * GB, GB)].rearrange("g p r j -> p g (r j)"),
                                   pw[:, b.slot(2)].rearrange("p g r j -> p g (r j)")).then_inc(pw_saved[b.slot(2)], 16)

                def round_at(s):
                    off = s.off - done[0]
                    return At(s.loop, off // 2, 2), off % 2

                with nc.Block() as block:
                    @block.sync
                    def _(sp):
                        sp.dma_start(w_stage, in_WT.rearrange("(k p) h -> p k h", p=P)).then_inc(w_loaded, 16)

                        def load(s):
                            if s.reuses(4):
                                sp.wait_ge(xn_ready, s.n - 3)
                            sp.dma_start(x_t[:, s.slot(4), :], x_rev[ds(s.n, 1)].rearrange("a p d -> (a p) d")
                                         ).then_inc(x_loaded[s.slot(4)], 16)

                        run_steps(sp, 0, CH, 4, 4, 4, load)

                    @block.scalar
                    def _(act):
                        act.dma_start(la_dt[:, 0], log_A_real).then_inc(setup_loaded, 16)
                        for q in range(Q):
                            act.dma_start(la_dt[N * q:N * q + N, 1], log_dt[q:q + 1, :].rearrange("a g -> (a g)")
                                          .partition_broadcast(N)).then_inc(setup_loaded, 16)
                        act.dma_start(a_im[:, 0], A_imag).then_inc(setup_loaded, 16)
                        act.dma_start(c_ri[:, 0], C_re).then_inc(setup_loaded, 16)
                        act.dma_start(c_ri[:, 1], C_im).then_inc(setup_loaded, 16)
                        act.dma_start(skip[:, :], D_skip).then_inc(setup_loaded, 16)
                        act.dma_start(in_bias[:, :], in_b.partition_broadcast(P)).then_inc(setup_loaded, 16)
                        act.wait_ge(w_loaded, 16)
                        nc.scalar.activation(w_hi[:, :, :], w_stage, ACT.Copy).then_inc(w_split, 1)

                        def step(s):
                            c = s + 2
                            if c.within(CH):
                                act.wait_ge(shift_ready, c.n + 1)
                                if c.reuses(2):
                                    act.wait_ge(tp_ready, c.n - 1)
                                i = c.slot(4)
                                nc.scalar.activation(xn[:, c.slot(2)], x_t[:, i], ACT.Identity, bias=shift[:, i],
                                                     scale=rstd[:, i]).then_inc(xn_ready, 1)
                            c = s + 1
                            if c.within(CH):
                                act.wait_ge(tp_ready, c.n + 1)
                                if c.reuses(2):
                                    act.wait_ge(u_ready, c.n - 1)
                                nc.scalar.activation(xn_hi[:, c.slot(2)].rearrange("p k t -> p (k t)"),
                                                     tp[:, c.slot(2), :], ACT.Copy).then_inc(hi_ready, 1)

                        run_steps(act, -2, CH, 4, 4, 4, step)

                    @block.tensor
                    def _(pe):
                        pe.wait_ge(ident_step, 2)
                        pe.wait_ge(w_split, 2)

                        def step(s):
                            c = s + 1
                            if c.within(CH):
                                pe.wait_ge(xn_ready, c.n + 1)
                                if c.reuses(2):
                                    pe.wait_ge(lo_ready, c.n - 1)
                                for k in range(KD):
                                    last = nc.tensor.transpose(tp[:, c.slot(2), k * P:(k + 1) * P],
                                                               xn[:, c.slot(2), k * P:(k + 1) * P], ident[:, :])
                                last.then_inc(tp_ready, 1)
                            if s.within(CH):
                                pe.wait_ge(lo_ready, s.n + 1)
                                if s.reuses(2):
                                    pe.wait_ge(u_stored, s.n - 1)
                                three_pass(up[:, s.slot(2), :], KD,
                                           lambda k: (xn_hi[:, s.slot(2), k], xn_lo[:, s.slot(2), k]),
                                           lambda k: (w_hi[:, k], w_lo[:, k])).then_inc(u_ready, 1)

                        run_steps(pe, -1, CH, 4, 4, 4, step)

                    @block.vector
                    def _(dve):
                        dve.wait_ge(w_split, 1)
                        nc.vector.tensor_tensor(w_lo[:, :, :], w_stage, w_hi[:, :, :].bitcast(F32),
                                                ALU.subtract).then_inc(w_split, 1)
                        dve.wait_ge(w_split, 2)

                        def step(s):
                            c = s + 3
                            if c.within(CH):
                                i = c.slot(4)
                                dve.wait_ge(x_loaded[i], 16 * c.turn(4) + 16)
                                nc.vector.bn_stats(st[:, i], x_t[:, i]).then_inc(stats_done, 1)
                                dve.wait_ge(stats_done, c.n + 1)
                                hold(dve, dve_passed)
                                nc.vector.bn_aggr(mv[:, i], st[:, i]).then_inc(aggr_done, 1)
                                dve.wait_ge(aggr_done, c.n + 1)
                                nc.vector.tensor_scalar(var[:, i], mv[:, i, 1:2], EPS, None,
                                                        ALU.add).then_inc(var_ready, 1)
                            c = s + 2
                            if c.within(CH):
                                dve.wait_ge(rstd_ready, c.n + 1)
                                i = c.slot(4)
                                nc.vector.scalar_tensor_tensor(shift[:, i], mv[:, i, 0:1], -1.0, rstd[:, i],
                                                               ALU.mult, ALU.mult).then_inc(shift_ready, 1)
                            c = s + 1
                            if c.within(CH):
                                dve.wait_ge(hi_ready, c.n + 1)
                                nc.vector.tensor_tensor(
                                    xn_lo[:, c.slot(2)].rearrange("p k t -> p (k t)"), tp[:, c.slot(2), :],
                                    xn_hi[:, c.slot(2)].rearrange("p k t -> p (k t)").bitcast(F32),
                                    ALU.subtract).then_inc(lo_ready, 1)
                            if s.within(CH):
                                dve.wait_ge(u_ready, s.n + 1)
                                nc.vector.tensor_tensor(u[:, ds(s.n, 1), :].rearrange("p a d -> p (a d)"),
                                                        up[:, s.slot(2), :], in_bias[:, :],
                                                        ALU.add).then_inc(u_stored, 1)

                        done[0] = -3

                        def chunk():
                            step(At(None, done[0], 4))
                            done[0] += 1

                        for _ in range(3):
                            chunk()
                        dve.wait_ge(setup_loaded, 16 * (6 + Q))
                        dve.wait_ge(const_ready, 2)
                        count, work = [0], [0]

                        def link(ins, size=G):
                            count[0] += 1
                            ins.then_inc(setup_step, 1)
                            dve.wait_ge(setup_step, count[0])
                            work[0] += size + G
                            if work[0] > SETUP_SHARE:
                                work[0] = 0
                                chunk()

                        def exp_of(dst, src, r, p, k, e_int, size):
                            link(nc.vector.tensor_scalar(src, src, -100.0, 88.3, ALU.max, ALU.min), size)
                            link(nc.vector.tensor_scalar(k, src, LOG2E, ROUND, ALU.mult, ALU.add), size)
                            link(nc.vector.tensor_scalar(k, k, -ROUND, -127.0, ALU.add, ALU.max), size)
                            link(nc.vector.scalar_tensor_tensor(r, k, -LN2_HI, src, ALU.mult, ALU.add), size)
                            link(nc.vector.scalar_tensor_tensor(r, k, -LN2_LO, r, ALU.mult, ALU.add), size)
                            link(nc.vector.tensor_scalar(p, r, 1.0 / math.factorial(8), None, ALU.mult), size)
                            for m in range(7, 0, -1):
                                link(nc.vector.scalar_tensor_tensor(p, p, 1.0 / math.factorial(m), r,
                                                                    ALU.add, ALU.mult), size)
                            link(nc.vector.tensor_scalar(k, k, 127.0, 8388608.0, ALU.add, ALU.mult), size)
                            link(nc.vector.tensor_copy(e_int, k), size)
                            link(nc.vector.scalar_tensor_tensor(dst, p, 1.0, e_int.bitcast(F32), ALU.add, ALU.mult), size)

                        two = [take(2, G) for _ in range(4)]
                        two_i = take(2, G, dt=I32)
                        exp_of(two[0], la_dt, two[1], two[2], two[3], two_i, 2 * G)
                        minus_a, dt_ = two[0][:, 0], two[0][:, 1]
                        re_k, ph_k = take(*WIDE), take(*WIDE)
                        link(nc.vector.scalar_tensor_tensor(re_k[:, 0], minus_a, -1.0, dt_, ALU.mult, ALU.mult))
                        for k in range(1, POW):
                            link(nc.vector.tensor_scalar(re_k[:, k], re_k[:, 0], float(2 ** k), None, ALU.mult))
                        ang, trn = take(1, G)[:, 0], take(1, G)[:, 0]
                        link(nc.vector.tensor_tensor(ang, a_im[:, 0], dt_, ALU.mult))
                        link(nc.vector.tensor_scalar(trn, ang, 1.0 / (2 * math.pi), ROUND, ALU.mult, ALU.add))
                        link(nc.vector.tensor_scalar(trn, trn, -ROUND, None, ALU.add))
                        for part in (TURN_HI, TURN_MID, TURN_LO):
                            link(nc.vector.scalar_tensor_tensor(ang, trn, -part, ang, ALU.mult, ALU.add))
                        link(nc.vector.tensor_scalar(ph_k[:, 0], ang, 1.0 / (2 * math.pi), None, ALU.mult))
                        for k in range(1, POW):
                            link(nc.vector.tensor_scalar(ang, ph_k[:, k - 1], 2.0, None, ALU.mult))
                            link(nc.vector.tensor_scalar(trn, ang, ROUND, None, ALU.add))
                            link(nc.vector.tensor_scalar(trn, trn, -ROUND, None, ALU.add))
                            link(nc.vector.tensor_tensor(ph_k[:, k], ang, trn, ALU.subtract))
                        mag, r_, p_, k_ = (take(*WIDE) for _ in range(4))
                        k_i = take(*WIDE, dt=I32)
                        exp_of(mag, re_k, r_, p_, k_, k_i, POW * G)
                        half, sq = r_, p_
                        sin_h, cos_h = k_, re_k
                        link(nc.vector.tensor_scalar(half, ph_k, math.pi, None, ALU.mult), POW * G)
                        link(nc.vector.tensor_tensor(sq, half, half, ALU.mult), POW * G)
                        for dst, top in ((sin_h, 13), (cos_h, 14)):
                            sign = lambda m: (-1.0) ** (m // 2)
                            link(nc.vector.tensor_scalar(dst, sq, sign(top) / math.factorial(top), None, ALU.mult), POW * G)
                            for m in range(top - 2, 1, -2):
                                link(nc.vector.scalar_tensor_tensor(dst, dst, sign(m) / math.factorial(m), sq,
                                                                    ALU.add, ALU.mult), POW * G)
                        link(nc.vector.scalar_tensor_tensor(sin_h, sin_h, 1.0, half, ALU.add, ALU.mult), POW * G)
                        link(nc.vector.tensor_scalar(cos_h, cos_h, 1.0, None, ALU.add), POW * G)
                        link(nc.vector.scalar_tensor_tensor(cos_h, cos_h, 2.0, sin_h, ALU.mult, ALU.mult), POW * G)
                        link(nc.vector.scalar_tensor_tensor(sin_h, sin_h, -2.0, sin_h, ALU.mult, ALU.mult), POW * G)
                        link(nc.vector.scalar_tensor_tensor(w_pow[:, 0], sin_h, 1.0, mag, ALU.add, ALU.mult), POW * G)
                        link(nc.vector.tensor_tensor(w_pow[:, 1], cos_h, mag, ALU.mult), POW * G)
                        w128r, w128i = w_pow[:, 0, POW - 1], w_pow[:, 1, POW - 1]
                        link(nc.vector.tensor_copy(scan_same[:, 0], w128r))
                        link(nc.vector.tensor_copy(scan_same[:, 1], w128r))
                        link(nc.vector.tensor_scalar(scan_cross[:, 0], w128i, -1.0, None, ALU.mult))
                        link(nc.vector.tensor_copy(scan_cross[:, 1], w128i))
                        wr, wi = w_pow[:, 0, 0], w_pow[:, 1, 0]
                        den, t, qr, qi, cr, ci, wm = (take(1, G)[:, 0] for _ in range(7))
                        link(nc.vector.tensor_tensor(den, minus_a, minus_a, ALU.mult))
                        link(nc.vector.tensor_tensor(t, a_im[:, 0], a_im[:, 0], ALU.mult))
                        link(nc.vector.tensor_tensor(den, den, t, ALU.add))
                        link(nc.vector.reciprocal(den, den))
                        link(nc.vector.tensor_scalar(wm, wr, -1.0, None, ALU.add))
                        link(nc.vector.tensor_tensor(qr, wi, a_im[:, 0], ALU.mult))
                        link(nc.vector.tensor_tensor(t, wm, minus_a, ALU.mult))
                        link(nc.vector.tensor_tensor(qr, qr, t, ALU.subtract))
                        link(nc.vector.tensor_tensor(qi, wm, a_im[:, 0], ALU.mult))
                        link(nc.vector.tensor_tensor(t, wi, minus_a, ALU.mult))
                        link(nc.vector.scalar_tensor_tensor(qi, qi, -1.0, t, ALU.mult, ALU.subtract))
                        link(nc.vector.tensor_tensor(qr, qr, den, ALU.mult))
                        link(nc.vector.tensor_tensor(qi, qi, den, ALU.mult))
                        C_r, C_i = c_ri[:, 0], c_ri[:, 1]
                        link(nc.vector.tensor_tensor(cr, C_r, qr, ALU.mult))
                        link(nc.vector.tensor_tensor(t, C_i, qi, ALU.mult))
                        link(nc.vector.tensor_tensor(cr, cr, t, ALU.subtract))
                        link(nc.vector.tensor_tensor(ci, C_r, qi, ALU.mult))
                        link(nc.vector.tensor_tensor(t, C_i, qr, ALU.mult))
                        link(nc.vector.tensor_tensor(ci, ci, t, ALU.add))
                        link(nc.vector.tensor_scalar(cr, cr, 2.0, None, ALU.mult))
                        link(nc.vector.tensor_scalar(ci, ci, 2.0, None, ALU.mult))
                        for q in range(Q):
                            link(nc.vector.tensor_scalar(tap_weights[:, 0, :, q], cr, head_mask[:, q:q + 1], None,
                                                         ALU.mult))
                            link(nc.vector.tensor_scalar(tap_weights[:, 1, :, q], ci, head_mask[:, q:q + 1], -1.0,
                                                         ALU.mult, ALU.mult))
                        link(nc.vector.tensor_tensor(qr, cr, wr, ALU.mult))
                        link(nc.vector.tensor_tensor(t, ci, wi, ALU.mult))
                        link(nc.vector.tensor_tensor(carry_scale[:, 0], qr, t, ALU.subtract))
                        link(nc.vector.tensor_tensor(qi, cr, wi, ALU.mult))
                        link(nc.vector.tensor_tensor(t, ci, wr, ALU.mult))
                        nc.vector.tensor_tensor(carry_scale[:, 1], qi, t, ALU.add).then_inc(setup_ready, 1)
                        dve.wait_ge(setup_ready, 1)

                        assert done[0] <= setup_chunk and CH - done[0] <= 2 * ROUNDS

                        def step_and_powers(s):
                            step(s)
                            powers(dve, *round_at(s))

                        run_steps(dve, done[0], CH, 4, done[0] + 4, 4, step_and_powers)
                        for n in range(CH - done[0], 2 * ROUNDS):
                            powers(dve, *round_at(At(None, done[0] + n, 4)))

                    @block.gpsimd
                    def _(pool):
                        nc.gpsimd.memset(minus_half[:, :], -0.5).then_inc(const_ready, 1)
                        nc.gpsimd.memset(ident[:, :], 0.0).then_inc(ident_step, 1)
                        pool.wait_ge(ident_step, 1)
                        nc.gpsimd.affine_select(out=ident[:, :], in_=ident[:, :], compare_op=ALU.not_equal, fill=1.0,
                                                base=0, pattern=[[-1, P]], channel_multiplier=1
                                                ).then_inc(ident_step, 1)
                        nc.gpsimd.memset(head_mask[:, :], 0.0).then_inc(ident_step, 1)
                        pool.wait_ge(ident_step, 3)
                        for q in range(Q):
                            last = nc.gpsimd.memset(head_mask[N * q:N * q + N, q:q + 1], 1.0)
                        last.then_inc(const_ready, 1)
                        pool.wait_ge(const_ready, 2)
                        hold(pool, pool_passed)

                        def step(s):
                            c = s + 3
                            if c.within(CH):
                                pool.wait_ge(var_ready, c.n + 1)
                                i = c.slot(4)
                                nc.gpsimd.tensor_tensor(rstd[:, i], var[:, i], minus_half[:, :],
                                                        ALU.pow).then_inc(rstd_ready, 1)

                        def step_and_save(s):
                            step(s)
                            b, half = round_at(s)
                            if half == 1:
                                save_powers(pool, b)

                        run_steps(pool, -3, done[0], 4, 1, 0, step)
                        run_steps(pool, done[0], CH, 4, done[0] + 4, 4, step_and_save)
                        for n in range((CH - done[0]) // 2, ROUNDS):
                            save_powers(pool, At(None, n, 2))
                        for i in range(2):
                            pool.wait_ge(pw_saved[i], 16 * ROUNDS // 2)

            with ExitStack() as ctx:
                sb, ps, sem = tensors(ctx)
                XR = 3
                states = sb("states", [P, XR, CH, 2, BG])
                pg = sb("pg", [P, 4, 2, P])
                v = sb("v", [P, 2, 2, P])
                taps = sb("taps", [P, 4, Q, P])
                carry = sb("carry", [P, 2, 2, CH, Q])
                taps_t = sb("taps_t", [P, P])
                kpad = sb("kpad", [P, 2 * P])
                scan_a = sb("scan_a", [P, 2, BG])
                scan_b = sb("scan_b", [P, 2, BG])
                scale_a = sb("scale_a", [P, 2, BG])
                scale_b = sb("scale_b", [P, 2, BG])
                vp = ps("vp", [P, 2, 512])
                xp = ps("xp", [P, 2, 512])
                kp = ps("kp", [P, 512])
                kt = ps("kt", [P, 512])
                yp = ps("yp", [P, 2, 512])

                pg_loaded = [sem(f"pg_loaded{i}") for i in range(4)]
                taps_loaded = [sem(f"taps_loaded{i}") for i in range(4)]
                pg_used, v_turned, v_ready, x_ready, x_kept = (
                    sem("pg_used"), sem("v_turned"), sem("v_ready"), sem("x_ready"), sem("x_kept"))
                taps_made, taps_copied, taps_turned, kpad_step, kpad_saved = (
                    sem("taps_made"), sem("taps_copied"), sem("taps_turned"), sem("kpad_step"), sem("kpad_saved"))
                scan_prod, scan_sum, scale_prod, scaled = (
                    sem("scan_prod"), sem("scan_sum"), sem("scale_prod"), sem("scaled"))
                cleared, carry_ready, y_ready, y_kept, y_saved = (
                    sem("cleared"), sem("carry_ready"), sem("y_ready"), sem("y_kept"), sem("y_saved"))
                kpad_cleared = sem("kpad_cleared")
                b_passed = {e: sem(f"b_passed_{e}") for e in ("pe", "act", "dve", "pool")}

                ORDER = [("in", 0), ("in", 1)]
                for b in range(NBATCH - 2):
                    ORDER += [("in", b + 2), ("out", b)]
                ORDER += [("out", NBATCH - 2), ("out", NBATCH - 1)]
                LOADS = {which: n * BG for n, which in enumerate(ORDER)}
                XN = CH * Q

                def group(i, r, b):
                    return At(i + b * (BG // 4), r, 4)

                def load_of(g, kind, b):
                    n = LOADS[kind, b] - b * BG
                    return g + n if g.loop is None else At(g.loop + n // 4, g.off, 4)

                def u_of(g):
                    return u[:, :, ds(g.n * Q, Q)]

                with nc.Block() as block:
                    @block.sync
                    def _(sp):
                        for kind, b in ORDER:
                            if kind == "out":
                                sp.wait_ge(kpad_saved, 16 * (b + 1))
                            with sp.Fori(0, BG // 4) as i:
                                for r in range(4):
                                    g = group(i, r, b)
                                    sp.wait_ge(pg_used, load_of(g, kind, b).n + 1)
                                    sp.dma_start(pg[:, r], powers_d[ds(g.n, 1)].rearrange("a p r j -> (a p) r j")
                                                 ).then_inc(pg_loaded[r], 16)
                                    if kind == "out":
                                        sp.wait_ge(y_ready, g.n + 1)
                                        rows = kernel_d[ds(g.n * Q, Q), 0:P]
                                        sp.dma_start(taps[:, r],
                                                     bass.AP(rows.tensor, rows.offset, [[1, P], [2 * P, Q], [1, P]])
                                                     ).then_inc(taps_loaded[r], 16)

                    @block.tensor
                    def _(pe):
                        pe.sem_inc(pg_used, 4)
                        pe.sem_inc(x_ready, 2)
                        pe.sem_inc(y_ready, 4)

                        def turn(g, local, b):
                            r = g.slot(4)
                            pe.wait_ge(pg_loaded[r], 16 * load_of(g, "in", b).turn(4) + 16)
                            pe.wait_ge(v_ready, g.n + 1)
                            for m in range(2):
                                last = nc.tensor.transpose(vp[:, g.slot(2), m * P:(m + 1) * P], pg[:, r, m], ident[:, :])
                            last.then_inc(v_turned, 1)
                            for m in range(2):
                                last = nc.tensor.matmul(kp[:, ds(local * Q, Q)], pg[:, r, m],
                                                        tap_weights[:, m, ds(g.n, 1), :].rearrange("p a q -> p (a q)"),
                                                        start=(m == 0), stop=(m == 1), skip_group_check=True)
                            last.then_inc(pg_used, 1)

                        def inputs(g):
                            pe.wait_ge(v_ready, g.n + 3)
                            pe.wait_ge(x_kept, g.n + 1)
                            for m in range(2):
                                last = nc.tensor.matmul(xp[:, g.slot(2), m * XN:(m + 1) * XN], v[:, g.slot(2), m],
                                                        u_of(g), start=True, stop=True)
                            last.then_inc(x_ready, 1)

                        for kind, b in ORDER:
                            if kind == "in":
                                if b > 0:
                                    pe.wait_ge(taps_copied, b)
                                g0 = At(None, b * BG, 4)
                                turn(g0, 0, b)
                                with pe.Fori(0, BG // 4 - 1) as i:
                                    for r in range(4):
                                        turn(group(i, r + 1, b), i * 4 + (r + 1), b)
                                        inputs(group(i, r, b))
                                for r in range(BG - 4, BG):
                                    if r + 1 < BG:
                                        turn(g0 + (r + 1), r + 1, b)
                                    inputs(g0 + r)
                                pe.wait_ge(taps_copied, b + 1)
                                if b > 0:
                                    pe.wait_ge(kpad_step, 2 * b)
                                nc.tensor.transpose(kt[:, 0:P], taps_t[:, :], ident[:, :]).then_inc(taps_turned, 1)
                            else:
                                with pe.Fori(0, BG // 4) as i:
                                    for r in range(4):
                                        g = group(i, r, b)
                                        s = g.slot(2)
                                        pe.wait_ge(pg_loaded[r], 16 * load_of(g, "out", b).turn(4) + 16)
                                        pe.wait_ge(taps_loaded[r], 16 * g.turn(4) + 16)
                                        pe.wait_ge(carry_ready, g.n + 1)
                                        pe.wait_ge(y_kept, g.n + 1)
                                        for m in range(2):
                                            last = nc.tensor.matmul(yp[:, s, 0:XN], pg[:, r, m],
                                                                    carry[:, s, m].rearrange("p c q -> p (c q)"),
                                                                    start=(m == 0), stop=False, skip_group_check=True)
                                        last.then_inc(pg_used, 1)
                                        for q in range(Q):
                                            last = nc.tensor.matmul(
                                                yp[:, s, 0:XN].rearrange("p (c q) -> p c q", q=Q)[:, :, q],
                                                taps[:, r, q],
                                                u[:, :, ds(g.n * Q + q, 1)].rearrange("p c a -> p (c a)"),
                                                start=False, stop=(q == Q - 1), skip_group_check=True)
                                        last.then_inc(y_ready, 1)

                    @block.scalar
                    def _(act):
                        act.sem_inc(v_ready, 2)
                        act.sem_inc(x_kept, 2)
                        act.sem_inc(y_kept, 2)

                        def copy_v(g):
                            act.wait_ge(v_turned, g.n + 1)
                            act.wait_ge(x_ready, g.n + 1)
                            nc.scalar.activation(v[:, g.slot(2)].rearrange("p m j -> p (m j)"), vp[:, g.slot(2), 0:2 * P],
                                                 ACT.Copy).then_inc(v_ready, 1)

                        def keep_x(g, local, b):
                            act.wait_ge(x_ready, g.n + 3)
                            hold(act, b_passed["act"])
                            for q in range(Q):
                                rows = slice(N * q, N * q + N)
                                last = nc.scalar.activation(
                                    states[rows, b % XR, :, :, ds(local, 1)].rearrange("p c m a -> p m (c a)"),
                                    xp[rows, g.slot(2), 0:2 * XN].rearrange("p (m c q) -> p m c q", m=2, q=Q)[:, :, :, q],
                                    ACT.Copy)
                            last.then_inc(x_kept, 1)

                        for kind, b in ORDER:
                            if kind == "in":
                                if b >= XR:
                                    act.wait_ge(carry_ready, BG * (b - XR + 1))
                                g0 = At(None, b * BG, 4)
                                copy_v(g0)
                                with act.Fori(0, BG // 4 - 1) as i:
                                    for r in range(4):
                                        copy_v(group(i, r + 1, b))
                                        keep_x(group(i, r, b), i * 4 + r, b)
                                for r in range(BG - 4, BG):
                                    if r + 1 < BG:
                                        copy_v(g0 + (r + 1))
                                    keep_x(g0 + r, r, b)
                                act.wait_ge(pg_used, 4 + LOADS[kind, b] + BG)
                                if b > 0:
                                    act.wait_ge(taps_turned, b)
                                nc.scalar.activation(taps_t[:, :], kp[:, 0:P], ACT.Copy).then_inc(taps_copied, 1)
                            else:
                                with act.Fori(0, BG // 4) as i:
                                    for r in range(4):
                                        g = group(i, r, b)
                                        act.wait_ge(y_ready, g.n + 5)
                                        hold(act, b_passed["act"])
                                        nc.scalar.activation(u_of(g).rearrange("p c q -> p c q"),
                                                             yp[:, g.slot(2), 0:XN].rearrange("p (c q) -> p c q", q=Q),
                                                             ACT.Copy).then_inc(y_kept, 1)
                                act.wait_ge(y_kept, 2 + BG * (b + 1))
                                act.dma_start(y_d[:, :, b * P:(b + 1) * P].rearrange("c p d -> p c d"),
                                              u[:, :, b * P:(b + 1) * P]).then_inc(y_saved, 16)
                        act.wait_ge(y_saved, 16 * NBATCH)

                    @block.vector
                    def _(dve):
                        nc.vector.memset(kpad[:, :], 0.0).then_inc(kpad_cleared, 1)
                        dve.wait_ge(kpad_cleared, 1)
                        dve.sem_inc(scaled, 2)
                        for kind, b in ORDER:
                            if kind != "in":
                                continue
                            dve.wait_ge(taps_turned, b + 1)
                            if b > 0:
                                dve.wait_ge(kpad_saved, 16 * b)
                            nc.vector.tensor_copy(kpad[:, P - 1:2 * P - 1], kt[:, 0:P]).then_inc(kpad_step, 1)
                            dve.wait_ge(kpad_step, 2 * b + 1)
                            nc.vector.tensor_tensor(kpad[:, P - 1:P], kpad[:, P - 1:P], skip[:, b:b + 1],
                                                    ALU.add).then_inc(kpad_step, 1)
                            dve.wait_ge(x_kept, 2 + BG * (b + 1))
                            S = states[:, b % XR]
                            same, cross = (t[:, :, b * BG:(b + 1) * BG] for t in (scan_same, scan_cross))
                            done = b * (CH - 1)
                            Dr, Di = (carry_scale[:, m:m + 1, b * BG:(b + 1) * BG].to_broadcast([P, 2, BG])
                                      for m in range(2))

                            def state(n):
                                return S[:, ds(n, 1)].rearrange("p a m g -> p (a m) g")

                            def scale_products(n):
                                dve.wait_ge(scaled, (n + done) * 2 + 2)
                                nc.vector.tensor_tensor(scale_a[:, :, :], state(n), Dr, ALU.mult).then_inc(scale_prod, 1)
                                nc.vector.tensor_tensor(scale_b[:, :, :], state(n), Di, ALU.mult).then_inc(scale_prod, 1)

                            def scale(n):
                                dve.wait_ge(scale_prod, (n + done) * 2 + 2)
                                nc.vector.tensor_tensor(state(n)[:, 0], scale_a[:, 0], scale_b[:, 1],
                                                        ALU.subtract).then_inc(scaled, 1)
                                nc.vector.scalar_tensor_tensor(state(n)[:, 1], scale_b[:, 0], -1.0, scale_a[:, 1],
                                                               ALU.mult, ALU.subtract).then_inc(scaled, 1)

                            def step(c):
                                first = c.loop is None and c.off == 0
                                n = c.n
                                for m in range(2):
                                    nc.vector.tensor_tensor(scan_b[:, m], cross[:, m], state(n)[:, 1 - m],
                                                            ALU.mult).then_inc(scan_prod, 1)
                                nc.vector.tensor_tensor(scan_a[:, :, :], same, state(n), ALU.mult).then_inc(scan_prod, 1)
                                if not first:
                                    scale_products(n - 1)
                                dve.wait_ge(scan_prod, (n + done) * 3 + 3)
                                nc.vector.tensor_tensor(scan_a[:, :, :], scan_a[:, :, :], scan_b[:, :, :],
                                                        ALU.add).then_inc(scan_sum, 1)
                                if not first:
                                    scale(n - 1)
                                dve.wait_ge(scan_sum, (n + done) * 2 + 1)
                                nc.vector.tensor_tensor(state(n + 1), state(n + 1), scan_a[:, :, :],
                                                        ALU.add).then_inc(scan_sum, 1)
                                dve.wait_ge(scan_sum, (n + done) * 2 + 2)

                            run_steps(dve, 0, CH - 1, 6, 1, 2, step)
                            scale_products(CH - 2)
                            scale(CH - 2)

                    @block.gpsimd
                    def _(pool):
                        nc.gpsimd.memset(carry[:, :, :, 0:1, :], 0.0).then_inc(cleared, 1)
                        pool.wait_ge(cleared, 1)

                        def save_taps(b):
                            pool.wait_ge(kpad_step, 2 * (b + 1))
                            pool.dma_start(kernel_d[b * P:(b + 1) * P, :], kpad[:, :]).then_inc(kpad_saved, 16)

                        save_taps(0)
                        for kind, b in ORDER:
                            if kind == "out":
                                if b + 1 < NBATCH:
                                    save_taps(b + 1)
                                pool.wait_ge(scaled, 2 + 2 * (CH - 1) * (b + 1))
                                with pool.Fori(0, BG // 4) as i:
                                    for r in range(4):
                                        g = group(i, r, b)
                                        pool.wait_ge(y_ready, g.n + 3)
                                        hold(pool, b_passed["pool"])
                                        nc.gpsimd.tensor_tensor(
                                            carry[:, g.slot(2), :, 1:CH, :],
                                            states[:, b % XR, 0:CH - 1, :, ds(i * 4 + r, 1)]
                                            .rearrange("p c m a -> p m (c a)").unsqueeze(3).to_broadcast([P, 2, CH - 1, Q]),
                                            head_mask[:, :].unsqueeze(1).unsqueeze(1).to_broadcast([P, 2, CH - 1, Q]),
                                            ALU.mult).then_inc(carry_ready, 1)

        with ExitStack() as ctx:
            sb, ps, sem = tensors(ctx)
            gw_hi, gw_lo = sb("gw_hi", [P, KD, 2 * D], F32R), sb("gw_lo", [P, KD, 2 * D], F32R)
            ow_hi, ow_lo = sb("ow_hi", [P, KD, D], F32R), sb("ow_lo", [P, KD, D], F32R)
            glu_bias, half_bias = sb("glu_bias", [P, 2 * KD]), sb("half_bias", [P, KD])
            out_bias = sb("out_bias", [P, D])
            y_t, xc = sb("y_t", [P, 2, TB, D]), sb("xc", [P, 2, TB, D])
            g_f = sb("g_f", [P, 2, BT])
            g_hi, g_lo = sb("g_hi", [P, 2, KD, BT], F32R), sb("g_lo", [P, 2, KD, BT], F32R)
            th, za_b, v_f = sb("th", [P, 2, BT]), sb("za_b", [P, 2, BT]), sb("v_f", [P, 2, BT])
            v_hi, v_lo = sb("v_hi", [P, 2, KD, BT], F32R), sb("v_lo", [P, 2, KD, BT], F32R)
            xn_c, xnb, r_t, rn = (sb(n, [P, 2, D]) for n in ("xn_c", "xnb", "r_t", "rn"))
            x1_t, x2_t = sb("x1_t", [P, 2, TB, D]), sb("x2_t", [P, 2, D])
            x2T = sb("x2T", [P, 2, KD, P])
            stc, mvc = sb("stc", [P, 3, 4, 6]), sb("mvc", [P, 3, 4, 2])
            varc, rstdc = sb("varc", [P, 3, 4, 1]), sb("rstdc", [P, 3, 4, 1])
            typ, zp = ps("typ", [P, 512]), ps("zp", [P, 2, 2, 512])
            op, txp = ps("op", [P, 2, 512]), ps("txp", [P, 512])

            wl, bl, ws_, wstep = sem("wl"), sem("bl"), sem("ws_"), sem("wstep")
            y_loaded = [sem(f"y_loaded{i}") for i in range(2)]
            xc_loaded = [sem(f"xc_loaded{i}") for i in range(2)]
            (ty_ready, g_ready, g_hi_ready, g_lo_ready, z_ready, th_ready, za_ready, v_ready_c, v_hi_ready, v_lo_ready,
             o_ready, r_ready, rn_ready, x1_ready, x2_ready, tx_ready, x2T_ready, xn_done, xnb_ready) = (
                sem(n) for n in ("ty_ready", "g_ready", "g_hi_ready", "g_lo_ready", "z_ready", "th_ready", "za_ready",
                                 "v_ready_c", "v_hi_ready", "v_lo_ready", "o_ready", "r_ready", "rn_ready", "x1_ready",
                                 "x2_ready", "tx_ready", "x2T_ready", "xn_done", "xnb_ready"))
            stat, aggr, var_c, root = ([sem(f"{n}_{w}") for w in ("x", "r", "x1")] for n in ("stat", "aggr", "var", "root"))
            x1_saved = [sem(f"x1_saved{i}") for i in range(2)]
            x2T_saved = [sem(f"x2T_saved{i}") for i in range(2)]
            dve_held = sem("dve_held")
            gw_stage = x1_t[:, :, :, :].rearrange("p a k t -> p (a k t)").rearrange("p (k n) -> p k n", k=KD)
            ow_stage = xc[:, 1]

            def of_block(a):
                return a.slot(8) // 4, a.slot(8) % 4

            def quarters(eng, step, first=-5, last=8):
                run_steps(eng, first, CH + last, 8, 16, 14, step)

            with nc.Block() as block:
                @block.sync
                def _(sp):
                    sp.dma_start(gw_stage, glu_WT.rearrange("(k p) n -> p k n", p=P)).then_inc(wl, 16)
                    sp.dma_start(ow_stage, out_WT.rearrange("(k p) n -> p k n", p=P)).then_inc(wl, 16)
                    sp.dma_start(glu_bias[:, :], glu_b).then_inc(bl, 16)
                    sp.dma_start(out_bias[:, :], out_b.partition_broadcast(P)).then_inc(bl, 16)
                    x_b = x.rearrange("(b j p) d -> b p j d", p=P, j=TB)
                    y_b = y_d.rearrange("(b j) p d -> b p j d", j=TB)
                    x1_b = x1_d.rearrange("(b j) p d -> b p j d", j=TB)
                    def one(ap, n):
                        return ap[ds(n, 1)].rearrange("a p j d -> (a p) j d")

                    def step(s):
                        b = s + 2
                        if b.within(NBLK):
                            if b.reuses(2):
                                sp.wait_ge(ty_ready, (b.n - 1) * 4)
                            sp.dma_start(y_t[:, b.slot(2)], one(y_b, b.n)).then_inc(y_loaded[b.slot(2)], 16)
                        if s.within(NBLK):
                            if s.reuses(2):
                                sp.wait_ge(x1_ready, (s.n - 1) * 4)
                            if s.loop is None and s.off == 1:
                                sp.wait_ge(wstep, 1)
                            sp.dma_start(xc[:, s.slot(2)], one(x_b, s.n)).then_inc(xc_loaded[s.slot(2)], 16)
                        b = s + (-3)
                        if b.within(NBLK):
                            sp.wait_ge(x1_ready, b.n * 4 + 4)
                            sp.dma_start(one(x1_b, b.n), x1_t[:, b.slot(2)]).then_inc(x1_saved[b.slot(2)], 16)

                    run_steps(sp, -2, NBLK + 3, 2, 6, 5, step)
                    for i in range(2):
                        sp.wait_ge(x1_saved[i], 16 * NBLK // 2)
                        sp.wait_ge(x2T_saved[i], 16 * CH // 2)

                @block.tensor
                def _(pe):
                    def step(m):
                        if m.loop is None and m.off == 0:
                            pe.wait_ge(wstep, 4)
                        if m.within(CH):
                            bs, o = of_block(m)
                            pe.wait_ge(g_lo_ready, m.n + 1 + (3 - o))
                            if m.reuses(2):
                                pe.wait_ge(th_ready, m.n - 1)
                                pe.wait_ge(za_ready, m.n - 1)
                            for half in range(2):
                                cols = slice(half * D + o * P, half * D + (o + 1) * P)
                                last = three_pass(zp[:, m.slot(2), half], KD,
                                                  lambda k: (gw_hi[:, k, cols], gw_lo[:, k, cols]),
                                                  lambda k: (g_hi[:, bs, k], g_lo[:, bs, k]))
                            last.then_inc(z_ready, 1)
                        a = m + 5
                        if a.within(CH):
                            bs, k = of_block(a)
                            if k == 0:
                                pe.wait_ge(y_loaded[bs], 16 * a.turn(8) + 16)
                            if a.reuses(1):
                                pe.wait_ge(g_ready, a.n)
                            for j in range(TB):
                                last = nc.tensor.transpose(typ[:, j * P:(j + 1) * P],
                                                           y_t[:, bs, j, k * P:(k + 1) * P], ident[:, :])
                            last.then_inc(ty_ready, 1)
                        a = m + (-4)
                        if a.within(CH):
                            bs, j = of_block(a)
                            pe.wait_ge(v_lo_ready, a.n + 1 + (3 - j))
                            if a.reuses(2):
                                pe.wait_ge(r_ready, a.n - 1)
                            toks = slice(j * P, (j + 1) * P)
                            three_pass(op[:, a.slot(2)], KD,
                                       lambda k: (v_hi[:, bs, k, toks], v_lo[:, bs, k, toks]),
                                       lambda k: (ow_hi[:, k], ow_lo[:, k])).then_inc(o_ready, 1)
                        a = m + (-7)
                        if a.within(CH):
                            pe.wait_ge(x2_ready, a.n + 1)
                            if a.reuses(1):
                                pe.wait_ge(x2T_ready, a.n)
                            for k in range(KD):
                                last = nc.tensor.transpose(txp[:, k * P:(k + 1) * P],
                                                           x2_t[:, a.slot(2), k * P:(k + 1) * P], ident[:, :])
                            last.then_inc(tx_ready, 1)

                    quarters(pe, step)

                @block.scalar
                def _(act):
                    act.wait_ge(wl, 32)
                    nc.scalar.activation(gw_hi[:, :, :], gw_stage, ACT.Copy).then_inc(ws_, 1)
                    nc.scalar.activation(ow_hi[:, :, :], ow_stage, ACT.Copy).then_inc(ws_, 1)
                    def step(m):
                        if m.loop is None and m.off == 0:
                            act.wait_ge(wstep, 4)
                        if m.within(CH):
                            o, r = m.slot(4), m.slot(2)
                            act.wait_ge(z_ready, m.n + 1)
                            if m.reuses(2):
                                act.wait_ge(v_ready_c, m.n - 1)
                            nc.scalar.activation(th[:, r], zp[:, r, 1], ACT.Tanh, bias=half_bias[:, o:o + 1],
                                                 scale=0.5).then_inc(th_ready, 1)
                            nc.scalar.activation(za_b[:, r], zp[:, r, 0], ACT.Identity, bias=glu_bias[:, o:o + 1],
                                                 scale=1.0).then_inc(za_ready, 1)
                        a = m + 5
                        if a.within(CH):
                            bs, k = of_block(a)
                            act.wait_ge(ty_ready, a.n + 1)
                            if a.reuses(2):
                                act.wait_ge(g_lo_ready, a.n - 1)
                            nc.scalar.activation(g_f[:, a.slot(2)], typ[:, :], ACT.Gelu).then_inc(g_ready, 1)
                            if a.reuses(8):
                                act.wait_ge(z_ready, a.n - 4 - k)
                            act.wait_ge(g_ready, a.n + 1)
                            nc.scalar.activation(g_hi[:, bs, k], g_f[:, a.slot(2)], ACT.Copy).then_inc(g_hi_ready, 1)
                        if m.within(CH):
                            bs, o = of_block(m)
                            act.wait_ge(v_ready_c, m.n + 1)
                            if m.reuses(8):
                                act.wait_ge(o_ready, m.n - 4 - o)
                            nc.scalar.activation(v_hi[:, bs, o], v_f[:, m.slot(2)], ACT.Copy).then_inc(v_hi_ready, 1)
                        a = m + (-7)
                        if a.within(CH):
                            act.wait_ge(tx_ready, a.n + 1)
                            if a.reuses(2):
                                act.wait_ge(x2T_saved[a.slot(2)], 16 * a.turn(2))
                            nc.scalar.activation(x2T[:, a.slot(2)], txp[:, :].rearrange("p (k t) -> p k t", k=KD),
                                                 ACT.Copy).then_inc(x2T_ready, 1)
                        a = m + (-8)
                        if a.within(CH):
                            act.wait_ge(x2T_ready, a.n + 1)
                            act.dma_start(x2T_d.rearrange("(k p) t -> p k t", p=P)[:, :, ds(a.n * P, P)],
                                          x2T[:, a.slot(2)]).then_inc(x2T_saved[a.slot(2)], 16)

                    quarters(act, step)

                @block.vector
                def _(dve):
                    dve.wait_ge(ws_, 2)
                    nc.vector.tensor_tensor(ow_lo[:, :, :], ow_stage, ow_hi[:, :, :].bitcast(F32),
                                            ALU.subtract).then_inc(wstep, 1)
                    nc.vector.tensor_tensor(gw_lo[:, :, :], gw_stage, gw_hi[:, :, :].bitcast(F32),
                                            ALU.subtract).then_inc(wstep, 1)
                    dve.wait_ge(bl, 32)
                    nc.vector.tensor_scalar(half_bias[:, :], glu_bias[:, KD:2 * KD], 0.5, None, ALU.mult).then_inc(wstep, 1)
                    nc.vector.memset(stc[:, :, :, :], 0.0).then_inc(wstep, 1)
                    dve.wait_ge(wstep, 4)

                    def variance(which, a, src):
                        i = a.slot(4)
                        nc.vector.bn_stats(stc[:, which, i], src).then_inc(stat[which], 1)
                        dve.wait_ge(stat[which], a.n + 1)
                        hold(dve, dve_held)
                        nc.vector.bn_aggr(mvc[:, which, i], stc[:, which, i]).then_inc(aggr[which], 1)
                        dve.wait_ge(aggr[which], a.n + 1)
                        nc.vector.tensor_scalar(varc[:, which, i], mvc[:, which, i, 1:2], EPS, None,
                                                ALU.add).then_inc(var_c[which], 1)

                    def normalise(which, a, dst, src, done):
                        i = a.slot(4)
                        dve.wait_ge(root[which], a.n + 1)
                        nc.vector.tensor_scalar(dst, src, mvc[:, which, i, 0:1], rstdc[:, which, i], ALU.subtract,
                                                ALU.mult).then_inc(done, 1)

                    def step(m):
                        a = m + (-6)
                        if a.within(CH):
                            bs, j = of_block(a)
                            if a.reuses(2):
                                dve.wait_ge(tx_ready, a.n - 1)
                            normalise(2, a, x2_t[:, a.slot(2)], x1_t[:, bs, j], x2_ready)
                        a = m + (-5)
                        if a.within(CH):
                            if a.reuses(2):
                                dve.wait_ge(x1_ready, a.n - 1)
                            normalise(1, a, rn[:, a.slot(2)], r_t[:, a.slot(2)], rn_ready)
                        a = m + (-3)
                        if a.within(CH):
                            bs, j = of_block(a)
                            if j == 0:
                                dve.wait_ge(xc_loaded[bs], 16 * a.turn(8) + 16)
                            variance(0, a, xc[:, bs, j])
                        a = m + (-4)
                        if a.within(CH):
                            bs, j = of_block(a)
                            if a.reuses(2):
                                dve.wait_ge(xnb_ready, a.n - 1)
                            normalise(0, a, xn_c[:, a.slot(2)], xc[:, bs, j], xn_done)
                        if m.within(CH):
                            r = m.slot(2)
                            dve.wait_ge(th_ready, m.n + 1)
                            dve.wait_ge(za_ready, m.n + 1)
                            if m.reuses(2):
                                dve.wait_ge(v_lo_ready, m.n - 1)
                            nc.vector.scalar_tensor_tensor(v_f[:, r], th[:, r], 1.0, za_b[:, r], ALU.add,
                                                           ALU.mult).then_inc(v_ready_c, 1)
                        a = m + 5
                        if a.within(CH):
                            bs, k = of_block(a)
                            dve.wait_ge(g_hi_ready, a.n + 1)
                            nc.vector.tensor_tensor(g_lo[:, bs, k], g_f[:, a.slot(2)], g_hi[:, bs, k].bitcast(F32),
                                                    ALU.subtract).then_inc(g_lo_ready, 1)
                        if m.within(CH):
                            bs, o = of_block(m)
                            dve.wait_ge(v_hi_ready, m.n + 1)
                            nc.vector.tensor_tensor(v_lo[:, bs, o], v_f[:, m.slot(2)], v_hi[:, bs, o].bitcast(F32),
                                                    ALU.subtract).then_inc(v_lo_ready, 1)
                        a = m + (-4)
                        if a.within(CH):
                            dve.wait_ge(o_ready, a.n + 1)
                            dve.wait_ge(xnb_ready, a.n + 1)
                            nc.vector.scalar_tensor_tensor(r_t[:, a.slot(2)], op[:, a.slot(2)], 0.5, xnb[:, a.slot(2)],
                                                           ALU.mult, ALU.add).then_inc(r_ready, 1)
                            dve.wait_ge(r_ready, a.n + 1)
                            variance(1, a, r_t[:, a.slot(2)])
                        a = m + (-5)
                        if a.within(CH):
                            bs, j = of_block(a)
                            dve.wait_ge(x1_ready, a.n + 1)
                            variance(2, a, x1_t[:, bs, j])

                    quarters(dve, step)

                @block.gpsimd
                def _(pool):
                    def root_of(which, a):
                        i = a.slot(4)
                        pool.wait_ge(var_c[which], a.n + 1)
                        nc.gpsimd.tensor_tensor(rstdc[:, which, i], varc[:, which, i], minus_half[:, :],
                                                ALU.pow).then_inc(root[which], 1)

                    def step(m):
                        a = m + (-5)
                        if a.within(CH):
                            bs, j = of_block(a)
                            pool.wait_ge(rn_ready, a.n + 1)
                            if a.reuses(8) and j == 0:
                                pool.wait_ge(x1_saved[bs], 16 * a.turn(8))
                            nc.gpsimd.tensor_tensor(x1_t[:, bs, j], rn[:, a.slot(2)], xc[:, bs, j],
                                                    ALU.add).then_inc(x1_ready, 1)
                        a = m + (-3)
                        if a.within(CH):
                            root_of(0, a)
                        a = m + (-4)
                        if a.within(CH):
                            pool.wait_ge(xn_done, a.n + 1)
                            if a.reuses(2):
                                pool.wait_ge(r_ready, a.n - 1)
                            nc.gpsimd.tensor_tensor(xnb[:, a.slot(2)], xn_c[:, a.slot(2)], out_bias[:, :],
                                                    ALU.add).then_inc(xnb_ready, 1)
                            root_of(1, a)
                        a = m + (-5)
                        if a.within(CH):
                            root_of(2, a)

                    pool.wait_ge(bl, 32)
                    quarters(pool, step)

        with ExitStack() as ffn:
            sb, _, _ = tensors(ffn)
            m1_hi, m1_lo = sb("m1_hi", [P, KD, F], F32R), sb("m1_lo", [P, KD, F], F32R)
            m2_hi, m2_lo = sb("m2_hi", [P, FT, D], F32R), sb("m2_lo", [P, FT, D], F32R)
            mb1, mb2 = sb("mb1", [P, FT]), sb("mb2", [P, D])
            gate_sum = sb("gate_sum", [P, KD, NBLK])
            gate = sb("gate", [P, E])

            with ExitStack() as ctx:
                sb, ps, sem = tensors(ctx)
                gs = sb("gs", [P, KD, D])
                gt_hi, gt_lo = sb("gt_hi", [P, KD, D], F32R), sb("gt_lo", [P, KD, D], F32R)
                gate_bias = sb("gate_bias", [P, KD])
                x2_in = sb("x2_in", [P, 2, KD, BT])
                xg_hi, xg_lo = sb("xg_hi", [P, 2, KD, BT], F32R), sb("xg_lo", [P, 2, KD, BT], F32R)
                relu = sb("relu", [P, BT])
                hp = ps("hp", [P, 4, 512])
                gw_loaded, gsplit, gb_loaded = sem("gw_loaded"), sem("gsplit"), sem("gb_loaded")
                xg_loaded = [sem(f"xg_loaded{i}") for i in range(2)]
                xg_hi_ready, xg_lo_ready, h_ready, h_summed = (
                    sem("xg_hi_ready"), sem("xg_lo_ready"), sem("h_ready"), sem("h_summed"))
                h_passed = sem("h_passed")

                with nc.Block() as block:
                    @block.sync
                    def _(sp):
                        sp.dma_start(gs[:, :, :], gate_w1T.rearrange("(k p) o -> p k o", p=P)).then_inc(gw_loaded, 16)
                        sp.dma_start(gate_bias[:, :], gate_b1).then_inc(gb_loaded, 16)
                        x2T_b = x2T_d.rearrange("(k p) t -> p k t", p=P)

                        def step(s):
                            if s.reuses(2):
                                sp.wait_ge(xg_lo_ready, s.n - 1)
                            sp.dma_start(x2_in[:, s.slot(2)], x2T_b[:, :, ds(s.n * BT, BT)]
                                         ).then_inc(xg_loaded[s.slot(2)], 16)

                        run_steps(sp, 0, NBLK, 2, 2, 2, step)

                    @block.scalar
                    def _(act):
                        act.wait_ge(gw_loaded, 16)
                        nc.scalar.activation(gt_hi[:, :, :], gs[:, :, :], ACT.Copy).then_inc(gsplit, 1)
                        act.wait_ge(gb_loaded, 16)

                        def step(s):
                            a = s + 1
                            if a.within(NBLK):
                                act.wait_ge(xg_loaded[a.slot(2)], 16 * a.turn(2) + 16)
                                if a.reuses(2):
                                    act.wait_ge(h_ready, 4 * (a.n - 1))
                                nc.scalar.activation(xg_hi[:, a.slot(2)], x2_in[:, a.slot(2)],
                                                     ACT.Copy).then_inc(xg_hi_ready, 1)
                            if s.within(NBLK):
                                for o in range(KD):
                                    act.wait_ge(h_ready, 4 * s.n + o + 1)
                                    if o or s.reuses(1):
                                        act.wait_ge(h_summed, 4 * s.n + o)
                                    hold(act, h_passed)
                                    nc.scalar.activation(relu[:, :], hp[:, o], ACT.Relu, bias=gate_bias[:, o:o + 1],
                                                         scale=1.0, accum_out=gate_sum[:, o, ds(s.n, 1)]
                                                         ).then_inc(h_summed, 1)

                        run_steps(act, -1, NBLK, 2, 2, 2, step)

                    @block.vector
                    def _(dve):
                        dve.wait_ge(gsplit, 1)
                        nc.vector.tensor_tensor(gt_lo[:, :, :], gs[:, :, :], gt_hi[:, :, :].bitcast(F32),
                                                ALU.subtract).then_inc(gsplit, 1)

                        def step(s):
                            dve.wait_ge(xg_hi_ready, s.n + 1)
                            i = s.slot(2)
                            nc.vector.tensor_tensor(xg_lo[:, i], x2_in[:, i], xg_hi[:, i].bitcast(F32),
                                                    ALU.subtract).then_inc(xg_lo_ready, 1)

                        run_steps(dve, 0, NBLK, 2, 2, 2, step)

                    @block.tensor
                    def _(pe):
                        pe.wait_ge(gsplit, 2)

                        def step(s):
                            pe.wait_ge(xg_lo_ready, s.n + 1)
                            for o in range(KD):
                                if s.reuses(1):
                                    pe.wait_ge(h_summed, 4 * (s.n - 1) + o + 1)
                                cols = slice(o * P, (o + 1) * P)
                                three_pass(hp[:, o], KD, lambda k: (gt_hi[:, k, cols], gt_lo[:, k, cols]),
                                           lambda k: (xg_hi[:, s.slot(2), k], xg_lo[:, s.slot(2), k])
                                           ).then_inc(h_ready, 1)

                        run_steps(pe, 0, NBLK, 2, 2, 2, step)

            with ExitStack() as ctx:
                sb, ps, sem = tensors(ctx)
                PC = F // 2
                PIECES = KD * F // PC
                expert, base_w, mixed = sb("expert", [P, E, PC]), sb("base_w", [P, 2, PC]), sb("mixed", [P, 2, PC])
                g_mean, g_wide = sb("g_mean", [P, KD]), sb("g_wide", [P, KD, P])
                gw2, gb2 = sb("gw2", [P, KD, E]), sb("gb2", [P, E])
                tb1, tb2 = sb("tb1", [P, E, FT]), sb("tb2", [P, E, D])
                gp = ps("gp", [P, 512])
                small_loaded, g_step, g_prod, g_ready, bias_step = (
                    sem("small_loaded"), sem("g_step"), sem("g_prod"), sem("gate_ready"), sem("bias_step"))
                expert_loaded = [sem(f"expert_loaded{e}") for e in range(E)]
                base_loaded = [sem(f"base_loaded{i}") for i in range(2)]
                mix_step, mix_hi, mix_lo = sem("mix_step"), sem("mix_hi"), sem("mix_lo")
                mix_passed = sem("mix_passed")

                def pieces(eng, weight, step):
                    with eng.Fori(0, PIECES // 2) as i:
                        for r in range(2):
                            step(At(i + weight * (PIECES // 2), r, 2), i, r)

                def piece_of(weight, wide, i, r):
                    if weight == 0:
                        return wide.rearrange("(k p) (r f) -> k r p f", p=P, r=2)[ds(i, 1), r].rearrange("a p f -> (a p) f")
                    return wide.rearrange("(i r q p) h -> i r p q h", p=P, r=2, q=2)[ds(i, 1), r].rearrange(
                        "a p q h -> (a p) q h")

                def to(weight, tile):
                    return tile if weight == 0 else tile.rearrange("p (q h) -> p q h", q=2)

                def place(weight, half, i, r):
                    if weight == 0:
                        return half[:, ds(i, 1), r * PC:(r + 1) * PC].rearrange("p a f -> p (a f)")
                    return half[:, ds(i * 4 + 2 * r, 2), :].rearrange("p a f -> p (a f)")

                with nc.Block() as block:
                    @block.sync
                    def _(sp):
                        for weight, (W, TW) in enumerate(((W1T, TW1T), (W2T, TW2T))):
                            def step(s, i, r):
                                sp.wait_ge(mix_step, s.n * E + 1)
                                sp.dma_start(to(weight, base_w[:, r]), piece_of(weight, W, i, r)).then_inc(base_loaded[r], 16)
                                for e in range(E):
                                    sp.wait_ge(mix_step, (s.n + 1) * E + e + 1)
                                    sp.dma_start(to(weight, expert[:, e]), piece_of(weight, TW[e], i, r)
                                                 ).then_inc(expert_loaded[e], 16)
                            pieces(sp, weight, step)

                    @block.scalar
                    def _(act):
                        act.dma_start(gw2[:, :, :], gate_w2T.rearrange("(k p) e -> p k e", p=P)).then_inc(small_loaded, 16)
                        act.dma_start(gb2[:, :], gate_b2.partition_broadcast(P)).then_inc(small_loaded, 16)
                        act.dma_start(mb1[:, :], b1).then_inc(small_loaded, 16)
                        act.dma_start(mb2[:, :], b2.partition_broadcast(P)).then_inc(small_loaded, 16)
                        act.dma_start(tb1[:, :, :], Tb1T).then_inc(small_loaded, 16)
                        act.dma_start(tb2[:, :, :].rearrange("p e d -> p (e d)"),
                                      Tb2.rearrange("e d -> (e d)").partition_broadcast(P)).then_inc(small_loaded, 16)
                        for weight, hi in enumerate((m1_hi, m2_hi)):
                            def step(s, i, r):
                                act.wait_ge(mix_step, (s.n + 3) * E)
                                hold(act, mix_passed)
                                nc.scalar.activation(place(weight, hi, i, r), mixed[:, r], ACT.Copy).then_inc(mix_hi, 1)
                            pieces(act, weight, step)

                    @block.tensor
                    def _(pe):
                        pe.wait_ge(g_step, 3)
                        for k in range(KD):
                            last = nc.tensor.matmul(gp[:, 0:E], g_wide[:, k], gw2[:, k], start=(k == 0), stop=(k == KD - 1))
                        last.then_inc(g_prod, 1)

                    @block.vector
                    def _(dve):
                        dve.sem_inc(mix_step, 2 * E)
                        nc.vector.reduce_sum(g_mean[:, :], gate_sum[:, :, :], AX_X).then_inc(g_step, 1)
                        dve.wait_ge(g_step, 1)
                        nc.vector.tensor_scalar(g_mean[:, :], g_mean[:, :], 1.0 / L, None, ALU.mult).then_inc(g_step, 1)
                        dve.wait_ge(g_step, 2)
                        dve.wait_ge(small_loaded, 16 * 6)
                        nc.vector.tensor_copy(g_wide[:, :, :], g_mean[:, :].unsqueeze(2).to_broadcast([P, KD, P])
                                              ).then_inc(g_step, 1)
                        dve.wait_ge(g_prod, 1)
                        nc.vector.tensor_tensor(gate[:, :], gp[:, 0:E], gb2[:, :], ALU.add).then_inc(g_ready, 1)
                        dve.wait_ge(g_ready, 1)
                        count = 0
                        for e in range(E):
                            for dst, src in ((mb1, tb1), (mb2, tb2)):
                                if count > 1:
                                    dve.wait_ge(bias_step, count - 1)
                                nc.vector.scalar_tensor_tensor(dst[:, :], src[:, e], gate[:, e:e + 1], dst[:, :],
                                                               ALU.mult, ALU.add).then_inc(bias_step, 1)
                                count += 1
                        for weight, (hi, lo) in enumerate(((m1_hi, m1_lo), (m2_hi, m2_lo))):
                            def step(s, i, r):
                                dve.wait_ge(base_loaded[r], 16 * s.turn(2) + 16)
                                dve.wait_ge(mix_lo, s.n + 1)
                                for e in range(E):
                                    dve.wait_ge(expert_loaded[e], 16 * s.n + 16)
                                    if e:
                                        dve.wait_ge(mix_step, (s.n + 2) * E + e)
                                    nc.vector.scalar_tensor_tensor(mixed[:, r], expert[:, e], gate[:, e:e + 1],
                                                                   base_w[:, r] if e == 0 else mixed[:, r],
                                                                   ALU.mult, ALU.add).then_inc(mix_step, 1)
                                dve.wait_ge(mix_hi, s.n + 1)
                                nc.vector.tensor_tensor(place(weight, lo, i, r), mixed[:, r],
                                                        place(weight, hi, i, r).bitcast(F32),
                                                        ALU.subtract).then_inc(mix_lo, 1)
                            pieces(dve, weight, step)

                    @block.gpsimd
                    def _(pool):
                        pool.sem_inc(mix_lo, 2)

            with ExitStack() as ctx:
                sb, ps, sem = tensors(ctx)
                x2_f = sb("x2_f", [P, KD, BT])
                xf_hi, xf_lo = sb("xf_hi", [P, KD, BT], F32R), sb("xf_lo", [P, KD, BT], F32R)
                h_f = sb("h_f", [P, 2, BT])
                h_hi, h_lo = sb("h_hi", [P, 4, BT], F32R), sb("h_lo", [P, 4, BT], F32R)
                o_t, x1_f, fin = sb("o_t", [P, TB, D]), sb("x1_f", [P, TB, D]), sb("fin", [P, TB, D])
                stf, mvf = sb("stf", [P, TB, 6]), sb("mvf", [P, TB, 2])
                varf, rstdf = sb("varf", [P, TB, 1]), sb("rstdf", [P, TB, 1])
                hp2, opf = ps("hp2", [P, 4, 512]), ps("opf", [P, TB, 512])
                x2f_loaded, x1f_loaded, fin_saved = sem("x2f_loaded"), sem("x1f_loaded"), sem("fin_saved")
                xf_hi_ready, xf_lo_ready, h1_ready, hf_ready, h_hi_ready, h_lo_ready, mm2_done = (
                    sem(n) for n in ("xf_hi_ready", "xf_lo_ready", "h1_ready", "hf_ready", "h_hi_ready", "h_lo_ready",
                                     "mm2_done"))
                ot_ready, statf, aggrf, var_f, root_f, norm_f, fin_ready, f_held = (
                    sem(n) for n in ("ot_ready", "statf", "aggrf", "var_f", "root_f", "norm_f", "fin_ready", "f_held"))
                NM = NBLK * FT
                LAG = 2

                def tiles(eng, step):
                    run_steps(eng, -1, NM + FT // 2, FT, FT, FT + FT // 2, step)

                def block_of(m):
                    return (m.off // FT if m.loop is None else m.loop + m.off // FT), m.off % FT

                with nc.Block() as block:
                    @block.sync
                    def _(sp):
                        x2T_b = x2T_d.rearrange("(k p) t -> p k t", p=P)
                        x1_b = x1_d.rearrange("(b j) p d -> b p j d", j=TB)
                        out_b_ = out.rearrange("(b j p) d -> b p j d", j=TB, p=P)

                        def one(ap, n):
                            return ap[ds(n, 1)].rearrange("a p j d -> (a p) j d")

                        def step(s):
                            b = s + 1
                            if b.within(NBLK):
                                if b.reuses(1):
                                    sp.wait_ge(xf_lo_ready, b.n)
                                sp.dma_start(x2_f[:, :, :], x2T_b[:, :, ds(b.n * BT, BT)]).then_inc(x2f_loaded, 16)
                            b = s + (-1)
                            if s.within(NBLK):
                                if s.reuses(1):
                                    sp.wait_ge(fin_ready, (s.n + 1) * TB)
                                sp.dma_start(x1_f[:, :, :], one(x1_b, s.n)).then_inc(x1f_loaded, 16)
                            if b.within(NBLK):
                                sp.wait_ge(fin_ready, (b.n + 2) * TB)
                                sp.dma_start(one(out_b_, b.n), fin[:, :, :]).then_inc(fin_saved, 16)

                        run_steps(sp, -1, NBLK + 1, 1, 2, 2, step)
                        sp.wait_ge(fin_saved, 16 * NBLK)

                    @block.tensor
                    def _(pe):
                        def inner(m):
                            if not m.within(NM):
                                return
                            b, f = block_of(m)
                            if f == 0:
                                pe.wait_ge(xf_lo_ready, b + 1)
                            if m.reuses(4):
                                pe.wait_ge(hf_ready, m.n - 3)
                            cols = slice(f * P, (f + 1) * P)
                            three_pass(hp2[:, m.slot(4)], KD, lambda k: (m1_hi[:, k, cols], m1_lo[:, k, cols]),
                                       lambda k: (xf_hi[:, k], xf_lo[:, k])).then_inc(h1_ready, 1)

                        def outer(m):
                            if not m.within(NM):
                                return
                            b, f = block_of(m)
                            pe.wait_ge(h_lo_ready, m.n + 1)
                            s4 = m.slot(4)
                            for j in range(TB):
                                if f == 0 and m.reuses(FT):
                                    pe.wait_ge(ot_ready, (b - 1) * TB + j + 1)
                                toks = slice(j * P, (j + 1) * P)
                                passes = ((h_hi, m2_hi), (h_hi, m2_lo), (h_lo, m2_hi))
                                for n, (l, r) in enumerate(passes):
                                    last = nc.tensor.matmul(opf[:, j], l[:, s4, toks], r[:, f],
                                                            start=(f == 0 and n == 0), stop=(f == FT - 1 and n == 2))
                            last.then_inc(mm2_done, 1)

                        def step(m):
                            if m.off % FT == 0:
                                outer(m + (-LAG))
                                inner(m)
                            else:
                                inner(m)
                                outer(m + (-LAG))

                        tiles(pe, step)

                    @block.scalar
                    def _(act):
                        def split(b, first):
                            act.wait_ge(x2f_loaded, 16 * b + 16)
                            if not first:
                                act.wait_ge(h1_ready, b * FT)
                            nc.scalar.activation(xf_hi[:, :, :], x2_f[:, :, :], ACT.Copy).then_inc(xf_hi_ready, 1)

                        def step(m):
                            if m.loop is None and m.off == -1:
                                split(0, True)
                                return
                            if not m.within(NM):
                                return
                            b, f = block_of(m)
                            act.wait_ge(h1_ready, m.n + 1)
                            if m.reuses(2):
                                act.wait_ge(h_lo_ready, m.n - 1)
                            nc.scalar.activation(h_f[:, m.slot(2)], hp2[:, m.slot(4)], ACT.Gelu_apprx_tanh,
                                                 bias=mb1[:, f:f + 1], scale=1.0).then_inc(hf_ready, 1)
                            act.wait_ge(hf_ready, m.n + 1)
                            if m.reuses(4):
                                act.wait_ge(mm2_done, m.n - 3)
                            nc.scalar.activation(h_hi[:, m.slot(4)], h_f[:, m.slot(2)], ACT.Copy).then_inc(h_hi_ready, 1)
                            if f == FT - 1 and (m + FT).within(NM):
                                split(b + 1, False)

                        tiles(act, step)

                    @block.vector
                    def _(dve):
                        def split(b):
                            dve.wait_ge(xf_hi_ready, b + 1)
                            nc.vector.tensor_tensor(xf_lo[:, :, :], x2_f[:, :, :], xf_hi[:, :, :].bitcast(F32),
                                                    ALU.subtract).then_inc(xf_lo_ready, 1)

                        def step(m):
                            if m.loop is None and m.off == -1:
                                split(0)
                                return
                            b, f = block_of(m)
                            if m.within(NM):
                                dve.wait_ge(h_hi_ready, m.n + 1)
                                if m.reuses(4):
                                    dve.wait_ge(mm2_done, m.n - 3)
                                nc.vector.tensor_tensor(h_lo[:, m.slot(4)], h_f[:, m.slot(2)],
                                                        h_hi[:, m.slot(4)].bitcast(F32),
                                                        ALU.subtract).then_inc(h_lo_ready, 1)
                                if f == FT - 1 and (m + FT).within(NM):
                                    split(b + 1)
                            if not m.reuses(FT) or not (m + (-FT)).within(NM):
                                return
                            c = b - 1
                            if f == LAG - 1:
                                dve.wait_ge(mm2_done, b * FT)
                                dve.wait_ge(fin_ready, b * TB)
                                for j in range(TB):
                                    nc.vector.tensor_tensor(o_t[:, j], opf[:, j], mb2[:, :], ALU.add).then_inc(ot_ready, 1)
                            j = f - LAG
                            if 0 <= j < TB:
                                dve.wait_ge(ot_ready, c * TB + j + 1)
                                nc.vector.bn_stats(stf[:, j], o_t[:, j]).then_inc(statf, 1)
                                dve.wait_ge(statf, c * TB + j + 1)
                                hold(dve, f_held)
                                nc.vector.bn_aggr(mvf[:, j], stf[:, j]).then_inc(aggrf, 1)
                                dve.wait_ge(aggrf, c * TB + j + 1)
                                nc.vector.tensor_scalar(varf[:, j], mvf[:, j, 1:2], EPS, None, ALU.add).then_inc(var_f, 1)
                            j -= 1
                            if 0 <= j < TB:
                                dve.wait_ge(root_f, c * TB + j + 1)
                                nc.vector.tensor_scalar(o_t[:, j], o_t[:, j], mvf[:, j, 0:1], rstdf[:, j], ALU.subtract,
                                                        ALU.mult).then_inc(norm_f, 1)

                        tiles(dve, step)

                    @block.gpsimd
                    def _(pool):
                        def step(s):
                            pool.wait_ge(x1f_loaded, 16 * s.n + 16)
                            if s.reuses(1):
                                pool.wait_ge(fin_saved, 16 * s.n)
                            for j in range(TB):
                                pool.wait_ge(var_f, s.n * TB + j + 1)
                                nc.gpsimd.tensor_tensor(rstdf[:, j], varf[:, j], minus_half[:, :],
                                                        ALU.pow).then_inc(root_f, 1)
                                pool.wait_ge(norm_f, s.n * TB + j + 1)
                                nc.gpsimd.tensor_tensor(fin[:, j], o_t[:, j], x1_f[:, j], ALU.add).then_inc(fin_ready, 1)

                        pool.sem_inc(fin_ready, TB)
                        run_steps(pool, 0, NBLK, 1, 2, 2, step)


def laid_out(a):
    import numpy as np

    a = {k: np.asarray(v) for k, v in a.items()}
    x = a["L0_attn_x"][0]
    L, D = x.shape
    E, F, _ = a["L0_ffn_TW1"].shape
    N = a["L0_attn_C"].shape[1]
    Q, G = P // N, D * N // P
    columns = lambda v: v.reshape(-1, P).T
    by_group = lambda v: v.reshape(G, Q, N).transpose(1, 2, 0).reshape(P, G)
    given = {
        "x": x,
        "x_rev": x.reshape(L // P, P, D)[:, ::-1],
        "in_WT": a["L0_attn_in_W"].T,
        "in_b": a["L0_attn_in_b"],
        "log_dt": a["L0_attn_log_dt"].reshape(G, Q).T,
        "C_re": by_group(a["L0_attn_C"][..., 0]),
        "C_im": by_group(a["L0_attn_C"][..., 1]),
        "log_A_real": by_group(a["L0_attn_log_A_real"]),
        "A_imag": by_group(a["L0_attn_A_imag"]),
        "D_skip": columns(a["L0_attn_D_skip"]),
        "glu_WT": a["L0_attn_glu_W"].T,
        "glu_b": columns(a["L0_attn_glu_b"]),
        "out_WT": a["L0_attn_out_W"].T,
        "out_b": a["L0_attn_out_b"],
        "gate_w1T": a["L0_ffn_gate_w1"].T,
        "gate_b1": columns(a["L0_ffn_gate_b1"]),
        "gate_w2T": a["L0_ffn_gate_w2"].T,
        "gate_b2": a["L0_ffn_gate_b2"],
        "W1T": a["L0_ffn_W1"].T,
        "b1": columns(a["L0_ffn_b1"]),
        "W2T": a["L0_ffn_W2"].T,
        "b2": a["L0_ffn_b2"],
        "TW1T": a["L0_ffn_TW1"].transpose(0, 2, 1),
        "Tb1T": a["L0_ffn_Tb1"].reshape(E, F // P, P).transpose(2, 0, 1),
        "TW2T": a["L0_ffn_TW2"].transpose(0, 2, 1),
        "Tb2": a["L0_ffn_Tb2"],
    }
    return {k: np.ascontiguousarray(v) for k, v in given.items()}


def kernel(**inputs):
    import concourse.bacc as bacc
    from concourse.bass_utils import run_bass_kernel_spmd

    arrays = laid_out(inputs)
    nc = bacc.Bacc("TRN2", target_bir_lowering=False, num_devices=1)
    args = [nc.dram_tensor(f"in_{k}", v.shape, mybir.dt.from_np(v.dtype), kind="ExternalInput").ap()
            for k, v in arrays.items()]
    out = nc.dram_tensor("out", arrays["x"].shape, F32, kind="ExternalOutput").ap()
    s4d_glu_and_gated_ffn(nc, *args, out)
    r = run_bass_kernel_spmd(nc, [{f"in_{k}": v for k, v in arrays.items()}], core_ids=[0])
    return r.results[0]["out"][None]
```

```python
import math
from contextlib import ExitStack

import concourse.bass as bass
from concourse import mybir

F32 = mybir.dt.float32
F32R = mybir.dt.float32r
I32 = mybir.dt.int32
ALU = mybir.AluOpType
ACT = mybir.ActivationFunctionType
AX_X = mybir.AxisListType.X
ds = bass.ds

P = 128
EPS = 1e-5
ROUND = 12582912.0
LOG2E = 1.4426950408889634
LN2_HI, LN2_LO = 0.693359375, -2.12194440054690583e-4
TURN_HI, TURN_MID = 6.28125, 1.93500518798828125e-3
TURN_LO = 2 * math.pi - TURN_HI - TURN_MID


class At:

    def __init__(self, loop, off, unroll):
        self.loop, self.off, self.unroll = loop, off, unroll

    def __add__(self, k):
        return At(self.loop, self.off + k, self.unroll)

    @property
    def n(self):
        return self.off if self.loop is None else self.loop * self.unroll + self.off

    def turn(self, ring):
        assert self.unroll % ring == 0
        return self.off // ring if self.loop is None else self.loop * (self.unroll // ring) + self.off // ring

    def slot(self, ring):
        assert self.unroll % ring == 0
        return self.off % ring

    def within(self, count):
        return self.loop is not None or 0 <= self.off < count

    def reuses(self, ring):
        return self.loop is not None or self.off >= ring


def hold(eng, passed):
    eng.sem_inc(passed, 1)


def run_steps(eng, first, count, unroll, head, tail, step):
    loops = max(0, (count - tail - head) // unroll)
    if loops < 2:
        loops = 0
    for n in range(first, head):
        step(At(None, n, unroll))
    if loops:
        with eng.Fori(0, loops) as i:
            for r in range(unroll):
                step(At(i, head + r, unroll))
    for n in range(head + loops * unroll, count):
        step(At(None, n, unroll))


def s4d_glu_and_gated_ffn(
    nc, x, x_rev, in_WT, in_b, log_dt, C_re, C_im, log_A_real, A_imag, D_skip, glu_WT, glu_b, out_WT, out_b,
    gate_w1T, gate_b1, gate_w2T, gate_b2, W1T, b1, W2T, b2, TW1T, Tb1T, TW2T, Tb2, out,
):
    L, D = x.shape
    F = W1T.shape[1]
    E = TW1T.shape[0]
    N = 32
    Q = P // N
    G = D // Q
    CH = L // P
    KD = D // P
    FT = F // P
    BG = P // Q
    NBATCH = G // BG
    TB = 4
    BT = TB * P
    NBLK = CH // TB
    POW = 8

    scratch = lambda name, shape: nc.dram_tensor(name, shape, F32, kind="Internal").ap()
    powers_d = scratch("powers_d", (G, P, 2, P))
    kernel_d = scratch("kernel_d", (D, 2 * P))
    y_d = scratch("y_d", (CH, P, D))
    x1_d = scratch("x1_d", (CH, P, D))
    x2T_d = scratch("x2T_d", (D, L))
    part_d = scratch("part_d", (NBLK, P, TB, D))

    with ExitStack() as whole:
        def tensors(ctx):
            sb = lambda name, shape, dt=F32: ctx.enter_context(nc.sbuf_tensor(name, shape, dt))
            ps = lambda name, shape: ctx.enter_context(nc.psum_tensor(name, shape, F32))
            sem = lambda name: ctx.enter_context(nc.semaphore(name))
            return sb, ps, sem

        sb, _, _ = tensors(whole)
        ident = sb("ident", [P, P])
        minus_half = sb("minus_half", [P, 1])

        def three_pass(out_, pairs, lhs, rhs):
            last = None
            for k in range(pairs):
                lh, ll = lhs(k)
                rh, rl = rhs(k)
                for m, (a, b) in enumerate(((lh, rh), (lh, rl), (ll, rh))):
                    last = nc.tensor.matmul(out_, a, b, start=(k == 0 and m == 0),
                                            stop=(k == pairs - 1 and m == 2))
            return last

        with ExitStack() as conv:
            sb, _, _ = tensors(conv)
            u = sb("u", [P, CH, D])
            head_mask = sb("head_mask", [P, Q])
            scan_same = sb("scan_same", [P, 2, G])
            scan_cross = sb("scan_cross", [P, 2, G])
            scale_same = sb("scale_same", [P, 2, G])
            scale_cross = sb("scale_cross", [P, 2, G])
            tap_weights = sb("tap_weights", [P, 2, G, Q])
            skip = sb("skip", [P, KD])

            with ExitStack() as ctx:
                sb, ps, sem = tensors(ctx)
                x_t = sb("x_t", [P, 4, D])
                xn = sb("xn", [P, 2, D])
                xn_hi = sb("xn_hi", [P, 2, KD, P], F32R)
                xn_lo = sb("xn_lo", [P, 2, KD, P], F32R)
                w_hi = sb("w_hi", [P, KD, D], F32R)
                w_lo = sb("w_lo", [P, KD, D], F32R)
                in_bias = sb("in_bias", [P, D])
                total = sb("total", [P, 4, 1])
                minus_mean = sb("minus_mean", [P, 4, 1])
                squares = sb("squares", [P, 4, 1])
                passed_on = ps("passed_on", [P, D])
                var = sb("var", [P, 4, 1])
                rstd = sb("rstd", [P, 4, 1])
                shift = sb("shift", [P, 4, 1])
                w_pow = sb("w_pow", [P, 2, POW, G])
                GB = 8
                pw = sb("pw", [P, 2, GB, 2, P])
                pw_tmp = sb("pw_tmp", [P, GB, 2, P // 2])
                GQ = 4
                pq = sb("pq", [P, GQ, 2, P])
                pq_tmp = sb("pq_tmp", [P, GQ, P // 2])
                tp = ps("tp", [P, 2, 512])
                up = ps("up", [P, 2, 512])

                w_loaded, const_ready, w_split = sem("w_loaded"), sem("const_ready"), sem("w_split")
                ident_step = sem("ident_step")
                setup_loaded, setup_step, setup_ready = sem("setup_loaded"), sem("setup_step"), sem("setup_ready")
                x_loaded = [sem(f"x_loaded{i}") for i in range(4)]
                total_ready, mean_ready, squares_ready, var_ready, rstd_ready, shift_ready = (
                    sem(n) for n in ("total_ready", "mean_ready", "squares_ready", "var_ready", "rstd_ready",
                                     "shift_ready"))
                xn_ready, tp_ready, hi_ready, lo_ready, u_ready, u_stored = (
                    sem("xn_ready"), sem("tp_ready"), sem("hi_ready"), sem("lo_ready"), sem("u_ready"), sem("u_stored"))
                act_passed, pool_passed = sem("act_passed"), sem("pool_passed")
                pw_step, pw_saved = sem("pw_step"), [sem(f"pw_saved{i}") for i in range(2)]
                pq_step, pq_saved = sem("pq_step"), sem("pq_saved")

                SETUP_SHARE = 11 * G
                room = u[:, :, :].rearrange("p c d -> p (c d)")
                took = [CH * D - 14 * POW * G]
                setup_chunk = took[0] // D

                def take(*shape, dt=F32):
                    n = math.prod(shape)
                    t = room[:, took[0]:took[0] + n]
                    took[0] += n
                    if dt is not F32:
                        t = t.bitcast(dt)
                    names = "abc"[:len(shape)]
                    return t.rearrange(f"p ({' '.join(names)}) -> p {' '.join(names)}",
                                       **dict(zip(names, shape)))

                w_stage = take(KD, D)
                la_dt = take(2, G)
                a_im = take(1, G)
                c_ri = take(2, G)
                WIDE = (POW, G)

                done = [0]
                LAST = 7
                ROUNDS = G * 7 // 8 // GB
                POOL_FIRST = ROUNDS * GB
                POOL_ROUNDS = (G - POOL_FIRST) // GQ
                PW_STEPS = 2 + 4 * (POW - 1)

                def powers(dve, b, half):
                    s = b.slot(2)
                    base = b.n * PW_STEPS
                    if half == 0:
                        if b.reuses(2):
                            dve.wait_ge(pw_saved[s], 16 * b.turn(2))
                        nc.vector.memset(pw[:, s, :, 0, 0:1], 1.0).then_inc(pw_step, 1)
                        nc.vector.memset(pw[:, s, :, 1, 0:1], 0.0).then_inc(pw_step, 1)
                    for k in (range(POW - 2), [POW - 2])[half]:
                        n = 2 ** k
                        wr, wi = (w_pow[:, m, k, ds(b.n * GB, GB)].unsqueeze(2).unsqueeze(2)
                                  .to_broadcast([P, GB, 2, n]) for m in range(2))
                        low, high, t = pw[:, s, :, :, 0:n], pw[:, s, :, :, n:2 * n], pw_tmp[:, :, :, 0:n]
                        dve.wait_ge(pw_step, base + 2 + 4 * k)
                        nc.vector.tensor_tensor(t, low, wi, ALU.mult).then_inc(pw_step, 1)
                        nc.vector.tensor_tensor(high, low, wr, ALU.mult).then_inc(pw_step, 1)
                        dve.wait_ge(pw_step, base + 4 + 4 * k)
                        nc.vector.tensor_tensor(high[:, :, 0], high[:, :, 0], t[:, :, 1],
                                                ALU.subtract).then_inc(pw_step, 1)
                        nc.vector.tensor_tensor(high[:, :, 1], high[:, :, 1], t[:, :, 0],
                                                ALU.add).then_inc(pw_step, 1)

                def pool_powers(pool, b, part):
                    groups = ds(b.n * GQ + POOL_FIRST, GQ)
                    count = [2 + 6 * n for n in (0, 3, 5)] + [2 + 6 * 6 + 3]
                    count = [0 if part == 0 else count[part]]

                    def link(ins):
                        count[0] += 1
                        ins.then_inc(pq_step, 1)
                        pool.wait_ge(pq_step, b.n * (2 + 6 * (POW - 1)) + count[0])
                        hold(pool, pool_passed)

                    if part == 0:
                        if b.reuses(1):
                            pool.wait_ge(pq_saved, 16 * b.n)
                            hold(pool, pool_passed)
                        link(nc.gpsimd.memset(pq[:, :, 0, 0:1], 1.0))
                        link(nc.gpsimd.memset(pq[:, :, 1, 0:1], 0.0))
                    for k, parts in (((0, "ri"), (1, "ri"), (2, "ri")), ((3, "ri"), (4, "ri")), ((5, "ri"), (6, "r")),
                                     ((6, "i"),))[part]:
                        n = 2 ** k
                        wr, wi = (w_pow[:, m, k, groups].unsqueeze(2).to_broadcast([P, GQ, n]) for m in range(2))
                        re, im, t = pq[:, :, 0, 0:n], pq[:, :, 1, 0:n], pq_tmp[:, :, 0:n]
                        for which in parts:
                            high = pq[:, :, "ri".index(which), n:2 * n]
                            a, c, sign = (wr, wi, ALU.subtract) if which == "r" else (wi, wr, ALU.add)
                            link(nc.gpsimd.tensor_tensor(high, re, a, ALU.mult))
                            link(nc.gpsimd.tensor_tensor(t, im, c, ALU.mult))
                            link(nc.gpsimd.tensor_tensor(high, high, t, sign))
                    if part == 3:
                        pool.dma_start(powers_d[groups].rearrange("g p r j -> p g (r j)"),
                                       pq[:, :, :, :].rearrange("p g r j -> p g (r j)")).then_inc(pq_saved, 16)

                def save_powers(pool, b):
                    pool.wait_ge(pw_step, (b.n + 1) * PW_STEPS)
                    pool.dma_start(powers_d[ds(b.n * GB, GB)].rearrange("g p r j -> p g (r j)"),
                                   pw[:, b.slot(2)].rearrange("p g r j -> p g (r j)")).then_inc(pw_saved[b.slot(2)], 16)

                def round_at(s):
                    off = s.off - done[0]
                    return At(s.loop, off // 2, 4), off % 2

                with nc.Block() as block:
                    @block.sync
                    def _(sp):
                        sp.dma_start(w_stage, in_WT.rearrange("(k p) h -> p k h", p=P)).then_inc(w_loaded, 16)

                        def load(s):
                            if s.reuses(4):
                                sp.wait_ge(xn_ready, s.n - 3)
                            sp.dma_start(x_t[:, s.slot(4), :], x_rev[ds(s.n, 1)].rearrange("a p d -> (a p) d")
                                         ).then_inc(x_loaded[s.slot(4)], 16)

                        run_steps(sp, 0, CH, 4, 4, 4, load)

                    @block.scalar
                    def _(act):
                        act.dma_start(la_dt[:, 0], log_A_real).then_inc(setup_loaded, 16)
                        for q in range(Q):
                            act.dma_start(la_dt[N * q:N * q + N, 1], log_dt[q:q + 1, :].rearrange("a g -> (a g)")
                                          .partition_broadcast(N)).then_inc(setup_loaded, 16)
                        act.dma_start(a_im[:, 0], A_imag).then_inc(setup_loaded, 16)
                        act.dma_start(c_ri[:, 0], C_re).then_inc(setup_loaded, 16)
                        act.dma_start(c_ri[:, 1], C_im).then_inc(setup_loaded, 16)
                        act.dma_start(skip[:, :], D_skip).then_inc(setup_loaded, 16)
                        act.dma_start(in_bias[:, :], in_b.partition_broadcast(P)).then_inc(setup_loaded, 16)
                        act.wait_ge(w_loaded, 16)
                        nc.scalar.activation(w_hi[:, :, :], w_stage, ACT.Copy).then_inc(w_split, 1)

                        def step(s):
                            c = s + 2
                            if c.within(CH):
                                act.wait_ge(shift_ready, c.n + 1)
                                if c.reuses(2):
                                    act.wait_ge(tp_ready, c.n - 1)
                                i = c.slot(4)
                                nc.scalar.activation(xn[:, c.slot(2)], x_t[:, i], ACT.Identity, bias=shift[:, i],
                                                     scale=rstd[:, i]).then_inc(xn_ready, 1)
                            c = s + 1
                            if c.within(CH):
                                act.wait_ge(tp_ready, c.n + 1)
                                if c.reuses(2):
                                    act.wait_ge(u_ready, c.n - 1)
                                nc.scalar.activation(xn_hi[:, c.slot(2)].rearrange("p k t -> p (k t)"),
                                                     tp[:, c.slot(2), :], ACT.Copy).then_inc(hi_ready, 1)
                            c = s + 3
                            if c.within(CH):
                                act.wait_ge(mean_ready, c.n + 1)
                                act.wait_ge(total_ready, c.n + 1)
                                hold(act, act_passed)
                                i = c.slot(4)
                                nc.scalar.activation(passed_on[:, :], x_t[:, i], ACT.Square, bias=minus_mean[:, i],
                                                     scale=1.0, accum_out=squares[:, i]).then_inc(squares_ready, 1)
                            c = s + 4
                            if c.within(CH):
                                i = c.slot(4)
                                act.wait_ge(x_loaded[i], 16 * c.turn(4) + 16)
                                if c.reuses(1):
                                    act.wait_ge(squares_ready, c.n)
                                hold(act, act_passed)
                                nc.scalar.activation(passed_on[:, :], x_t[:, i], ACT.Identity, bias=0.0,
                                                     scale=1.0, accum_out=total[:, i]).then_inc(total_ready, 1)

                        run_steps(act, -4, CH, 4, 4, 4, step)

                    @block.tensor
                    def _(pe):
                        pe.wait_ge(ident_step, 2)
                        pe.wait_ge(w_split, 2)

                        def step(s):
                            c = s + 1
                            if c.within(CH):
                                pe.wait_ge(xn_ready, c.n + 1)
                                if c.reuses(2):
                                    pe.wait_ge(lo_ready, c.n - 1)
                                for k in range(KD):
                                    last = nc.tensor.transpose(tp[:, c.slot(2), k * P:(k + 1) * P],
                                                               xn[:, c.slot(2), k * P:(k + 1) * P], ident[:, :])
                                last.then_inc(tp_ready, 1)
                            if s.within(CH):
                                pe.wait_ge(lo_ready, s.n + 1)
                                if s.reuses(2):
                                    pe.wait_ge(u_stored, s.n - 1)
                                three_pass(up[:, s.slot(2), :], KD,
                                           lambda k: (xn_hi[:, s.slot(2), k], xn_lo[:, s.slot(2), k]),
                                           lambda k: (w_hi[:, k], w_lo[:, k])).then_inc(u_ready, 1)

                        run_steps(pe, -1, CH, 4, 4, 4, step)

                    @block.vector
                    def _(dve):
                        dve.wait_ge(w_split, 1)
                        nc.vector.tensor_tensor(w_lo[:, :, :], w_stage, w_hi[:, :, :].bitcast(F32),
                                                ALU.subtract).then_inc(w_split, 1)
                        dve.wait_ge(w_split, 2)

                        def step(s):
                            c = s + 2
                            if c.within(CH):
                                dve.wait_ge(rstd_ready, c.n + 1)
                                i = c.slot(4)
                                nc.vector.tensor_tensor(shift[:, i], minus_mean[:, i], rstd[:, i],
                                                        ALU.mult).then_inc(shift_ready, 1)
                            c = s + 1
                            if c.within(CH):
                                dve.wait_ge(hi_ready, c.n + 1)
                                nc.vector.tensor_tensor(
                                    xn_lo[:, c.slot(2)].rearrange("p k t -> p (k t)"), tp[:, c.slot(2), :],
                                    xn_hi[:, c.slot(2)].rearrange("p k t -> p (k t)").bitcast(F32),
                                    ALU.subtract).then_inc(lo_ready, 1)
                            if s.within(CH):
                                dve.wait_ge(u_ready, s.n + 1)
                                nc.vector.tensor_tensor(u[:, ds(s.n, 1), :].rearrange("p a d -> p (a d)"),
                                                        up[:, s.slot(2), :], in_bias[:, :],
                                                        ALU.add).then_inc(u_stored, 1)
                            c = s + 4
                            if c.within(CH):
                                dve.wait_ge(total_ready, c.n + 1)
                                i = c.slot(4)
                                nc.vector.tensor_scalar(minus_mean[:, i], total[:, i], -1.0 / D, None,
                                                        ALU.mult).then_inc(mean_ready, 1)
                            c = s + 3
                            if c.within(CH):
                                dve.wait_ge(squares_ready, c.n + 1)
                                i = c.slot(4)
                                nc.vector.tensor_scalar(var[:, i], squares[:, i], 1.0 / D, EPS, ALU.mult,
                                                        ALU.add).then_inc(var_ready, 1)

                        done[0] = -4

                        def chunk():
                            step(At(None, done[0], 8))
                            done[0] += 1

                        for _ in range(4):
                            chunk()
                        dve.wait_ge(setup_loaded, 16 * (6 + Q))
                        dve.wait_ge(const_ready, 2)
                        count, work = [0], [0]

                        def link(ins, size=G):
                            count[0] += 1
                            ins.then_inc(setup_step, 1)
                            dve.wait_ge(setup_step, count[0])
                            work[0] += size + G
                            if work[0] > SETUP_SHARE:
                                work[0] = 0
                                chunk()

                        def exp_of(dst, src, r, p, k, e_int, size):
                            link(nc.vector.tensor_scalar(src, src, -100.0, 88.3, ALU.max, ALU.min), size)
                            link(nc.vector.tensor_scalar(k, src, LOG2E, ROUND, ALU.mult, ALU.add), size)
                            link(nc.vector.tensor_scalar(k, k, -ROUND, -127.0, ALU.add, ALU.max), size)
                            link(nc.vector.scalar_tensor_tensor(r, k, -LN2_HI, src, ALU.mult, ALU.add), size)
                            link(nc.vector.scalar_tensor_tensor(r, k, -LN2_LO, r, ALU.mult, ALU.add), size)
                            link(nc.vector.tensor_scalar(p, r, 1.0 / math.factorial(8), None, ALU.mult), size)
                            for m in range(7, 0, -1):
                                link(nc.vector.scalar_tensor_tensor(p, p, 1.0 / math.factorial(m), r,
                                                                    ALU.add, ALU.mult), size)
                            link(nc.vector.tensor_scalar(k, k, 127.0, 8388608.0, ALU.add, ALU.mult), size)
                            link(nc.vector.tensor_copy(e_int, k), size)
                            link(nc.vector.scalar_tensor_tensor(dst, p, 1.0, e_int.bitcast(F32), ALU.add, ALU.mult), size)

                        two = [take(2, G) for _ in range(4)]
                        two_i = take(2, G, dt=I32)
                        exp_of(two[0], la_dt, two[1], two[2], two[3], two_i, 2 * G)
                        minus_a, dt_ = two[0][:, 0], two[0][:, 1]
                        re_k, ph_k = take(*WIDE), take(*WIDE)
                        link(nc.vector.scalar_tensor_tensor(re_k[:, 0], minus_a, -1.0, dt_, ALU.mult, ALU.mult))
                        for k in range(1, POW):
                            link(nc.vector.tensor_scalar(re_k[:, k], re_k[:, 0], float(2 ** k), None, ALU.mult))
                        ang, trn = take(1, G)[:, 0], take(1, G)[:, 0]
                        link(nc.vector.tensor_tensor(ang, a_im[:, 0], dt_, ALU.mult))
                        link(nc.vector.tensor_scalar(trn, ang, 1.0 / (2 * math.pi), ROUND, ALU.mult, ALU.add))
                        link(nc.vector.tensor_scalar(trn, trn, -ROUND, None, ALU.add))
                        for part in (TURN_HI, TURN_MID, TURN_LO):
                            link(nc.vector.scalar_tensor_tensor(ang, trn, -part, ang, ALU.mult, ALU.add))
                        link(nc.vector.tensor_scalar(ph_k[:, 0], ang, 1.0 / (2 * math.pi), None, ALU.mult))
                        for k in range(1, POW):
                            link(nc.vector.tensor_scalar(ang, ph_k[:, k - 1], 2.0, None, ALU.mult))
                            link(nc.vector.tensor_scalar(trn, ang, ROUND, None, ALU.add))
                            link(nc.vector.tensor_scalar(trn, trn, -ROUND, None, ALU.add))
                            link(nc.vector.tensor_tensor(ph_k[:, k], ang, trn, ALU.subtract))
                        mag, r_, p_, k_ = (take(*WIDE) for _ in range(4))
                        k_i = take(*WIDE, dt=I32)
                        exp_of(mag, re_k, r_, p_, k_, k_i, POW * G)
                        half, sq = r_, p_
                        sin_h, cos_h = k_, re_k
                        link(nc.vector.tensor_scalar(half, ph_k, math.pi, None, ALU.mult), POW * G)
                        link(nc.vector.tensor_tensor(sq, half, half, ALU.mult), POW * G)
                        for dst, top in ((sin_h, 13), (cos_h, 14)):
                            sign = lambda m: (-1.0) ** (m // 2)
                            link(nc.vector.tensor_scalar(dst, sq, sign(top) / math.factorial(top), None, ALU.mult), POW * G)
                            for m in range(top - 2, 1, -2):
                                link(nc.vector.scalar_tensor_tensor(dst, dst, sign(m) / math.factorial(m), sq,
                                                                    ALU.add, ALU.mult), POW * G)
                        link(nc.vector.scalar_tensor_tensor(sin_h, sin_h, 1.0, half, ALU.add, ALU.mult), POW * G)
                        link(nc.vector.tensor_scalar(cos_h, cos_h, 1.0, None, ALU.add), POW * G)
                        link(nc.vector.scalar_tensor_tensor(cos_h, cos_h, 2.0, sin_h, ALU.mult, ALU.mult), POW * G)
                        link(nc.vector.scalar_tensor_tensor(sin_h, sin_h, -2.0, sin_h, ALU.mult, ALU.mult), POW * G)
                        link(nc.vector.scalar_tensor_tensor(w_pow[:, 0], sin_h, 1.0, mag, ALU.add, ALU.mult), POW * G)
                        link(nc.vector.tensor_tensor(w_pow[:, 1], cos_h, mag, ALU.mult), POW * G)
                        w128r, w128i = w_pow[:, 0, POW - 1], w_pow[:, 1, POW - 1]
                        link(nc.vector.tensor_copy(scan_same[:, 0], w128r))
                        link(nc.vector.tensor_copy(scan_same[:, 1], w128r))
                        link(nc.vector.tensor_scalar(scan_cross[:, 0], w128i, -1.0, None, ALU.mult))
                        link(nc.vector.tensor_copy(scan_cross[:, 1], w128i))
                        wr, wi = w_pow[:, 0, 0], w_pow[:, 1, 0]
                        den, t, qr, qi, cr, ci, wm = (take(1, G)[:, 0] for _ in range(7))
                        link(nc.vector.tensor_tensor(den, minus_a, minus_a, ALU.mult))
                        link(nc.vector.tensor_tensor(t, a_im[:, 0], a_im[:, 0], ALU.mult))
                        link(nc.vector.tensor_tensor(den, den, t, ALU.add))
                        link(nc.vector.reciprocal(den, den))
                        link(nc.vector.tensor_scalar(wm, wr, -1.0, None, ALU.add))
                        link(nc.vector.tensor_tensor(qr, wi, a_im[:, 0], ALU.mult))
                        link(nc.vector.tensor_tensor(t, wm, minus_a, ALU.mult))
                        link(nc.vector.tensor_tensor(qr, qr, t, ALU.subtract))
                        link(nc.vector.tensor_tensor(qi, wm, a_im[:, 0], ALU.mult))
                        link(nc.vector.tensor_tensor(t, wi, minus_a, ALU.mult))
                        link(nc.vector.scalar_tensor_tensor(qi, qi, -1.0, t, ALU.mult, ALU.subtract))
                        link(nc.vector.tensor_tensor(qr, qr, den, ALU.mult))
                        link(nc.vector.tensor_tensor(qi, qi, den, ALU.mult))
                        C_r, C_i = c_ri[:, 0], c_ri[:, 1]
                        link(nc.vector.tensor_tensor(cr, C_r, qr, ALU.mult))
                        link(nc.vector.tensor_tensor(t, C_i, qi, ALU.mult))
                        link(nc.vector.tensor_tensor(cr, cr, t, ALU.subtract))
                        link(nc.vector.tensor_tensor(ci, C_r, qi, ALU.mult))
                        link(nc.vector.tensor_tensor(t, C_i, qr, ALU.mult))
                        link(nc.vector.tensor_tensor(ci, ci, t, ALU.add))
                        link(nc.vector.tensor_scalar(cr, cr, 2.0, None, ALU.mult))
                        link(nc.vector.tensor_scalar(ci, ci, 2.0, None, ALU.mult))
                        for q in range(Q):
                            link(nc.vector.tensor_scalar(tap_weights[:, 0, :, q], cr, head_mask[:, q:q + 1], None,
                                                         ALU.mult))
                            link(nc.vector.tensor_scalar(tap_weights[:, 1, :, q], ci, head_mask[:, q:q + 1], -1.0,
                                                         ALU.mult, ALU.mult))
                        link(nc.vector.tensor_tensor(qr, cr, wr, ALU.mult))
                        link(nc.vector.tensor_tensor(t, ci, wi, ALU.mult))
                        for m in range(2):
                            link(nc.vector.tensor_tensor(scale_same[:, m], qr, t, ALU.subtract))
                        link(nc.vector.tensor_tensor(qi, cr, wi, ALU.mult))
                        link(nc.vector.tensor_tensor(t, ci, wr, ALU.mult))
                        link(nc.vector.tensor_tensor(scale_cross[:, 1], qi, t, ALU.add))
                        nc.vector.tensor_scalar(scale_cross[:, 0], scale_cross[:, 1], -1.0, None,
                                                ALU.mult).then_inc(setup_ready, 1)
                        dve.wait_ge(setup_ready, 1)

                        assert done[0] <= setup_chunk and CH - LAST - done[0] < 2 * ROUNDS

                        def step_and_powers(s):
                            step(s)
                            b, half = round_at(s)
                            if s.loop is not None or b.off < ROUNDS:
                                powers(dve, b, half)

                        run_steps(dve, done[0], CH, 8, done[0] + 8, LAST, step_and_powers)
                        for n in range(CH - done[0], 2 * ROUNDS):
                            powers(dve, *round_at(At(None, done[0] + n, 8)))

                    @block.gpsimd
                    def _(pool):
                        nc.gpsimd.memset(minus_half[:, :], -0.5).then_inc(const_ready, 1)
                        nc.gpsimd.memset(ident[:, :], 0.0).then_inc(ident_step, 1)
                        pool.wait_ge(ident_step, 1)
                        nc.gpsimd.affine_select(out=ident[:, :], in_=ident[:, :], compare_op=ALU.not_equal, fill=1.0,
                                                base=0, pattern=[[-1, P]], channel_multiplier=1
                                                ).then_inc(ident_step, 1)
                        nc.gpsimd.memset(head_mask[:, :], 0.0).then_inc(ident_step, 1)
                        pool.wait_ge(ident_step, 3)
                        for q in range(Q):
                            last = nc.gpsimd.memset(head_mask[N * q:N * q + N, q:q + 1], 1.0)
                        last.then_inc(const_ready, 1)
                        pool.wait_ge(const_ready, 2)
                        hold(pool, pool_passed)

                        def step(s):
                            c = s + 3
                            if c.within(CH):
                                pool.wait_ge(var_ready, c.n + 1)
                                i = c.slot(4)
                                nc.gpsimd.tensor_tensor(rstd[:, i], var[:, i], minus_half[:, :],
                                                        ALU.pow).then_inc(rstd_ready, 1)

                        def step_and_save(s):
                            step(s)
                            b, half = round_at(s)
                            if half == 1 and (s.loop is not None or b.off < ROUNDS):
                                save_powers(pool, b)
                            off = s.off - done[0]
                            if half == 0 and (s.loop is not None or off // 8 < POOL_ROUNDS):
                                pool_powers(pool, At(s.loop, off // 8, 1), off % 8 // 2)

                        run_steps(pool, -3, done[0], 4, 1, 0, step)
                        pool.wait_ge(setup_ready, 1)
                        run_steps(pool, done[0], CH, 8, done[0] + 8, LAST, step_and_save)
                        for n in range((CH - done[0]) // 2, ROUNDS):
                            save_powers(pool, At(None, n, 4))
                        for n in range(CH - done[0] + (CH - done[0]) % 2, 8 * POOL_ROUNDS, 2):
                            pool_powers(pool, At(None, n // 8, 1), n % 8 // 2)
                        pool.wait_ge(pq_saved, 16 * POOL_ROUNDS)
                        for i in range(2):
                            pool.wait_ge(pw_saved[i], 16 * ROUNDS // 2)

            with ExitStack() as ctx:
                sb, ps, sem = tensors(ctx)
                XR = 3
                states = sb("states", [P, XR, CH, 2, BG])
                pg = sb("pg", [P, 4, 2, P])
                v = sb("v", [P, 2, 2, P])
                taps = sb("taps", [P, 4, Q, P])
                carry = sb("carry", [P, 2, 2, CH, Q])
                taps_t = sb("taps_t", [P, P])
                kpad = sb("kpad", [P, 2 * P])
                scan_a = sb("scan_a", [P, 2, BG])
                scan_b = sb("scan_b", [P, 2, BG])
                SC = 4
                scale_a = sb("scale_a", [P, SC, 2, BG])
                scale_b = sb("scale_b", [P, SC, 2, BG])
                vp = ps("vp", [P, 2, 512])
                xp = ps("xp", [P, 2, 512])
                kp = ps("kp", [P, 512])
                kt = ps("kt", [P, 512])
                yp = ps("yp", [P, 2, 512])

                pg_loaded = [sem(f"pg_loaded{i}") for i in range(4)]
                taps_loaded = [sem(f"taps_loaded{i}") for i in range(4)]
                pg_used, v_turned, v_ready, x_ready, x_kept = (
                    sem("pg_used"), sem("v_turned"), sem("v_ready"), sem("x_ready"), sem("x_kept"))
                taps_made, taps_copied, taps_turned, kpad_step, kpad_saved = (
                    sem("taps_made"), sem("taps_copied"), sem("taps_turned"), sem("kpad_step"), sem("kpad_saved"))
                scan_prod, scan_sum, scale_prod, scaled = (
                    sem("scan_prod"), sem("scan_sum"), sem("scale_prod"), sem("scaled"))
                cleared, carry_ready, y_ready, y_kept, y_saved = (
                    sem("cleared"), sem("carry_ready"), sem("y_ready"), sem("y_kept"), sem("y_saved"))
                kpad_cleared = sem("kpad_cleared")
                b_passed = {e: sem(f"b_passed_{e}") for e in ("pe", "act", "dve", "pool")}

                ORDER = [("in", 0), ("in", 1)]
                for b in range(NBATCH - 2):
                    ORDER += [("in", b + 2), ("out", b)]
                ORDER += [("out", NBATCH - 2), ("out", NBATCH - 1)]
                LOADS = {which: n * BG for n, which in enumerate(ORDER)}
                XN = CH * Q

                def group(i, r, b):
                    return At(i + b * (BG // 4), r, 4)

                def load_of(g, kind, b):
                    n = LOADS[kind, b] - b * BG
                    return g + n if g.loop is None else At(g.loop + n // 4, g.off, 4)

                def u_of(g):
                    return u[:, :, ds(g.n * Q, Q)]

                with nc.Block() as block:
                    @block.sync
                    def _(sp):
                        for kind, b in ORDER:
                            if kind == "out":
                                sp.wait_ge(kpad_saved, 16 * (b + 1))
                            with sp.Fori(0, BG // 4) as i:
                                for r in range(4):
                                    g = group(i, r, b)
                                    sp.wait_ge(pg_used, load_of(g, kind, b).n + 1)
                                    sp.dma_start(pg[:, r], powers_d[ds(g.n, 1)].rearrange("a p r j -> (a p) r j")
                                                 ).then_inc(pg_loaded[r], 16)
                                    if kind == "out":
                                        sp.wait_ge(y_ready, g.n + 1)
                                        rows = kernel_d[ds(g.n * Q, Q), 0:P]
                                        sp.dma_start(taps[:, r],
                                                     bass.AP(rows.tensor, rows.offset, [[1, P], [2 * P, Q], [1, P]])
                                                     ).then_inc(taps_loaded[r], 16)

                    @block.tensor
                    def _(pe):
                        pe.sem_inc(pg_used, 4)
                        pe.sem_inc(x_ready, 2)
                        pe.sem_inc(y_ready, 4)

                        def turn(g, local, b):
                            r = g.slot(4)
                            pe.wait_ge(pg_loaded[r], 16 * load_of(g, "in", b).turn(4) + 16)
                            pe.wait_ge(v_ready, g.n + 1)
                            for m in range(2):
                                last = nc.tensor.transpose(vp[:, g.slot(2), m * P:(m + 1) * P], pg[:, r, m], ident[:, :])
                            last.then_inc(v_turned, 1)
                            for m in range(2):
                                last = nc.tensor.matmul(kp[:, ds(local * Q, Q)], pg[:, r, m],
                                                        tap_weights[:, m, ds(g.n, 1), :].rearrange("p a q -> p (a q)"),
                                                        start=(m == 0), stop=(m == 1), skip_group_check=True)
                            last.then_inc(pg_used, 1)

                        def inputs(g):
                            pe.wait_ge(v_ready, g.n + 3)
                            pe.wait_ge(x_kept, g.n + 1)
                            for m in range(2):
                                last = nc.tensor.matmul(xp[:, g.slot(2), m * XN:(m + 1) * XN], v[:, g.slot(2), m],
                                                        u_of(g), start=True, stop=True)
                            last.then_inc(x_ready, 1)

                        for kind, b in ORDER:
                            if kind == "in":
                                if b > 0:
                                    pe.wait_ge(taps_copied, b)
                                g0 = At(None, b * BG, 4)
                                turn(g0, 0, b)
                                with pe.Fori(0, BG // 4 - 1) as i:
                                    for r in range(4):
                                        turn(group(i, r + 1, b), i * 4 + (r + 1), b)
                                        inputs(group(i, r, b))
                                for r in range(BG - 4, BG):
                                    if r + 1 < BG:
                                        turn(g0 + (r + 1), r + 1, b)
                                    inputs(g0 + r)
                                pe.wait_ge(taps_copied, b + 1)
                                if b > 0:
                                    pe.wait_ge(kpad_step, 2 * b)
                                nc.tensor.transpose(kt[:, 0:P], taps_t[:, :], ident[:, :]).then_inc(taps_turned, 1)
                            else:
                                with pe.Fori(0, BG // 4) as i:
                                    for r in range(4):
                                        g = group(i, r, b)
                                        s = g.slot(2)
                                        pe.wait_ge(pg_loaded[r], 16 * load_of(g, "out", b).turn(4) + 16)
                                        pe.wait_ge(taps_loaded[r], 16 * g.turn(4) + 16)
                                        pe.wait_ge(carry_ready, g.n + 1)
                                        pe.wait_ge(y_kept, g.n + 1)
                                        for m in range(2):
                                            last = nc.tensor.matmul(yp[:, s, 0:XN], pg[:, r, m],
                                                                    carry[:, s, m].rearrange("p c q -> p (c q)"),
                                                                    start=(m == 0), stop=False, skip_group_check=True)
                                        last.then_inc(pg_used, 1)
                                        for q in range(Q):
                                            last = nc.tensor.matmul(
                                                yp[:, s, 0:XN].rearrange("p (c q) -> p c q", q=Q)[:, :, q],
                                                taps[:, r, q],
                                                u[:, :, ds(g.n * Q + q, 1)].rearrange("p c a -> p (c a)"),
                                                start=False, stop=(q == Q - 1), skip_group_check=True)
                                        last.then_inc(y_ready, 1)

                    @block.scalar
                    def _(act):
                        act.sem_inc(v_ready, 2)
                        act.sem_inc(x_kept, 2)
                        act.sem_inc(y_kept, 2)

                        def copy_v(g):
                            act.wait_ge(v_turned, g.n + 1)
                            act.wait_ge(x_ready, g.n + 1)
                            nc.scalar.activation(v[:, g.slot(2)].rearrange("p m j -> p (m j)"), vp[:, g.slot(2), 0:2 * P],
                                                 ACT.Copy).then_inc(v_ready, 1)

                        def keep_x(g, local, b):
                            act.wait_ge(x_ready, g.n + 3)
                            hold(act, b_passed["act"])
                            for q in range(Q):
                                rows = slice(N * q, N * q + N)
                                last = nc.scalar.activation(
                                    states[rows, b % XR, :, :, ds(local, 1)].rearrange("p c m a -> p m (c a)"),
                                    xp[rows, g.slot(2), 0:2 * XN].rearrange("p (m c q) -> p m c q", m=2, q=Q)[:, :, :, q],
                                    ACT.Copy)
                            last.then_inc(x_kept, 1)

                        for kind, b in ORDER:
                            if kind == "in":
                                if b >= XR:
                                    act.wait_ge(carry_ready, BG * (b - XR + 1))
                                g0 = At(None, b * BG, 4)
                                copy_v(g0)
                                with act.Fori(0, BG // 4 - 1) as i:
                                    for r in range(4):
                                        copy_v(group(i, r + 1, b))
                                        keep_x(group(i, r, b), i * 4 + r, b)
                                for r in range(BG - 4, BG):
                                    if r + 1 < BG:
                                        copy_v(g0 + (r + 1))
                                    keep_x(g0 + r, r, b)
                                act.wait_ge(pg_used, 4 + LOADS[kind, b] + BG)
                                if b > 0:
                                    act.wait_ge(taps_turned, b)
                                nc.scalar.activation(taps_t[:, :], kp[:, 0:P], ACT.Copy).then_inc(taps_copied, 1)
                            else:
                                def spread(g, local):
                                    act.wait_ge(y_ready, g.n + 3)
                                    hold(act, b_passed["act"])
                                    for q in range(Q):
                                        rows = slice(N * q, N * q + N)
                                        last = nc.scalar.activation(
                                            carry[rows, g.slot(2), :, 1:CH, q],
                                            states[rows, b % XR, 0:CH - 1, :, ds(local, 1)].rearrange("p c m a -> p m (c a)"),
                                            ACT.Copy)
                                    last.then_inc(carry_ready, 1)

                                act.wait_ge(cleared, 1)
                                act.wait_ge(scaled, 2 + 2 * (CH // SC) * (b + 1))
                                g0 = At(None, b * BG, 4)
                                spread(g0, 0)
                                spread(g0 + 1, 1)

                                def keep_y(g):
                                    act.wait_ge(y_ready, g.n + 5)
                                    hold(act, b_passed["act"])
                                    nc.scalar.activation(u_of(g), yp[:, g.slot(2), 0:XN].rearrange("p (c q) -> p c q", q=Q),
                                                         ACT.Copy).then_inc(y_kept, 1)

                                with act.Fori(0, BG // 4 - 1) as i:
                                    for r in range(4):
                                        spread(group(i, r + 2, b), i * 4 + (r + 2))
                                        keep_y(group(i, r, b))
                                for r in range(BG - 4, BG):
                                    if r + 2 < BG:
                                        spread(g0 + (r + 2), r + 2)
                                    keep_y(g0 + r)
                                act.wait_ge(y_kept, 2 + BG * (b + 1))
                                act.dma_start(y_d[:, :, b * P:(b + 1) * P].rearrange("c p d -> p c d"),
                                              u[:, :, b * P:(b + 1) * P]).then_inc(y_saved, 16)
                        act.wait_ge(y_saved, 16 * NBATCH)

                    @block.vector
                    def _(dve):
                        nc.vector.memset(kpad[:, :], 0.0).then_inc(kpad_cleared, 1)
                        dve.wait_ge(kpad_cleared, 1)
                        for kind, b in ORDER:
                            if kind != "in":
                                continue
                            dve.wait_ge(taps_turned, b + 1)
                            if b > 0:
                                dve.wait_ge(kpad_saved, 16 * b)
                            nc.vector.tensor_copy(kpad[:, P - 1:2 * P - 1], kt[:, 0:P]).then_inc(kpad_step, 1)
                            dve.wait_ge(kpad_step, 2 * b + 1)
                            nc.vector.tensor_tensor(kpad[:, P - 1:P], kpad[:, P - 1:P], skip[:, b:b + 1],
                                                    ALU.add).then_inc(kpad_step, 1)
                            dve.wait_ge(x_kept, 2 + BG * (b + 1))
                            S = states[:, b % XR]
                            same, cross = (t[:, :, b * BG:(b + 1) * BG] for t in (scan_same, scan_cross))
                            done = b * (CH - 1)
                            def state(n):
                                return S[:, ds(n, 1)].rearrange("p a m g -> p (a m) g")

                            def step(c):
                                n = c.n
                                for m in range(2):
                                    nc.vector.tensor_tensor(scan_b[:, m], cross[:, m], state(n)[:, 1 - m],
                                                            ALU.mult).then_inc(scan_prod, 1)
                                nc.vector.tensor_tensor(scan_a[:, :, :], same, state(n), ALU.mult).then_inc(scan_prod, 1)
                                dve.wait_ge(scan_prod, (n + done) * 3 + 3)
                                nc.vector.tensor_tensor(scan_a[:, :, :], scan_a[:, :, :], scan_b[:, :, :],
                                                        ALU.add).then_inc(scan_sum, 1)
                                dve.wait_ge(scan_sum, (n + done) * 2 + 1)
                                nc.vector.tensor_tensor(state(n + 1), state(n + 1), scan_a[:, :, :],
                                                        ALU.add).then_inc(scan_sum, 1)
                                dve.wait_ge(scan_sum, (n + done) * 2 + 2)

                            run_steps(dve, 0, CH - 1, 6, 1, 2, step)

                    @block.gpsimd
                    def _(pool):
                        nc.gpsimd.memset(carry[:, :, :, :, :], 0.0).then_inc(cleared, 1)
                        pool.sem_inc(scaled, 2)

                        def save_taps(b):
                            pool.wait_ge(kpad_step, 2 * (b + 1))
                            pool.dma_start(kernel_d[b * P:(b + 1) * P, :], kpad[:, :]).then_inc(kpad_saved, 16)

                        save_taps(0)
                        for kind, b in ORDER:
                            if kind == "out":
                                if b + 1 < NBATCH:
                                    save_taps(b + 1)
                                pool.wait_ge(scan_sum, 2 * (CH - 1) * (b + 1))
                                same, cross = (t[:, :, b * BG:(b + 1) * BG].unsqueeze(1).to_broadcast([P, SC, 2, BG])
                                               for t in (scale_same, scale_cross))
                                with pool.Fori(0, CH // SC) as i:
                                    n = i + b * (CH // SC)
                                    S = states[:, b % XR, ds(i * SC, SC)]
                                    pool.wait_ge(scaled, n * 2 + 2)
                                    hold(pool, b_passed["pool"])
                                    nc.gpsimd.tensor_tensor(scale_a[:, :, :, :], S, same, ALU.mult).then_inc(scale_prod, 1)
                                    nc.gpsimd.tensor_tensor(scale_b[:, :, :, :], S, cross, ALU.mult).then_inc(scale_prod, 1)
                                    pool.wait_ge(scale_prod, n * 2 + 2)
                                    hold(pool, b_passed["pool"])
                                    nc.gpsimd.tensor_tensor(S[:, :, 0], scale_a[:, :, 0], scale_b[:, :, 1],
                                                            ALU.subtract).then_inc(scaled, 1)
                                    nc.gpsimd.tensor_tensor(S[:, :, 1], scale_b[:, :, 0], scale_a[:, :, 1],
                                                            ALU.subtract).then_inc(scaled, 1)

        with ExitStack() as ctx:
            sb, ps, _ = tensors(ctx)
            semaphores = []

            def sem(name):
                semaphores.append(nc.alloc_semaphore(name=name))
                return semaphores[-1]

            gw_hi, gw_lo = sb("gw_hi", [P, KD, 2 * D], F32R), sb("gw_lo", [P, KD, 2 * D], F32R)
            ow_hi, ow_lo = sb("ow_hi", [P, KD, D], F32R), sb("ow_lo", [P, KD, D], F32R)
            glu_bias, half_bias = sb("glu_bias", [P, 2 * KD]), sb("half_bias", [P, KD])
            out_bias = sb("out_bias", [P, D])
            y_t, xc = sb("y_t", [P, 2, TB, D]), sb("xc", [P, 2, TB, D])
            g_f = sb("g_f", [P, 2, BT])
            g_hi, g_lo = sb("g_hi", [P, 2, KD, BT], F32R), sb("g_lo", [P, 2, KD, BT], F32R)
            th, za_b, v_f = sb("th", [P, 2, BT]), sb("za_b", [P, 2, BT]), sb("v_f", [P, 2, BT])
            v_hi, v_lo = sb("v_hi", [P, 2, KD, BT], F32R), sb("v_lo", [P, 2, KD, BT], F32R)
            xn_c, xnb, r_t, rn = (sb(n, [P, 2, D]) for n in ("xn_c", "xnb", "r_t", "rn"))
            x1_t, x2_t = sb("x1_t", [P, 2, TB, D]), sb("x2_t", [P, 2, D])
            x2T = sb("x2T", [P, 2, KD, P])
            stc, mvc = sb("stc", [P, 3, 4, 6]), sb("mvc", [P, 3, 4, 2])
            varc, rstdc = sb("varc", [P, 3, 4, 1]), sb("rstdc", [P, 3, 4, 1])
            typ, zp = ps("typ", [P, 512]), ps("zp", [P, 2, 2, 512])
            op, txp = ps("op", [P, 2, 512]), ps("txp", [P, 512])

            HALVES = (slice(0, KD // 2), slice(KD // 2, KD))
            glu_w_loaded = [sem(f"glu_w_loaded{i}") for i in range(2)]
            out_w_loaded, biases_loaded, glu_w_hi_ready, glu_w_step, out_w_split = (
                sem(n) for n in ("out_w_loaded", "biases_loaded", "glu_w_hi_ready", "glu_w_step", "out_w_split"))
            y_loaded = [sem(f"y_loaded{i}") for i in range(2)]
            xc_loaded = [sem(f"xc_loaded{i}") for i in range(2)]
            (ty_ready, g_ready, g_hi_ready, g_lo_ready, z_ready, th_ready, za_ready, v_ready_c, v_hi_ready, v_lo_ready,
             o_ready, r_ready, rn_ready, x1_ready, x2_ready, tx_ready, x2T_ready, xn_done, xnb_ready) = (
                sem(n) for n in ("ty_ready", "g_ready", "g_hi_ready", "g_lo_ready", "z_ready", "th_ready", "za_ready",
                                 "v_ready_c", "v_hi_ready", "v_lo_ready", "o_ready", "r_ready", "rn_ready", "x1_ready",
                                 "x2_ready", "tx_ready", "x2T_ready", "xn_done", "xnb_ready"))
            stat, aggr, var_c, root = ([sem(f"{n}_{w}") for w in ("x", "r", "x1")] for n in ("stat", "aggr", "var", "root"))
            x1_saved = [sem(f"x1_saved{i}") for i in range(2)]
            x2T_saved = [sem(f"x2T_saved{i}") for i in range(2)]
            dve_held = sem("dve_held")
            gw_stage = x1_t[:, :, :, :].rearrange("p a k t -> p (a k t)").rearrange("p (k n) -> p k n", k=KD)
            ow_stage = xc[:, 1]

            def of_block(a):
                return a.slot(8) // 4, a.slot(8) % 4

            def quarters(eng, step, first=-5, last=8):
                run_steps(eng, first, CH + last, 8, 16, 14, step)

            with nc.Block() as block:
                @block.sync
                def _(sp):
                    for i, k in enumerate(HALVES):
                        sp.dma_start(gw_stage[:, k], glu_WT.rearrange("(k p) n -> p k n", p=P)[:, k]).then_inc(glu_w_loaded[i], 16)
                    sp.dma_start(glu_bias[:, :], glu_b).then_inc(biases_loaded, 16)
                    sp.dma_start(out_bias[:, :], out_b.partition_broadcast(P)).then_inc(biases_loaded, 16)
                    x_b = x.rearrange("(b j p) d -> b p j d", p=P, j=TB)
                    y_b = y_d.rearrange("(b j) p d -> b p j d", j=TB)
                    x1_b = x1_d.rearrange("(b j) p d -> b p j d", j=TB)
                    def one(ap, n):
                        return ap[ds(n, 1)].rearrange("a p j d -> (a p) j d")

                    def step(s):
                        b = s + 2
                        if b.within(NBLK):
                            if b.reuses(2):
                                sp.wait_ge(ty_ready, (b.n - 1) * 4)
                            sp.dma_start(y_t[:, b.slot(2)], one(y_b, b.n)).then_inc(y_loaded[b.slot(2)], 16)
                            if b.loop is None and b.off == 0:
                                sp.dma_start(ow_stage, out_WT.rearrange("(k p) n -> p k n", p=P)).then_inc(out_w_loaded, 16)
                        if s.within(NBLK):
                            if s.reuses(2):
                                sp.wait_ge(x1_ready, (s.n - 1) * 4)
                            if s.loop is None and s.off == 1:
                                sp.wait_ge(out_w_split, 2)
                            sp.dma_start(xc[:, s.slot(2)], one(x_b, s.n)).then_inc(xc_loaded[s.slot(2)], 16)
                        b = s + (-3)
                        if b.within(NBLK):
                            sp.wait_ge(x1_ready, b.n * 4 + 4)
                            sp.dma_start(one(x1_b, b.n), x1_t[:, b.slot(2)]).then_inc(x1_saved[b.slot(2)], 16)

                    run_steps(sp, -2, NBLK + 3, 2, 6, 5, step)
                    for i in range(2):
                        sp.wait_ge(x1_saved[i], 16 * NBLK // 2)
                        sp.wait_ge(x2T_saved[i], 16 * CH // 2)

                @block.tensor
                def _(pe):
                    def step(m):
                        if m.loop is None and m.off == 0:
                            pe.wait_ge(glu_w_step, 4)
                        if m.loop is None and m.off == 4:
                            pe.wait_ge(out_w_split, 2)
                        if m.within(CH):
                            bs, o = of_block(m)
                            pe.wait_ge(g_lo_ready, m.n + 1 + (3 - o))
                            if m.reuses(2):
                                pe.wait_ge(th_ready, m.n - 1)
                                pe.wait_ge(za_ready, m.n - 1)
                            for half in range(2):
                                cols = slice(half * D + o * P, half * D + (o + 1) * P)
                                last = three_pass(zp[:, m.slot(2), half], KD,
                                                  lambda k: (gw_hi[:, k, cols], gw_lo[:, k, cols]),
                                                  lambda k: (g_hi[:, bs, k], g_lo[:, bs, k]))
                            last.then_inc(z_ready, 1)
                        a = m + 5
                        if a.within(CH):
                            bs, k = of_block(a)
                            if k == 0:
                                pe.wait_ge(y_loaded[bs], 16 * a.turn(8) + 16)
                            if a.reuses(1):
                                pe.wait_ge(g_ready, a.n)
                            for j in range(TB):
                                last = nc.tensor.transpose(typ[:, j * P:(j + 1) * P],
                                                           y_t[:, bs, j, k * P:(k + 1) * P], ident[:, :])
                            last.then_inc(ty_ready, 1)
                        a = m + (-4)
                        if a.within(CH):
                            bs, j = of_block(a)
                            pe.wait_ge(v_lo_ready, a.n + 1 + (3 - j))
                            if a.reuses(2):
                                pe.wait_ge(r_ready, a.n - 1)
                            toks = slice(j * P, (j + 1) * P)
                            three_pass(op[:, a.slot(2)], KD,
                                       lambda k: (v_hi[:, bs, k, toks], v_lo[:, bs, k, toks]),
                                       lambda k: (ow_hi[:, k], ow_lo[:, k])).then_inc(o_ready, 1)
                        a = m + (-7)
                        if a.within(CH):
                            pe.wait_ge(x2_ready, a.n + 1)
                            if a.reuses(1):
                                pe.wait_ge(x2T_ready, a.n)
                            for k in range(KD):
                                last = nc.tensor.transpose(txp[:, k * P:(k + 1) * P],
                                                           x2_t[:, a.slot(2), k * P:(k + 1) * P], ident[:, :])
                            last.then_inc(tx_ready, 1)

                    quarters(pe, step)

                @block.scalar
                def _(act):
                    for i, k in enumerate(HALVES):
                        act.wait_ge(glu_w_loaded[i], 16)
                        nc.scalar.activation(gw_hi[:, k], gw_stage[:, k], ACT.Copy).then_inc(glu_w_hi_ready, 1)
                    def step(m):
                        if m.loop is None and m.off == 0:
                            act.wait_ge(out_w_loaded, 16)
                            nc.scalar.activation(ow_hi[:, :, :], ow_stage, ACT.Copy).then_inc(out_w_split, 1)
                            act.wait_ge(glu_w_step, 4)
                        if m.within(CH):
                            o, r = m.slot(4), m.slot(2)
                            act.wait_ge(z_ready, m.n + 1)
                            if m.reuses(2):
                                act.wait_ge(v_ready_c, m.n - 1)
                            nc.scalar.activation(th[:, r], zp[:, r, 1], ACT.Tanh, bias=half_bias[:, o:o + 1],
                                                 scale=0.5).then_inc(th_ready, 1)
                            nc.scalar.activation(za_b[:, r], zp[:, r, 0], ACT.Identity, bias=glu_bias[:, o:o + 1],
                                                 scale=1.0).then_inc(za_ready, 1)
                        a = m + 5
                        if a.within(CH):
                            bs, k = of_block(a)
                            act.wait_ge(ty_ready, a.n + 1)
                            if a.reuses(2):
                                act.wait_ge(g_lo_ready, a.n - 1)
                            nc.scalar.activation(g_f[:, a.slot(2)], typ[:, :], ACT.Gelu).then_inc(g_ready, 1)
                            if a.reuses(8):
                                act.wait_ge(z_ready, a.n - 4 - k)
                            act.wait_ge(g_ready, a.n + 1)
                            nc.scalar.activation(g_hi[:, bs, k], g_f[:, a.slot(2)], ACT.Copy).then_inc(g_hi_ready, 1)
                        if m.within(CH):
                            bs, o = of_block(m)
                            act.wait_ge(v_ready_c, m.n + 1)
                            if m.reuses(8):
                                act.wait_ge(o_ready, m.n - 4 - o)
                            nc.scalar.activation(v_hi[:, bs, o], v_f[:, m.slot(2)], ACT.Copy).then_inc(v_hi_ready, 1)
                        a = m + (-7)
                        if a.within(CH):
                            act.wait_ge(tx_ready, a.n + 1)
                            if a.reuses(2):
                                act.wait_ge(x2T_saved[a.slot(2)], 16 * a.turn(2))
                            nc.scalar.activation(x2T[:, a.slot(2)], txp[:, :].rearrange("p (k t) -> p k t", k=KD),
                                                 ACT.Copy).then_inc(x2T_ready, 1)
                        a = m + (-8)
                        if a.within(CH):
                            act.wait_ge(x2T_ready, a.n + 1)
                            act.dma_start(x2T_d.rearrange("(k p) t -> p k t", p=P)[:, :, ds(a.n * P, P)],
                                          x2T[:, a.slot(2)]).then_inc(x2T_saved[a.slot(2)], 16)

                    quarters(act, step)

                @block.vector
                def _(dve):
                    for i, k in enumerate(HALVES):
                        dve.wait_ge(glu_w_hi_ready, i + 1)
                        nc.vector.tensor_tensor(gw_lo[:, k], gw_stage[:, k], gw_hi[:, k].bitcast(F32),
                                                ALU.subtract).then_inc(glu_w_step, 1)
                    dve.wait_ge(biases_loaded, 32)
                    nc.vector.tensor_scalar(half_bias[:, :], glu_bias[:, KD:2 * KD], 0.5, None, ALU.mult).then_inc(glu_w_step, 1)
                    nc.vector.memset(stc[:, :, :, :], 0.0).then_inc(glu_w_step, 1)
                    dve.wait_ge(glu_w_step, 4)

                    def variance(which, a, src):
                        i = a.slot(4)
                        nc.vector.bn_stats(stc[:, which, i], src).then_inc(stat[which], 1)
                        dve.wait_ge(stat[which], a.n + 1)
                        hold(dve, dve_held)
                        nc.vector.bn_aggr(mvc[:, which, i], stc[:, which, i]).then_inc(aggr[which], 1)
                        dve.wait_ge(aggr[which], a.n + 1)
                        nc.vector.tensor_scalar(varc[:, which, i], mvc[:, which, i, 1:2], EPS, None,
                                                ALU.add).then_inc(var_c[which], 1)

                    def normalise(which, a, dst, src, done):
                        i = a.slot(4)
                        dve.wait_ge(root[which], a.n + 1)
                        nc.vector.tensor_scalar(dst, src, mvc[:, which, i, 0:1], rstdc[:, which, i], ALU.subtract,
                                                ALU.mult).then_inc(done, 1)

                    def step(m):
                        if m.loop is None and m.off == 1:
                            dve.wait_ge(out_w_split, 1)
                            nc.vector.tensor_tensor(ow_lo[:, :, :], ow_stage, ow_hi[:, :, :].bitcast(F32),
                                                    ALU.subtract).then_inc(out_w_split, 1)
                        a = m + (-6)
                        if a.within(CH):
                            bs, j = of_block(a)
                            if a.reuses(2):
                                dve.wait_ge(tx_ready, a.n - 1)
                            normalise(2, a, x2_t[:, a.slot(2)], x1_t[:, bs, j], x2_ready)
                        a = m + (-5)
                        if a.within(CH):
                            if a.reuses(2):
                                dve.wait_ge(x1_ready, a.n - 1)
                            normalise(1, a, rn[:, a.slot(2)], r_t[:, a.slot(2)], rn_ready)
                        a = m + (-3)
                        if a.within(CH):
                            bs, j = of_block(a)
                            if j == 0:
                                dve.wait_ge(xc_loaded[bs], 16 * a.turn(8) + 16)
                            variance(0, a, xc[:, bs, j])
                        a = m + (-4)
                        if a.within(CH):
                            bs, j = of_block(a)
                            if a.reuses(2):
                                dve.wait_ge(xnb_ready, a.n - 1)
                            normalise(0, a, xn_c[:, a.slot(2)], xc[:, bs, j], xn_done)
                        if m.within(CH):
                            r = m.slot(2)
                            dve.wait_ge(th_ready, m.n + 1)
                            dve.wait_ge(za_ready, m.n + 1)
                            if m.reuses(2):
                                dve.wait_ge(v_lo_ready, m.n - 1)
                            nc.vector.scalar_tensor_tensor(v_f[:, r], th[:, r], 1.0, za_b[:, r], ALU.add,
                                                           ALU.mult).then_inc(v_ready_c, 1)
                        a = m + 5
                        if a.within(CH):
                            bs, k = of_block(a)
                            dve.wait_ge(g_hi_ready, a.n + 1)
                            nc.vector.tensor_tensor(g_lo[:, bs, k], g_f[:, a.slot(2)], g_hi[:, bs, k].bitcast(F32),
                                                    ALU.subtract).then_inc(g_lo_ready, 1)
                        if m.within(CH):
                            bs, o = of_block(m)
                            dve.wait_ge(v_hi_ready, m.n + 1)
                            nc.vector.tensor_tensor(v_lo[:, bs, o], v_f[:, m.slot(2)], v_hi[:, bs, o].bitcast(F32),
                                                    ALU.subtract).then_inc(v_lo_ready, 1)
                        a = m + (-4)
                        if a.within(CH):
                            dve.wait_ge(o_ready, a.n + 1)
                            dve.wait_ge(xnb_ready, a.n + 1)
                            nc.vector.scalar_tensor_tensor(r_t[:, a.slot(2)], op[:, a.slot(2)], 0.5, xnb[:, a.slot(2)],
                                                           ALU.mult, ALU.add).then_inc(r_ready, 1)
                            dve.wait_ge(r_ready, a.n + 1)
                            variance(1, a, r_t[:, a.slot(2)])
                        a = m + (-5)
                        if a.within(CH):
                            bs, j = of_block(a)
                            dve.wait_ge(x1_ready, a.n + 1)
                            variance(2, a, x1_t[:, bs, j])

                    quarters(dve, step)

                @block.gpsimd
                def _(pool):
                    def root_of(which, a):
                        i = a.slot(4)
                        pool.wait_ge(var_c[which], a.n + 1)
                        nc.gpsimd.tensor_tensor(rstdc[:, which, i], varc[:, which, i], minus_half[:, :],
                                                ALU.pow).then_inc(root[which], 1)

                    def step(m):
                        a = m + (-5)
                        if a.within(CH):
                            bs, j = of_block(a)
                            pool.wait_ge(rn_ready, a.n + 1)
                            if a.reuses(8) and j == 0:
                                pool.wait_ge(x1_saved[bs], 16 * a.turn(8))
                            nc.gpsimd.tensor_tensor(x1_t[:, bs, j], rn[:, a.slot(2)], xc[:, bs, j],
                                                    ALU.add).then_inc(x1_ready, 1)
                        a = m + (-3)
                        if a.within(CH):
                            root_of(0, a)
                        a = m + (-4)
                        if a.within(CH):
                            pool.wait_ge(xn_done, a.n + 1)
                            if a.reuses(2):
                                pool.wait_ge(r_ready, a.n - 1)
                            nc.gpsimd.tensor_tensor(xnb[:, a.slot(2)], xn_c[:, a.slot(2)], out_bias[:, :],
                                                    ALU.add).then_inc(xnb_ready, 1)
                            root_of(1, a)
                        a = m + (-5)
                        if a.within(CH):
                            root_of(2, a)

                    pool.wait_ge(biases_loaded, 32)
                    quarters(pool, step)

            nc.clear_and_free_semaphores(semaphores)
            nc.all_engine_barrier()

        with ExitStack() as ffn:
            sb, _, _ = tensors(ffn)
            m1_hi, m1_lo = sb("m1_hi", [P, KD, F], F32R), sb("m1_lo", [P, KD, F], F32R)
            m2_hi, m2_lo = sb("m2_hi", [P, FT, D], F32R), sb("m2_lo", [P, FT, D], F32R)
            mb1, mb2 = sb("mb1", [P, FT]), sb("mb2", [P, D])
            gate_sum = sb("gate_sum", [P, KD, NBLK])
            gate = sb("gate", [P, E])

            PC = D
            PARTS = F // PC
            FT1 = FT // PARTS
            assert FT1 == KD

            def piece_of(weight, wide, part, n):
                if weight == 0:
                    return wide.rearrange("(k p) (c f) -> c k p f", p=P, f=PC)[part, ds(n, 1)].rearrange("a p f -> (a p) f")
                return wide.rearrange("(t p) h -> t p h", p=P)[ds(n + part * FT1, 1)].rearrange("a p h -> (a p) h")

            def place(weight, half, part, n):
                if weight == 0:
                    return half[:, ds(n, 1), part * PC:(part + 1) * PC].rearrange("p a f -> p (a f)")
                return half[:, ds(n + part * FT1, 1), :].rearrange("p a f -> p (a f)")

            with ExitStack() as ctx:
                sb, ps, sem = tensors(ctx)
                gs = sb("gs", [P, KD, D])
                gt_hi, gt_lo = sb("gt_hi", [P, KD, D], F32R), sb("gt_lo", [P, KD, D], F32R)
                gate_bias = sb("gate_bias", [P, KD])
                x2_in = sb("x2_in", [P, 2, KD, BT])
                xg_hi, xg_lo = sb("xg_hi", [P, 2, KD, BT], F32R), sb("xg_lo", [P, 2, KD, BT], F32R)
                relu = sb("relu", [P, BT])
                hp = ps("hp", [P, 4, 512])
                gw_loaded, gsplit, gb_loaded = sem("gw_loaded"), sem("gsplit"), sem("gb_loaded")
                xg_loaded = [sem(f"xg_loaded{i}") for i in range(2)]
                xg_hi_ready, xg_lo_ready, h_ready, h_summed = (
                    sem("xg_hi_ready"), sem("xg_lo_ready"), sem("h_ready"), sem("h_summed"))
                h_passed = sem("h_passed")

                with nc.Block() as block:
                    @block.sync
                    def _(sp):
                        sp.dma_start(gs[:, :, :], gate_w1T.rearrange("(k p) o -> p k o", p=P)).then_inc(gw_loaded, 16)
                        sp.dma_start(gate_bias[:, :], gate_b1).then_inc(gb_loaded, 16)
                        x2T_b = x2T_d.rearrange("(k p) t -> p k t", p=P)

                        def step(s):
                            if s.reuses(2):
                                sp.wait_ge(xg_lo_ready, s.n - 1)
                            sp.dma_start(x2_in[:, s.slot(2)], x2T_b[:, :, ds(s.n * BT, BT)]
                                         ).then_inc(xg_loaded[s.slot(2)], 16)

                        run_steps(sp, 0, NBLK, 2, 2, 2, step)

                    @block.scalar
                    def _(act):
                        act.wait_ge(gw_loaded, 16)
                        nc.scalar.activation(gt_hi[:, :, :], gs[:, :, :], ACT.Copy).then_inc(gsplit, 1)
                        act.wait_ge(gb_loaded, 16)

                        def step(s):
                            a = s + 1
                            if a.within(NBLK):
                                act.wait_ge(xg_loaded[a.slot(2)], 16 * a.turn(2) + 16)
                                if a.reuses(2):
                                    act.wait_ge(h_ready, 4 * (a.n - 1))
                                nc.scalar.activation(xg_hi[:, a.slot(2)], x2_in[:, a.slot(2)],
                                                     ACT.Copy).then_inc(xg_hi_ready, 1)
                            if s.within(NBLK):
                                for o in range(KD):
                                    act.wait_ge(h_ready, 4 * s.n + o + 1)
                                    if o or s.reuses(1):
                                        act.wait_ge(h_summed, 4 * s.n + o)
                                    hold(act, h_passed)
                                    nc.scalar.activation(relu[:, :], hp[:, o], ACT.Relu, bias=gate_bias[:, o:o + 1],
                                                         scale=1.0, accum_out=gate_sum[:, o, ds(s.n, 1)]
                                                         ).then_inc(h_summed, 1)

                        run_steps(act, -1, NBLK, 2, 2, 2, step)

                    @block.vector
                    def _(dve):
                        dve.wait_ge(gsplit, 1)
                        nc.vector.tensor_tensor(gt_lo[:, :, :], gs[:, :, :], gt_hi[:, :, :].bitcast(F32),
                                                ALU.subtract).then_inc(gsplit, 1)

                        def step(s):
                            dve.wait_ge(xg_hi_ready, s.n + 1)
                            i = s.slot(2)
                            nc.vector.tensor_tensor(xg_lo[:, i], x2_in[:, i], xg_hi[:, i].bitcast(F32),
                                                    ALU.subtract).then_inc(xg_lo_ready, 1)

                        run_steps(dve, 0, NBLK, 2, 2, 2, step)

                    @block.tensor
                    def _(pe):
                        pe.wait_ge(gsplit, 2)

                        def step(s):
                            pe.wait_ge(xg_lo_ready, s.n + 1)
                            for o in range(KD):
                                if s.reuses(1):
                                    pe.wait_ge(h_summed, 4 * (s.n - 1) + o + 1)
                                cols = slice(o * P, (o + 1) * P)
                                three_pass(hp[:, o], KD, lambda k: (gt_hi[:, k, cols], gt_lo[:, k, cols]),
                                           lambda k: (xg_hi[:, s.slot(2), k], xg_lo[:, s.slot(2), k])
                                           ).then_inc(h_ready, 1)

                        run_steps(pe, 0, NBLK, 2, 2, 2, step)

            with ExitStack() as ctx:
                sb, ps, sem = tensors(ctx)
                PIECES = KD
                expert, base_w, mixed = sb("expert", [P, 2, E, PC]), sb("base_w", [P, 2, PC]), sb("mixed", [P, 2, PC])
                g_mean, g_wide = sb("g_mean", [P, KD]), sb("g_wide", [P, KD, P])
                gw2, gb2 = sb("gw2", [P, KD, E]), sb("gb2", [P, E])
                tb1, tb2 = sb("tb1", [P, E, FT]), sb("tb2", [E, D])
                gate_T = sb("gate_T", [E, P])
                gp, gtp, tbp = ps("gp", [P, 512]), ps("gtp", [P, 512]), ps("tbp", [P, 512])
                gate_loaded, bias_loaded, g_step, g_prod, g_ready, bias_step = (
                    sem("gate_loaded"), sem("bias_loaded"), sem("g_step"), sem("g_prod"), sem("gate_ready"), sem("bias_step"))
                expert_loaded = [[sem(f"expert_loaded{i}_{e}") for e in range(E)] for i in range(2)]
                base_loaded = [sem(f"base_loaded{i}") for i in range(2)]
                mix_step, mix_hi, mix_lo = sem("mix_step"), sem("mix_hi"), sem("mix_lo")
                mix_passed, gate_T_ready = sem("mix_passed"), sem("gate_T_ready")

                def pieces(eng, weight, step):
                    with eng.Fori(0, PIECES // 2) as i:
                        for r in range(2):
                            step(At(i + weight * (PIECES // 2), r, 2), i * 2 + r)

                def added(s, e):
                    return (s.n - s.slot(2) + 2) * E + 2 * e + s.slot(2) + 1

                with nc.Block() as block:
                    @block.sync
                    def _(sp):
                        for weight, (W, TW) in enumerate(((W1T, TW1T), (W2T, TW2T))):
                            def step(s, n):
                                sp.wait_ge(mix_step, added(s, 0) - 2 * E)
                                sp.dma_start(base_w[:, s.slot(2)], piece_of(weight, W, 0, n)).then_inc(base_loaded[s.slot(2)], 16)
                                for e in range(E):
                                    sp.wait_ge(mix_step, added(s, e) - 2 * E)
                                    sp.dma_start(expert[:, s.slot(2), e], piece_of(weight, TW[e], 0, n)
                                                 ).then_inc(expert_loaded[s.slot(2)][e], 16)
                            pieces(sp, weight, step)

                    @block.scalar
                    def _(act):
                        act.dma_start(gw2[:, :, :], gate_w2T.rearrange("(k p) e -> p k e", p=P)).then_inc(gate_loaded, 16)
                        act.dma_start(gb2[:, :], gate_b2.partition_broadcast(P)).then_inc(gate_loaded, 16)
                        act.dma_start(mb1[:, :], b1).then_inc(bias_loaded, 16)
                        act.dma_start(mb2[:, :], b2.partition_broadcast(P)).then_inc(bias_loaded, 16)
                        act.dma_start(tb1[:, :, :], Tb1T).then_inc(bias_loaded, 16)
                        act.dma_start(tb2[:, :], Tb2).then_inc(bias_loaded, 16)
                        for weight, hi in enumerate((m1_hi, m2_hi)):
                            def step(s, n):
                                act.wait_ge(mix_step, added(s, E - 1))
                                hold(act, mix_passed)
                                nc.scalar.activation(place(weight, hi, 0, n), mixed[:, s.slot(2)], ACT.Copy).then_inc(mix_hi, 1)
                            pieces(act, weight, step)

                    @block.tensor
                    def _(pe):
                        pe.wait_ge(g_step, 3)
                        for k in range(KD):
                            last = nc.tensor.matmul(gp[:, 0:E], g_wide[:, k], gw2[:, k], start=(k == 0), stop=(k == KD - 1))
                        last.then_inc(g_prod, 1)
                        pe.wait_ge(g_ready, 1)
                        nc.tensor.transpose(gtp[0:E, 0:P], gate[:, :], ident[:, :]).then_inc(g_prod, 1)
                        pe.wait_ge(gate_T_ready, 1)
                        pe.wait_ge(bias_loaded, 16 * 4)
                        nc.tensor.matmul(tbp[:, 0:D], gate_T[:, :], tb2[:, :], start=True, stop=True).then_inc(g_prod, 1)

                    @block.vector
                    def _(dve):
                        dve.sem_inc(mix_step, 2 * E)
                        nc.vector.reduce_sum(g_mean[:, :], gate_sum[:, :, :], AX_X).then_inc(g_step, 1)
                        dve.wait_ge(g_step, 1)
                        nc.vector.tensor_scalar(g_mean[:, :], g_mean[:, :], 1.0 / L, None, ALU.mult).then_inc(g_step, 1)
                        dve.wait_ge(g_step, 2)
                        dve.wait_ge(gate_loaded, 16 * 2)
                        nc.vector.tensor_copy(g_wide[:, :, :], g_mean[:, :].unsqueeze(2).to_broadcast([P, KD, P])
                                              ).then_inc(g_step, 1)
                        dve.wait_ge(g_prod, 1)
                        nc.vector.tensor_tensor(gate[:, :], gp[:, 0:E], gb2[:, :], ALU.add).then_inc(g_ready, 1)
                        dve.wait_ge(g_prod, 2)
                        nc.vector.tensor_copy(gate_T[:, :], gtp[0:E, 0:P]).then_inc(gate_T_ready, 1)
                        for weight, (hi, lo) in enumerate(((m1_hi, m1_lo), (m2_hi, m2_lo))):
                            with dve.Fori(0, PIECES // 2) as i:
                                pair = [At(i + weight * (PIECES // 2), r, 2) for r in range(2)]
                                for s in pair:
                                    dve.wait_ge(base_loaded[s.slot(2)], 16 * s.turn(2) + 16)
                                dve.wait_ge(mix_lo, pair[1].n + 1)
                                for e in range(E):
                                    for r, s in enumerate(pair):
                                        dve.wait_ge(expert_loaded[r][e], 16 * s.turn(2) + 16)
                                        if e:
                                            dve.wait_ge(mix_step, added(s, e - 1))
                                        nc.vector.scalar_tensor_tensor(mixed[:, r], expert[:, r, e], gate[:, e:e + 1],
                                                                       base_w[:, r] if e == 0 else mixed[:, r],
                                                                       ALU.mult, ALU.add).then_inc(mix_step, 1)
                                for r, s in enumerate(pair):
                                    n = i * 2 + r
                                    dve.wait_ge(mix_hi, s.n + 1)
                                    nc.vector.tensor_tensor(place(weight, lo, 0, n), mixed[:, r],
                                                            place(weight, hi, 0, n).bitcast(F32),
                                                            ALU.subtract).then_inc(mix_lo, 1)
                            if weight == 0:
                                dve.wait_ge(bias_loaded, 16 * 4)
                                for e in range(E):
                                    if e:
                                        dve.wait_ge(bias_step, e)
                                    nc.vector.scalar_tensor_tensor(mb1[:, :], tb1[:, e], gate[:, e:e + 1], mb1[:, :],
                                                                   ALU.mult, ALU.add).then_inc(bias_step, 1)
                                dve.wait_ge(g_prod, 3)
                                nc.vector.tensor_tensor(mb2[:, :], tbp[:, 0:D], mb2[:, :], ALU.add).then_inc(bias_step, 1)

                    @block.gpsimd
                    def _(pool):
                        pool.sem_inc(mix_lo, 2)

            with ExitStack() as ctx:
                sb, ps, sem = tensors(ctx)
                x2_f = sb("x2_p", [P, KD, BT])
                xf_hi, xf_lo = sb("xp_hi", [P, KD, BT], F32R), sb("xp_lo", [P, KD, BT], F32R)
                h_f = sb("h_p", [P, 2, BT])
                h_hi, h_lo = sb("hp_hi", [P, 4, BT], F32R), sb("hp_lo", [P, 4, BT], F32R)
                part_t = sb("part_t", [P, TB, D])
                RING = 6
                expert, base_w, mixed = sb("expert_r", [P, RING, PC]), sb("base_r", [P, 2, PC]), sb("mixed_r", [P, 2, PC])
                hp1, opp = ps("hp1", [P, 4, 512]), ps("opp", [P, TB, 512])
                x2p_loaded, part_saved = sem("x2p_loaded"), sem("part_saved")
                xf_hi_ready, xf_lo_ready, h1_ready, hf_ready, h_hi_ready, h_lo_ready, mm2_done, part_ready = (
                    sem(n) for n in ("xp_hi_ready", "xp_lo_ready", "h1_ready_p", "hp_ready", "hp_hi_ready", "hp_lo_ready",
                                     "mm2_done_p", "part_ready"))
                expert_in = [sem(f"expert_in{i}") for i in range(RING)]
                base_in = [sem(f"base_in{i}") for i in range(2)]
                added, hi_mixed, lo_mixed, mix_held = (sem(n) for n in ("added", "hi_mixed", "lo_mixed", "mix_held"))
                NM = NBLK * FT1
                LAG = 2
                OTHER = 2 * (PARTS - 1)
                SPAN = NM // KD
                ADDS = OTHER * E // SPAN
                assert ADDS * SPAN == OTHER * E and (ADDS * SPAN) % RING == 0

                def tiles(eng, step, first=-1):
                    run_steps(eng, first, NM + FT1, SPAN, FT1, 2 * FT1, step)

                def block_of(m):
                    return At(m.loop, m.off // FT1, SPAN // FT1), m.off % FT1

                def additions(m):
                    for i in range(ADDS):
                        a = At(m.loop, m.off * ADDS + i, SPAN * ADDS)
                        yield a, At(a.loop, a.off // E, OTHER), a.off % E

                def finished(m):
                    return [x for _, x, e in additions(m + -1) if e == E - 1] if m.loop is not None or m.off > 0 else []

                def where(x):
                    s = x.off % OTHER
                    return s // (PARTS - 1), s % (PARTS - 1) + 1, (
                        x.off // OTHER if x.loop is None else x.loop + x.off // OTHER)

                with nc.Block() as block:
                    @block.sync
                    def _(sp):
                        x2T_b = x2T_d.rearrange("(k p) t -> p k t", p=P)

                        def step(m):
                            b, f = block_of(m)
                            if m.loop is None and m.off == -1:
                                b, f = At(None, -1, SPAN // FT1), FT1 - 1
                            n = b + 1
                            if f == FT1 - 1 and n.within(NBLK):
                                if n.reuses(1):
                                    sp.wait_ge(xf_lo_ready, n.n * 2)
                                sp.dma_start(x2_f[:, :, :], x2T_b[:, :, ds(n.n * BT, BT)]).then_inc(x2p_loaded, 16)
                            if m.within(NM):
                                for a, x, e in additions(m):
                                    weight, part, number = where(x)
                                    W, TW = ((W1T, TW1T), (W2T, TW2T))[weight]
                                    sp.wait_ge(added, a.n + 1)
                                    if e == 0:
                                        sp.dma_start(base_w[:, x.slot(2)], piece_of(weight, W, part, number)
                                                     ).then_inc(base_in[x.slot(2)], 16)
                                    sp.dma_start(expert[:, a.slot(RING)], piece_of(weight, TW[e], part, number)
                                                 ).then_inc(expert_in[a.slot(RING)], 16)
                            if f == LAG and b.reuses(1) and (b + -1).within(NBLK):
                                sp.wait_ge(part_ready, b.n * TB)
                                sp.dma_start(part_d[ds((b + -1).n, 1)].rearrange("a p j d -> (a p) j d"), part_t[:, :, :]
                                             ).then_inc(part_saved, 16)

                        tiles(sp, step)
                        sp.wait_ge(part_saved, 16 * NBLK)

                    @block.tensor
                    def _(pe):
                        def inner(m):
                            if not m.within(NM):
                                return
                            b, f = block_of(m)
                            if f == 0:
                                pe.wait_ge(xf_lo_ready, b.n * 2 + 2)
                            if m.reuses(4):
                                pe.wait_ge(hf_ready, m.n - 3)
                            cols = slice(f * P, (f + 1) * P)
                            three_pass(hp1[:, m.slot(4)], KD, lambda k: (m1_hi[:, k, cols], m1_lo[:, k, cols]),
                                       lambda k: (xf_hi[:, k], xf_lo[:, k])).then_inc(h1_ready, 1)

                        def outer(m):
                            if not m.within(NM):
                                return
                            b, f = block_of(m)
                            pe.wait_ge(h_lo_ready, m.n + 1)
                            s4 = m.slot(4)
                            for j in range(TB):
                                if f == 0 and b.reuses(1):
                                    pe.wait_ge(part_ready, (b.n - 1) * TB + j + 1)
                                toks = slice(j * P, (j + 1) * P)
                                passes = ((h_hi, m2_hi), (h_hi, m2_lo), (h_lo, m2_hi))
                                for n, (l, r) in enumerate(passes):
                                    last = nc.tensor.matmul(opp[:, j], l[:, s4, toks], r[:, f],
                                                            start=(f == 0 and n == 0), stop=(f == FT1 - 1 and n == 2))
                            last.then_inc(mm2_done, 1)

                        def step(m):
                            if m.off % FT1 == 0:
                                outer(m + (-LAG))
                                inner(m)
                            else:
                                inner(m)
                                outer(m + (-LAG))

                        tiles(pe, step, first=0)

                    @block.scalar
                    def _(act):
                        def split(n):
                            act.wait_ge(x2p_loaded, 16 * n.n + 16)
                            if n.reuses(1):
                                act.wait_ge(h1_ready, n.n * FT1)
                            for k in (slice(0, KD // 2), slice(KD // 2, KD)):
                                nc.scalar.activation(xf_hi[:, k], x2_f[:, k], ACT.Copy).then_inc(xf_hi_ready, 1)

                        def step(m):
                            if m.loop is None and m.off == -1:
                                split(At(None, 0, SPAN // FT1))
                                return
                            b, f = block_of(m)
                            if m.within(NM):
                                if f == FT1 - 1 and (b + 1).within(NBLK):
                                    split(b + 1)
                                act.wait_ge(h1_ready, m.n + 1)
                                if m.reuses(2):
                                    act.wait_ge(h_lo_ready, m.n - 1)
                                nc.scalar.activation(h_f[:, m.slot(2)], hp1[:, m.slot(4)], ACT.Gelu_apprx_tanh,
                                                     bias=mb1[:, f:f + 1], scale=1.0).then_inc(hf_ready, 1)
                                act.wait_ge(hf_ready, m.n + 1)
                                if m.reuses(4):
                                    act.wait_ge(mm2_done, m.n - 3)
                                nc.scalar.activation(h_hi[:, m.slot(4)], h_f[:, m.slot(2)], ACT.Copy).then_inc(h_hi_ready, 1)
                            if f == LAG - 1 and b.reuses(1) and (b + -1).within(NBLK):
                                act.wait_ge(mm2_done, b.n * FT1)
                                if b.reuses(2):
                                    act.wait_ge(part_saved, 16 * (b.n - 1))
                                for j in range(TB):
                                    nc.scalar.activation(part_t[:, j], opp[:, j], ACT.Copy).then_inc(part_ready, 1)
                            if m.loop is None and m.off > NM:
                                return
                            for x in finished(m):
                                weight, part, number = where(x)
                                act.wait_ge(added, RING + E + x.n * E)
                                hold(act, mix_held)
                                nc.scalar.activation(place(weight, (m1_hi, m2_hi)[weight], part, number),
                                                     mixed[:, x.slot(2)], ACT.Copy).then_inc(hi_mixed, 1)

                        tiles(act, step)

                    @block.vector
                    def _(dve):
                        dve.sem_inc(added, RING)
                        dve.sem_inc(lo_mixed, 2)

                        def split(n):
                            for half, k in enumerate((slice(0, KD // 2), slice(KD // 2, KD))):
                                dve.wait_ge(xf_hi_ready, n.n * 2 + half + 1)
                                nc.vector.tensor_tensor(xf_lo[:, k], x2_f[:, k], xf_hi[:, k].bitcast(F32),
                                                        ALU.subtract).then_inc(xf_lo_ready, 1)

                        def step(m):
                            if m.loop is None and m.off == -1:
                                split(At(None, 0, SPAN // FT1))
                                return
                            b, f = block_of(m)
                            if m.within(NM):
                                if f == FT1 - 1 and (b + 1).within(NBLK):
                                    split(b + 1)
                                dve.wait_ge(h_hi_ready, m.n + 1)
                                if m.reuses(4):
                                    dve.wait_ge(mm2_done, m.n - 3)
                                nc.vector.tensor_tensor(h_lo[:, m.slot(4)], h_f[:, m.slot(2)],
                                                        h_hi[:, m.slot(4)].bitcast(F32),
                                                        ALU.subtract).then_inc(h_lo_ready, 1)
                            if m.within(NM):
                                for a, x, e in additions(m):
                                    r = x.slot(2)
                                    if e == 0:
                                        dve.wait_ge(base_in[r], 16 * x.turn(2) + 16)
                                        dve.wait_ge(lo_mixed, x.n + 1)
                                    else:
                                        dve.wait_ge(added, a.n + RING)
                                    dve.wait_ge(expert_in[a.slot(RING)], 16 * a.turn(RING) + 16)
                                    nc.vector.scalar_tensor_tensor(mixed[:, r], expert[:, a.slot(RING)], gate[:, e:e + 1],
                                                                   base_w[:, r] if e == 0 else mixed[:, r],
                                                                   ALU.mult, ALU.add).then_inc(added, 1)
                            if m.loop is None and m.off > NM:
                                return
                            for x in finished(m):
                                weight, part, number = where(x)
                                hi, lo = ((m1_hi, m1_lo), (m2_hi, m2_lo))[weight]
                                dve.wait_ge(hi_mixed, x.n + 1)
                                nc.vector.tensor_tensor(place(weight, lo, part, number), mixed[:, x.slot(2)],
                                                        place(weight, hi, part, number).bitcast(F32),
                                                        ALU.subtract).then_inc(lo_mixed, 1)

                        tiles(dve, step)

            with ExitStack() as ctx:
                sb, ps, sem = tensors(ctx)
                x2_f = sb("x2_f", [P, KD, BT])
                xf_hi, xf_lo = sb("xf_hi", [P, KD, BT], F32R), sb("xf_lo", [P, KD, BT], F32R)
                h_f = sb("h_f", [P, 2, BT])
                h_hi, h_lo = sb("h_hi", [P, 4, BT], F32R), sb("h_lo", [P, 4, BT], F32R)
                o_t, x1_f, fin = sb("o_t", [P, TB, D]), sb("x1_f", [P, TB, D]), sb("fin", [P, TB, D])
                stf, mvf = sb("stf", [P, TB, 6]), sb("mvf", [P, TB, 2])
                varf, rstdf = sb("varf", [P, TB, 1]), sb("rstdf", [P, TB, 1])
                hp2, opf = ps("hp2", [P, 4, 512]), ps("opf", [P, TB, 512])
                x2f_loaded, x1f_loaded, part_loaded, part_biased, fin_saved = (
                    sem("x2f_loaded"), sem("x1f_loaded"), sem("part_loaded"), sem("part_biased"), sem("fin_saved"))
                xf_hi_ready, xf_lo_ready, h1_ready, hf_ready, h_hi_ready, h_lo_ready, mm2_done = (
                    sem(n) for n in ("xf_hi_ready", "xf_lo_ready", "h1_ready", "hf_ready", "h_hi_ready", "h_lo_ready",
                                     "mm2_done"))
                ot_ready, statf, aggrf, var_f, root_f, norm_f, fin_ready, f_held = (
                    sem(n) for n in ("ot_ready", "statf", "aggrf", "var_f", "root_f", "norm_f", "fin_ready", "f_held"))
                T = FT - FT1
                NM = NBLK * T
                LAG = 2

                def tiles(eng, step):
                    run_steps(eng, -1, NM + LAG + TB + 1, T, T, T + LAG + TB + 1, step)

                def block_of(m):
                    return (m.off // T if m.loop is None else m.loop + m.off // T), m.off % T

                with nc.Block() as block:
                    @block.sync
                    def _(sp):
                        x2T_b = x2T_d.rearrange("(k p) t -> p k t", p=P)
                        x1_b = x1_d.rearrange("(b j) p d -> b p j d", j=TB)
                        out_b_ = out.rearrange("(b j p) d -> b p j d", j=TB, p=P)

                        def one(ap, n):
                            return ap[ds(n, 1)].rearrange("a p j d -> (a p) j d")

                        def step(s):
                            b = s + 1
                            if b.within(NBLK):
                                if b.reuses(1):
                                    sp.wait_ge(xf_lo_ready, b.n * 2)
                                sp.dma_start(x2_f[:, :, :], x2T_b[:, :, ds(b.n * BT, BT)]).then_inc(x2f_loaded, 16)
                            b = s + (-1)
                            if s.within(NBLK):
                                if s.reuses(1):
                                    sp.wait_ge(fin_ready, (s.n + 1) * TB)
                                sp.dma_start(x1_f[:, :, :], one(x1_b, s.n)).then_inc(x1f_loaded, 16)
                                sp.dma_start(o_t[:, :, :], part_d[ds(s.n, 1)].rearrange("a p j d -> (a p) j d")
                                             ).then_inc(part_loaded, 16)
                            if b.within(NBLK):
                                sp.wait_ge(fin_ready, (b.n + 2) * TB)
                                sp.dma_start(one(out_b_, b.n), fin[:, :, :]).then_inc(fin_saved, 16)

                        run_steps(sp, -1, NBLK + 1, 1, 2, 2, step)
                        sp.wait_ge(fin_saved, 16 * NBLK)

                    @block.tensor
                    def _(pe):
                        def inner(m):
                            if not m.within(NM):
                                return
                            b, f = block_of(m)
                            if f == 0:
                                pe.wait_ge(xf_lo_ready, b * 2 + 2)
                            if m.reuses(4):
                                pe.wait_ge(hf_ready, m.n - 3)
                            cols = slice((FT1 + f) * P, (FT1 + f + 1) * P)
                            three_pass(hp2[:, m.slot(4)], KD, lambda k: (m1_hi[:, k, cols], m1_lo[:, k, cols]),
                                       lambda k: (xf_hi[:, k], xf_lo[:, k])).then_inc(h1_ready, 1)

                        def outer(m):
                            if not m.within(NM):
                                return
                            b, f = block_of(m)
                            pe.wait_ge(h_lo_ready, m.n + 1)
                            s4 = m.slot(4)
                            for j in range(TB):
                                if f == 0 and m.reuses(T):
                                    pe.wait_ge(ot_ready, (b - 1) * TB + j + 1)
                                toks = slice(j * P, (j + 1) * P)
                                passes = ((h_hi, m2_hi), (h_hi, m2_lo), (h_lo, m2_hi))
                                for n, (l, r) in enumerate(passes):
                                    last = nc.tensor.matmul(opf[:, j], l[:, s4, toks], r[:, FT1 + f],
                                                            start=(f == 0 and n == 0), stop=(f == T - 1 and n == 2))
                            last.then_inc(mm2_done, 1)

                        def step(m):
                            if m.off % T == 0:
                                outer(m + (-LAG))
                                inner(m)
                            else:
                                inner(m)
                                outer(m + (-LAG))

                        tiles(pe, step)

                    @block.scalar
                    def _(act):
                        def split(b, first):
                            act.wait_ge(x2f_loaded, 16 * b + 16)
                            if not first:
                                act.wait_ge(h1_ready, b * T)
                            for k in (slice(0, KD // 2), slice(KD // 2, KD)):
                                nc.scalar.activation(xf_hi[:, k], x2_f[:, k], ACT.Copy).then_inc(xf_hi_ready, 1)

                        def step(m):
                            if m.loop is None and m.off == -1:
                                split(0, True)
                                return
                            if not m.within(NM):
                                return
                            b, f = block_of(m)
                            if f == T - 1 and (m + T).within(NM):
                                split(b + 1, False)
                            act.wait_ge(h1_ready, m.n + 1)
                            if m.reuses(2):
                                act.wait_ge(h_lo_ready, m.n - 1)
                            nc.scalar.activation(h_f[:, m.slot(2)], hp2[:, m.slot(4)], ACT.Gelu_apprx_tanh,
                                                 bias=mb1[:, FT1 + f:FT1 + f + 1], scale=1.0).then_inc(hf_ready, 1)
                            act.wait_ge(hf_ready, m.n + 1)
                            if m.reuses(4):
                                act.wait_ge(mm2_done, m.n - 3)
                            nc.scalar.activation(h_hi[:, m.slot(4)], h_f[:, m.slot(2)], ACT.Copy).then_inc(h_hi_ready, 1)

                        tiles(act, step)

                    @block.vector
                    def _(dve):
                        def split(b):
                            for half, k in enumerate((slice(0, KD // 2), slice(KD // 2, KD))):
                                dve.wait_ge(xf_hi_ready, b * 2 + half + 1)
                                nc.vector.tensor_tensor(xf_lo[:, k], x2_f[:, k], xf_hi[:, k].bitcast(F32),
                                                        ALU.subtract).then_inc(xf_lo_ready, 1)

                        def step(m):
                            if m.loop is None and m.off == -1:
                                split(0)
                                return
                            b, f = block_of(m)
                            if m.within(NM):
                                if f == T - 1 and (m + T).within(NM):
                                    split(b + 1)
                                dve.wait_ge(h_hi_ready, m.n + 1)
                                if m.reuses(4):
                                    dve.wait_ge(mm2_done, m.n - 3)
                                nc.vector.tensor_tensor(h_lo[:, m.slot(4)], h_f[:, m.slot(2)],
                                                        h_hi[:, m.slot(4)].bitcast(F32),
                                                        ALU.subtract).then_inc(h_lo_ready, 1)
                            if f == T - 2 and m.within(NM):
                                dve.wait_ge(part_loaded, 16 * b + 16)
                                for j in range(TB):
                                    nc.vector.tensor_tensor(o_t[:, j], o_t[:, j], mb2[:, :], ALU.add).then_inc(part_biased, 1)
                            if not m.reuses(T) or not (m + (-T)).within(NM):
                                return
                            c = b - 1
                            if f == LAG - 1:
                                dve.wait_ge(mm2_done, b * T)
                                dve.wait_ge(part_biased, b * TB)
                                for j in range(TB):
                                    nc.vector.tensor_tensor(o_t[:, j], opf[:, j], o_t[:, j], ALU.add).then_inc(ot_ready, 1)
                            j = f - LAG
                            if 0 <= j < TB:
                                dve.wait_ge(ot_ready, c * TB + j + 1)
                                nc.vector.bn_stats(stf[:, j], o_t[:, j]).then_inc(statf, 1)
                                dve.wait_ge(statf, c * TB + j + 1)
                                hold(dve, f_held)
                                nc.vector.bn_aggr(mvf[:, j], stf[:, j]).then_inc(aggrf, 1)
                                dve.wait_ge(aggrf, c * TB + j + 1)
                                nc.vector.tensor_scalar(varf[:, j], mvf[:, j, 1:2], EPS, None, ALU.add).then_inc(var_f, 1)
                            j -= 1
                            if 0 <= j < TB:
                                dve.wait_ge(root_f, c * TB + j + 1)
                                nc.vector.tensor_scalar(o_t[:, j], o_t[:, j], mvf[:, j, 0:1], rstdf[:, j], ALU.subtract,
                                                        ALU.mult).then_inc(norm_f, 1)

                        tiles(dve, step)

                    @block.gpsimd
                    def _(pool):
                        def step(s):
                            pool.wait_ge(x1f_loaded, 16 * s.n + 16)
                            if s.reuses(1):
                                pool.wait_ge(fin_saved, 16 * s.n)
                            for j in range(TB):
                                pool.wait_ge(var_f, s.n * TB + j + 1)
                                nc.gpsimd.tensor_tensor(rstdf[:, j], varf[:, j], minus_half[:, :],
                                                        ALU.pow).then_inc(root_f, 1)
                                pool.wait_ge(norm_f, s.n * TB + j + 1)
                                nc.gpsimd.tensor_tensor(fin[:, j], o_t[:, j], x1_f[:, j], ALU.add).then_inc(fin_ready, 1)

                        pool.sem_inc(fin_ready, TB)
                        run_steps(pool, 0, NBLK, 1, 2, 2, step)


def laid_out(a):
    import numpy as np

    a = {k: np.asarray(v) for k, v in a.items()}
    x = a["L0_attn_x"][0]
    L, D = x.shape
    E, F, _ = a["L0_ffn_TW1"].shape
    N = a["L0_attn_C"].shape[1]
    Q, G = P // N, D * N // P
    columns = lambda v: v.reshape(-1, P).T
    by_group = lambda v: v.reshape(G, Q, N).transpose(1, 2, 0).reshape(P, G)
    given = {
        "x": x,
        "x_rev": x.reshape(L // P, P, D)[:, ::-1],
        "in_WT": a["L0_attn_in_W"].T,
        "in_b": a["L0_attn_in_b"],
        "log_dt": a["L0_attn_log_dt"].reshape(G, Q).T,
        "C_re": by_group(a["L0_attn_C"][..., 0]),
        "C_im": by_group(a["L0_attn_C"][..., 1]),
        "log_A_real": by_group(a["L0_attn_log_A_real"]),
        "A_imag": by_group(a["L0_attn_A_imag"]),
        "D_skip": columns(a["L0_attn_D_skip"]),
        "glu_WT": a["L0_attn_glu_W"].T,
        "glu_b": columns(a["L0_attn_glu_b"]),
        "out_WT": a["L0_attn_out_W"].T,
        "out_b": a["L0_attn_out_b"],
        "gate_w1T": a["L0_ffn_gate_w1"].T,
        "gate_b1": columns(a["L0_ffn_gate_b1"]),
        "gate_w2T": a["L0_ffn_gate_w2"].T,
        "gate_b2": a["L0_ffn_gate_b2"],
        "W1T": a["L0_ffn_W1"].T,
        "b1": columns(a["L0_ffn_b1"]),
        "W2T": a["L0_ffn_W2"].T,
        "b2": a["L0_ffn_b2"],
        "TW1T": a["L0_ffn_TW1"].transpose(0, 2, 1),
        "Tb1T": a["L0_ffn_Tb1"].reshape(E, F // P, P).transpose(2, 0, 1),
        "TW2T": a["L0_ffn_TW2"].transpose(0, 2, 1),
        "Tb2": a["L0_ffn_Tb2"],
    }
    return {k: np.ascontiguousarray(v) for k, v in given.items()}


def kernel(**inputs):
    import concourse.bacc as bacc
    from concourse.bass_utils import run_bass_kernel_spmd

    arrays = laid_out(inputs)
    nc = bacc.Bacc("TRN2", target_bir_lowering=False, num_devices=1)
    args = [nc.dram_tensor(f"in_{k}", v.shape, mybir.dt.from_np(v.dtype), kind="ExternalInput").ap()
            for k, v in arrays.items()]
    out = nc.dram_tensor("out", arrays["x"].shape, F32, kind="ExternalOutput").ap()
    s4d_glu_and_gated_ffn(nc, *args, out)
    r = run_bass_kernel_spmd(nc, [{f"in_{k}": v for k, v in arrays.items()}], core_ids=[0])
    return r.results[0]["out"][None]
```
